# Optimizing a Trainium2 kernel written in Bass

```python
import numpy as np
import jax
import jax.numpy as jnp

def _softmax(x, axis=-1):
    return jax.nn.softmax(x, axis=axis)

def _gelu(x):
    return jax.nn.gelu(x, approximate=True)

def _silu(x):
    return jax.nn.silu(x)

def _sigmoid(x):
    return jax.nn.sigmoid(x)

def _layernorm(x, axis=-1, eps=1e-05):
    m = jnp.mean(x, axis=axis, keepdims=True)
    v = jnp.var(x, axis=axis, keepdims=True)
    return (x - m) / jnp.sqrt(v + eps)

def _scatter_add(tgt, idx, src, axis=0):
    return tgt.at[idx].add(src)

def _segment_sum(src, seg, n):
    return jax.ops.segment_sum(src, seg, n)
kernel_name = 'mk_sandwich_d2_jaxref_r8_92eb59'

def setup_inputs(seed: int=0):
    np.random.seed(seed)
    _w = jnp.asarray

    def _L0_attn_setup():
        import jax, jax.numpy as jnp
        import numpy as np
        D_MODEL = 128
        N_QK = 32
        D_QK = 32
        N_OV = 256
        D_OV = 1
        SEQ = 128
        BATCH = 2
        VKV = 16
        ROT_DIM = 32
        ROT_BASE = 10000.0
        SCALE = D_QK ** 0.5

        def _kaiming(k, shape, fan_in):
            return jax.random.normal(k, shape, jnp.float32) * np.sqrt(2.0 / fan_in)

        def _rotary_sin_cos(n_ctx, rd, base):
            pos = jnp.arange(n_ctx, dtype=jnp.float32)
            dim = jnp.arange(rd // 2, dtype=jnp.float32)
            freq = base ** (dim / (rd / 2))
            freq = jnp.concatenate([freq, freq])
            angles = pos[:, None] / freq[None, :]
            return (jnp.sin(angles), jnp.cos(angles))

        def _apply_rotary(x, sin, cos, rd):
            s = x.shape[1]
            x_rot, x_pass = (x[..., :rd], x[..., rd:])
            flip = jnp.concatenate([-x_rot[..., rd // 2:], x_rot[..., :rd // 2]], axis=-1)
            rot = x_rot * cos[None, :s, None, :] + flip * sin[None, :s, None, :]
            return jnp.concatenate([rot, x_pass], axis=-1)
        key = jax.random.key(seed)
        ks = jax.random.split(key, 7)
        return {'resid': jax.random.normal(ks[0], (BATCH, SEQ, D_MODEL), jnp.float32), 'W_Q': _kaiming(ks[1], (N_QK, D_MODEL, D_QK), D_MODEL * D_QK), 'W_K': _kaiming(ks[2], (N_QK, D_MODEL, D_QK), D_MODEL * D_QK), 'W_V': _kaiming(ks[3], (N_OV, D_MODEL, D_OV), D_MODEL * D_OV), 'W_O': _kaiming(ks[4], (N_OV, D_OV, D_MODEL), D_OV * D_MODEL), 'b_Q': jnp.zeros((N_QK, D_QK), jnp.float32), 'b_K': jnp.zeros((N_QK, D_QK), jnp.float32), 'b_V': jnp.zeros((N_OV, D_OV), jnp.float32), 'virtual_k': _kaiming(ks[5], (VKV, N_QK, D_QK), N_QK * D_QK), 'virtual_v': jnp.zeros((VKV, N_OV, D_OV), jnp.float32)}
    _L0_attn_in = _L0_attn_setup()

    def _L0_ffn_setup():
        import jax, jax.numpy as jnp
        import numpy as np
        DIM = 128
        DEPTH = 2
        HEADS = 8
        DIM_HEAD = 64
        WINDOW = 64
        INNER = HEADS * DIM_HEAD
        HID = int(DIM * 4 * 2 / 3)
        B, N = (2, 1024)
        QK_SCALE = 8.0

        def shift_token(t):
            t1, t2 = jnp.split(t, 2, axis=-1)
            t2 = jnp.pad(t2, ((0, 0), (1, 0), (0, 0)))[:, :-1]
            return jnp.concatenate([t1, t2], axis=-1)

        def l2norm(t):
            return t / jnp.clip(jnp.linalg.norm(t, axis=-1, keepdims=True), 1e-12)

        def rotate_half(x):
            x1, x2 = jnp.split(x, 2, axis=-1)
            return jnp.concatenate([-x2, x1], axis=-1)

        def rotary_xpos(q, k):
            n = q.shape[-2]
            half_idx = jnp.arange(0, DIM_HEAD, 2, dtype=jnp.float32)
            inv_freq = 1.0 / 10000.0 ** (half_idx / DIM_HEAD)
            t = jnp.arange(n, dtype=jnp.float32)
            freqs = t[:, None] * inv_freq[None, :]
            freqs = jnp.concatenate([freqs, freqs], axis=-1)
            base = (half_idx + 0.4 * DIM_HEAD) / (1.4 * DIM_HEAD)
            power = (t - n // 2) / float(WINDOW // 2)
            scale = base[None, :] ** power[:, None]
            scale = jnp.concatenate([scale, scale], axis=-1)
            cos, sin = (jnp.cos(freqs), jnp.sin(freqs))
            q = q * cos * scale + rotate_half(q) * sin * scale
            k = k * cos / scale + rotate_half(k) * sin / scale
            return (q, k)

        def local_attention(q, k, v):
            b, h, n, d = q.shape
            w = n // WINDOW
            bq = q.reshape(b, h, w, WINDOW, d) * QK_SCALE
            bk = k.reshape(b, h, w, WINDOW, d)
            bv = v.reshape(b, h, w, WINDOW, d)

            def look_around(t):
                p = jnp.pad(t, ((0, 0), (0, 0), (1, 0), (0, 0), (0, 0)))
                return jnp.concatenate([p[:, :, :w], p[:, :, 1:]], axis=3)
            bk, bv = (look_around(bk), look_around(bv))
            bt = jnp.arange(n).reshape(w, WINDOW)
            btp = jnp.pad(bt, ((1, 0), (0, 0)), constant_values=-1)
            btk = jnp.concatenate([btp[:w], btp[1:]], axis=1)
            sim = jnp.einsum('bhwid,bhwjd->bhwij', bq, bk)
            i = bt[:, :, None]
            j = btk[:, None, :]
            mask = (i < j) | (i > j + WINDOW) | (j == -1)
            sim = jnp.where(mask, -jnp.finfo(sim.dtype).max, sim)
            attn = jax.nn.softmax(sim, axis=-1)
            out = jnp.einsum('bhwij,bhwjd->bhwid', attn, bv)
            return out.reshape(b, h, n, d)

        def _layer(x, wqkv, qs, ksc, wo, lg, lb, w1, b1, w2, b2):
            b, n, _ = x.shape
            h = shift_token(x)
            qkv = h @ wqkv
            q, k, v = jnp.split(qkv, 3, axis=-1)
            to_heads = lambda t: t.reshape(b, n, HEADS, DIM_HEAD).transpose(0, 2, 1, 3)
            q, k, v = (to_heads(q), to_heads(k), to_heads(v))
            q = l2norm(q) * qs
            k = l2norm(k) * ksc
            q, k = rotary_xpos(q, k)
            o = local_attention(q, k, v)
            o = o.transpose(0, 2, 1, 3).reshape(b, n, INNER)
            x = x + o @ wo
            h = shift_token(x)
            mu = h.mean(-1, keepdims=True)
            var = h.var(-1, keepdims=True)
            h = (h - mu) / jnp.sqrt(var + 1e-05) * lg + lb
            h = h @ w1 + b1
            a, g = jnp.split(h, 2, axis=-1)
            h = a * jax.nn.gelu(g, approximate=False)
            x = x + h @ w2 + b2
            return x
        key = jax.random.key(seed)
        ks = jax.random.split(key, 6)
        return {'x': jax.random.normal(ks[0], (B, N, DIM), jnp.float32), 'wqkv': jax.random.normal(ks[1], (DEPTH, DIM, 3 * INNER), jnp.float32) * 0.02, 'q_scale': jnp.ones((DEPTH, DIM_HEAD), jnp.float32), 'k_scale': jnp.ones((DEPTH, DIM_HEAD), jnp.float32), 'wo': jax.random.normal(ks[2], (DEPTH, INNER, DIM), jnp.float32) * 0.02, 'ln_g': jnp.ones((DEPTH, DIM), jnp.float32), 'ln_b': jnp.zeros((DEPTH, DIM), jnp.float32), 'w1': jax.random.normal(ks[3], (DEPTH, DIM, 2 * HID), jnp.float32) * 0.02, 'b1': jnp.zeros((DEPTH, 2 * HID), jnp.float32), 'w2': jax.random.normal(ks[4], (DEPTH, HID, DIM), jnp.float32) * 0.02, 'b2': jnp.zeros((DEPTH, DIM), jnp.float32)}
    _L0_ffn_in = _L0_ffn_setup()

    def _L1_attn_setup():
        import jax, jax.numpy as jnp
        import numpy as np
        D_MODEL = 128
        NUM_HEADS = 16
        DEPTH = D_MODEL // NUM_HEADS
        MAX_LEN = 625
        EPS = 1e-06

        def _make_rel_pos_emb():
            pos = np.arange(-MAX_LEN, MAX_LEN + 1, dtype=np.float32)[:, None]
            dim = np.arange(D_MODEL, dtype=np.float32)[None, :]
            angle = pos / 1250 ** (2 * (dim // 2) / D_MODEL)
            pe = np.where(dim % 2 == 0, np.sin(angle), np.cos(angle)).astype(np.float32)
            return jnp.asarray(pe)

        def _rel_shift(x):
            B, H, L, _ = x.shape
            x_padded = jnp.pad(x, ((0, 0), (0, 0), (0, 0), (1, 0)))
            x_padded = x_padded.reshape(B, H, 2 * L, L)
            x_shifted = x_padded[:, :, 1:, :].reshape(B, H, L, 2 * L - 1)
            return x_shifted[:, :, :, :L]
        key = jax.random.key(seed)
        ks = jax.random.split(key, 8)
        B, L = (2, 128)
        s = 1.0 / np.sqrt(D_MODEL)
        return {'x': jax.random.normal(ks[0], (B, L, D_MODEL), jnp.float32), 'gamma': jnp.ones((D_MODEL,), jnp.float32), 'beta': jnp.zeros((D_MODEL,), jnp.float32), 'Wq': jax.random.normal(ks[1], (D_MODEL, D_MODEL), jnp.float32) * s, 'Wk': jax.random.normal(ks[2], (D_MODEL, D_MODEL), jnp.float32) * s, 'Wv': jax.random.normal(ks[3], (D_MODEL, D_MODEL), jnp.float32) * s, 'Wr': jax.random.normal(ks[4], (D_MODEL, D_MODEL), jnp.float32) * s, 'u_bias': jax.random.normal(ks[5], (NUM_HEADS, DEPTH), jnp.float32) * 0.02, 'v_bias': jax.random.normal(ks[6], (NUM_HEADS, DEPTH), jnp.float32) * 0.02, 'Wo': jax.random.normal(ks[7], (D_MODEL, D_MODEL), jnp.float32) * s, 'bo': jnp.zeros((D_MODEL,), jnp.float32), 'rel_pos_emb': _make_rel_pos_emb()}
    _L1_attn_in = _L1_attn_setup()

    def _L1_ffn_setup():
        import jax, jax.numpy as jnp
        import numpy as np
        DIM = 128
        HIDDEN = 384
        SCALE = 1.0 / 127.0

        def _dequant(w_int, dtype):
            return w_int.astype(dtype) * jnp.asarray(SCALE, dtype)
        key = jax.random.key(seed)
        k_x, k_g, k_u, k_d = jax.random.split(key, 4)
        x = jax.random.normal(k_x, (4, 256, DIM), dtype=jnp.float32)
        w_gate = jax.random.randint(k_g, (HIDDEN, DIM), -127, 128, dtype=jnp.int32)
        w_up = jax.random.randint(k_u, (HIDDEN, DIM), -127, 128, dtype=jnp.int32)
        w_down = jax.random.randint(k_d, (DIM, HIDDEN), -127, 128, dtype=jnp.int32)
        return {'x': x, 'w_gate': w_gate, 'w_up': w_up, 'w_down': w_down}
    _L1_ffn_in = _L1_ffn_setup()
    _d = {'L0_attn_resid': _L0_attn_in['resid'], 'L0_attn_W_Q': _L0_attn_in['W_Q'], 'L0_attn_W_K': _L0_attn_in['W_K'], 'L0_attn_W_V': _L0_attn_in['W_V'], 'L0_attn_W_O': _L0_attn_in['W_O'], 'L0_attn_b_Q': _L0_attn_in['b_Q'], 'L0_attn_b_K': _L0_attn_in['b_K'], 'L0_attn_b_V': _L0_attn_in['b_V'], 'L0_attn_virtual_k': _L0_attn_in['virtual_k'], 'L0_attn_virtual_v': _L0_attn_in['virtual_v'], 'L0_ffn_wqkv': _L0_ffn_in['wqkv'], 'L0_ffn_q_scale': _L0_ffn_in['q_scale'], 'L0_ffn_k_scale': _L0_ffn_in['k_scale'], 'L0_ffn_wo': _L0_ffn_in['wo'], 'L0_ffn_ln_g': _L0_ffn_in['ln_g'], 'L0_ffn_ln_b': _L0_ffn_in['ln_b'], 'L0_ffn_w1': _L0_ffn_in['w1'], 'L0_ffn_b1': _L0_ffn_in['b1'], 'L0_ffn_w2': _L0_ffn_in['w2'], 'L0_ffn_b2': _L0_ffn_in['b2'], 'L1_attn_gamma': _L1_attn_in['gamma'], 'L1_attn_beta': _L1_attn_in['beta'], 'L1_attn_Wq': _L1_attn_in['Wq'], 'L1_attn_Wk': _L1_attn_in['Wk'], 'L1_attn_Wv': _L1_attn_in['Wv'], 'L1_attn_Wr': _L1_attn_in['Wr'], 'L1_attn_u_bias': _L1_attn_in['u_bias'], 'L1_attn_v_bias': _L1_attn_in['v_bias'], 'L1_attn_Wo': _L1_attn_in['Wo'], 'L1_attn_bo': _L1_attn_in['bo'], 'L1_attn_rel_pos_emb': _L1_attn_in['rel_pos_emb'], 'L1_ffn_w_gate': _L1_ffn_in['w_gate'], 'L1_ffn_w_up': _L1_ffn_in['w_up'], 'L1_ffn_w_down': _L1_ffn_in['w_down']}
    _x0 = _d['L0_attn_resid']
    _d['L0_attn_resid'] = jax.random.normal(jax.random.fold_in(jax.random.key(seed), 1), (4, 512, 128), dtype=_x0.dtype)
    del _x0
    return _d

def reference(L0_attn_resid, L0_attn_W_Q, L0_attn_W_K, L0_attn_W_V, L0_attn_W_O, L0_attn_b_Q, L0_attn_b_K, L0_attn_b_V, L0_attn_virtual_k, L0_attn_virtual_v, L0_ffn_wqkv, L0_ffn_q_scale, L0_ffn_k_scale, L0_ffn_wo, L0_ffn_ln_g, L0_ffn_ln_b, L0_ffn_w1, L0_ffn_b1, L0_ffn_w2, L0_ffn_b2, L1_attn_gamma, L1_attn_beta, L1_attn_Wq, L1_attn_Wk, L1_attn_Wv, L1_attn_Wr, L1_attn_u_bias, L1_attn_v_bias, L1_attn_Wo, L1_attn_bo, L1_attn_rel_pos_emb, L1_ffn_w_gate, L1_ffn_w_up, L1_ffn_w_down):

    def _L0_attn_ref(resid, W_Q, W_K, W_V, W_O, b_Q, b_K, b_V, virtual_k, virtual_v):
        import jax, jax.numpy as jnp
        import numpy as np
        D_MODEL = 128
        N_QK = 32
        D_QK = 32
        N_OV = 256
        D_OV = 1
        SEQ = 128
        BATCH = 2
        VKV = 16
        ROT_DIM = 32
        ROT_BASE = 10000.0
        SCALE = D_QK ** 0.5

        def _kaiming(k, shape, fan_in):
            return jax.random.normal(k, shape, jnp.float32) * np.sqrt(2.0 / fan_in)

        def _rotary_sin_cos(n_ctx, rd, base):
            pos = jnp.arange(n_ctx, dtype=jnp.float32)
            dim = jnp.arange(rd // 2, dtype=jnp.float32)
            freq = base ** (dim / (rd / 2))
            freq = jnp.concatenate([freq, freq])
            angles = pos[:, None] / freq[None, :]
            return (jnp.sin(angles), jnp.cos(angles))

        def _apply_rotary(x, sin, cos, rd):
            s = x.shape[1]
            x_rot, x_pass = (x[..., :rd], x[..., rd:])
            flip = jnp.concatenate([-x_rot[..., rd // 2:], x_rot[..., :rd // 2]], axis=-1)
            rot = x_rot * cos[None, :s, None, :] + flip * sin[None, :s, None, :]
            return jnp.concatenate([rot, x_pass], axis=-1)
        b, s, _ = resid.shape
        q = jnp.einsum('bsm,hmd->bshd', resid, W_Q) + b_Q
        k = jnp.einsum('bsm,hmd->bshd', resid, W_K) + b_K
        v = jnp.einsum('bsm,hmd->bshd', resid, W_V) + b_V
        sin, cos = _rotary_sin_cos(s, ROT_DIM, ROT_BASE)
        q = _apply_rotary(q, sin, cos, ROT_DIM)
        k = _apply_rotary(k, sin, cos, ROT_DIM)
        k = jnp.concatenate([k, jnp.broadcast_to(virtual_k[None], (b,) + virtual_k.shape)], axis=1)
        v = jnp.concatenate([v, jnp.broadcast_to(virtual_v[None], (b,) + virtual_v.shape)], axis=1)
        kv_len = s + VKV
        scores = jnp.einsum('bqhd,bkhd->bhqk', q, k) / SCALE
        mask = jnp.arange(kv_len)[None, :] <= jnp.arange(s)[:, None] + VKV
        scores = jnp.where(mask[None, None], scores, -jnp.inf)
        pattern = jax.nn.softmax(scores, axis=-1)
        pattern = jnp.where(jnp.isnan(pattern), 0.0, pattern)
        ratio = N_OV // N_QK
        v_g = v.reshape(b, kv_len, N_QK, ratio * D_OV)
        z = jnp.einsum('bhqk,bkhr->bqhr', pattern, v_g)
        z = z.reshape(b, s, N_OV, D_OV)
        out = jnp.einsum('bqhd,hdm->bqm', z, W_O)
        return out

    def _L0_ffn_ref(x, wqkv, q_scale, k_scale, wo, ln_g, ln_b, w1, b1, w2, b2):
        import jax, jax.numpy as jnp
        import numpy as np
        DIM = 128
        DEPTH = 2
        HEADS = 8
        DIM_HEAD = 64
        WINDOW = 64
        INNER = HEADS * DIM_HEAD
        HID = int(DIM * 4 * 2 / 3)
        B, N = (2, 1024)
        QK_SCALE = 8.0

        def shift_token(t):
            t1, t2 = jnp.split(t, 2, axis=-1)
            t2 = jnp.pad(t2, ((0, 0), (1, 0), (0, 0)))[:, :-1]
            return jnp.concatenate([t1, t2], axis=-1)

        def l2norm(t):
            return t / jnp.clip(jnp.linalg.norm(t, axis=-1, keepdims=True), 1e-12)

        def rotate_half(x):
            x1, x2 = jnp.split(x, 2, axis=-1)
            return jnp.concatenate([-x2, x1], axis=-1)

        def rotary_xpos(q, k):
            n = q.shape[-2]
            half_idx = jnp.arange(0, DIM_HEAD, 2, dtype=jnp.float32)
            inv_freq = 1.0 / 10000.0 ** (half_idx / DIM_HEAD)
            t = jnp.arange(n, dtype=jnp.float32)
            freqs = t[:, None] * inv_freq[None, :]
            freqs = jnp.concatenate([freqs, freqs], axis=-1)
            base = (half_idx + 0.4 * DIM_HEAD) / (1.4 * DIM_HEAD)
            power = (t - n // 2) / float(WINDOW // 2)
            scale = base[None, :] ** power[:, None]
            scale = jnp.concatenate([scale, scale], axis=-1)
            cos, sin = (jnp.cos(freqs), jnp.sin(freqs))
            q = q * cos * scale + rotate_half(q) * sin * scale
            k = k * cos / scale + rotate_half(k) * sin / scale
            return (q, k)

        def local_attention(q, k, v):
            b, h, n, d = q.shape
            w = n // WINDOW
            bq = q.reshape(b, h, w, WINDOW, d) * QK_SCALE
            bk = k.reshape(b, h, w, WINDOW, d)
            bv = v.reshape(b, h, w, WINDOW, d)

            def look_around(t):
                p = jnp.pad(t, ((0, 0), (0, 0), (1, 0), (0, 0), (0, 0)))
                return jnp.concatenate([p[:, :, :w], p[:, :, 1:]], axis=3)
            bk, bv = (look_around(bk), look_around(bv))
            bt = jnp.arange(n).reshape(w, WINDOW)
            btp = jnp.pad(bt, ((1, 0), (0, 0)), constant_values=-1)
            btk = jnp.concatenate([btp[:w], btp[1:]], axis=1)
            sim = jnp.einsum('bhwid,bhwjd->bhwij', bq, bk)
            i = bt[:, :, None]
            j = btk[:, None, :]
            mask = (i < j) | (i > j + WINDOW) | (j == -1)
            sim = jnp.where(mask, -jnp.finfo(sim.dtype).max, sim)
            attn = jax.nn.softmax(sim, axis=-1)
            out = jnp.einsum('bhwij,bhwjd->bhwid', attn, bv)
            return out.reshape(b, h, n, d)

        def _layer(x, wqkv, qs, ksc, wo, lg, lb, w1, b1, w2, b2):
            b, n, _ = x.shape
            h = shift_token(x)
            qkv = h @ wqkv
            q, k, v = jnp.split(qkv, 3, axis=-1)
            to_heads = lambda t: t.reshape(b, n, HEADS, DIM_HEAD).transpose(0, 2, 1, 3)
            q, k, v = (to_heads(q), to_heads(k), to_heads(v))
            q = l2norm(q) * qs
            k = l2norm(k) * ksc
            q, k = rotary_xpos(q, k)
            o = local_attention(q, k, v)
            o = o.transpose(0, 2, 1, 3).reshape(b, n, INNER)
            x = x + o @ wo
            h = shift_token(x)
            mu = h.mean(-1, keepdims=True)
            var = h.var(-1, keepdims=True)
            h = (h - mu) / jnp.sqrt(var + 1e-05) * lg + lb
            h = h @ w1 + b1
            a, g = jnp.split(h, 2, axis=-1)
            h = a * jax.nn.gelu(g, approximate=False)
            x = x + h @ w2 + b2
            return x
        for l in range(DEPTH):
            x = _layer(x, wqkv[l], q_scale[l], k_scale[l], wo[l], ln_g[l], ln_b[l], w1[l], b1[l], w2[l], b2[l])
        return x

    def _L1_attn_ref(x, gamma, beta, Wq, Wk, Wv, Wr, u_bias, v_bias, Wo, bo, rel_pos_emb):
        import jax, jax.numpy as jnp
        import numpy as np
        D_MODEL = 128
        NUM_HEADS = 16
        DEPTH = D_MODEL // NUM_HEADS
        MAX_LEN = 625
        EPS = 1e-06

        def _make_rel_pos_emb():
            pos = np.arange(-MAX_LEN, MAX_LEN + 1, dtype=np.float32)[:, None]
            dim = np.arange(D_MODEL, dtype=np.float32)[None, :]
            angle = pos / 1250 ** (2 * (dim // 2) / D_MODEL)
            pe = np.where(dim % 2 == 0, np.sin(angle), np.cos(angle)).astype(np.float32)
            return jnp.asarray(pe)

        def _rel_shift(x):
            B, H, L, _ = x.shape
            x_padded = jnp.pad(x, ((0, 0), (0, 0), (0, 0), (1, 0)))
            x_padded = x_padded.reshape(B, H, 2 * L, L)
            x_shifted = x_padded[:, :, 1:, :].reshape(B, H, L, 2 * L - 1)
            return x_shifted[:, :, :, :L]
        B, L, _ = x.shape
        mu = jnp.mean(x, axis=-1, keepdims=True)
        var = jnp.mean(jnp.square(x - mu), axis=-1, keepdims=True)
        xn = (x - mu) * jax.lax.rsqrt(var + EPS) * gamma + beta

        def heads(t):
            return t.reshape(B, L, NUM_HEADS, DEPTH).transpose(0, 2, 1, 3)
        q = heads(xn @ Wq)
        k = heads(xn @ Wk)
        v = heads(xn @ Wv)
        idx = jnp.arange(2 * L - 1) - (L - 1) + MAX_LEN
        r_emb = rel_pos_emb[idx]
        r = (r_emb @ Wr).reshape(2 * L - 1, NUM_HEADS, DEPTH).transpose(1, 0, 2)
        AC = jnp.einsum('bhld,bhmd->bhlm', q + u_bias[None, :, None, :], k)
        BD = jnp.einsum('bhld,hrd->bhlr', q + v_bias[None, :, None, :], r)
        score = (AC + _rel_shift(BD)) / jnp.sqrt(jnp.float32(DEPTH))
        attn = jax.nn.softmax(score, axis=-1)
        out = jnp.einsum('bhlm,bhmd->bhld', attn, v)
        out = out.transpose(0, 2, 1, 3).reshape(B, L, D_MODEL)
        return out @ Wo + bo

    def _L1_ffn_ref(x, w_gate, w_up, w_down):
        import jax, jax.numpy as jnp
        import numpy as np
        DIM = 128
        HIDDEN = 384
        SCALE = 1.0 / 127.0

        def _dequant(w_int, dtype):
            return w_int.astype(dtype) * jnp.asarray(SCALE, dtype)
        wg = _dequant(w_gate, x.dtype)
        wu = _dequant(w_up, x.dtype)
        wd = _dequant(w_down, x.dtype)
        gate = jnp.einsum('bsd,hd->bsh', x, wg)
        up = jnp.einsum('bsd,hd->bsh', x, wu)
        h = jax.nn.silu(gate) * up
        return jnp.einsum('bsh,dh->bsd', h, wd)
    x = L0_attn_resid
    x = x + _layernorm(_L0_attn_ref(_layernorm(x, axis=-1), L0_attn_W_Q, L0_attn_W_K, L0_attn_W_V, L0_attn_W_O, L0_attn_b_Q, L0_attn_b_K, L0_attn_b_V, L0_attn_virtual_k, L0_attn_virtual_v), axis=-1)
    x = x + _layernorm(_L0_ffn_ref(_layernorm(x, axis=-1), L0_ffn_wqkv, L0_ffn_q_scale, L0_ffn_k_scale, L0_ffn_wo, L0_ffn_ln_g, L0_ffn_ln_b, L0_ffn_w1, L0_ffn_b1, L0_ffn_w2, L0_ffn_b2), axis=-1)
    x = x + _layernorm(_L1_attn_ref(_layernorm(x, axis=-1), L1_attn_gamma, L1_attn_beta, L1_attn_Wq, L1_attn_Wk, L1_attn_Wv, L1_attn_Wr, L1_attn_u_bias, L1_attn_v_bias, L1_attn_Wo, L1_attn_bo, L1_attn_rel_pos_emb), axis=-1)
    x = x + _layernorm(_L1_ffn_ref(_layernorm(x, axis=-1), L1_ffn_w_gate, L1_ffn_w_up, L1_ffn_w_down), axis=-1)
    return x

_drawn_inputs = setup_inputs


def setup_inputs(seed=0):
    import zlib

    import numpy as np

    out = dict(_drawn_inputs(seed))
    spreads = {'L0_attn_b_Q': (0.0, 0.46),
     'L0_attn_b_K': (0.0, 0.8),
     'L0_attn_b_V': (0.0, 0.1),
     'L0_attn_virtual_v': (0.0, 2.0),
     'L0_ffn_q_scale': (1.0, 0.6),
     'L0_ffn_k_scale': (1.0, 0.6),
     'L0_ffn_ln_g': (1.0, 0.6),
     'L0_ffn_ln_b': (0.0, 0.8),
     'L0_ffn_b1': (0.0, 0.8),
     'L0_ffn_b2': (0.0, 0.8),
     'L1_attn_gamma': (1.0, 0.2),
     'L1_attn_beta': (0.0, 0.1),
     'L1_attn_bo': (0.0, 0.1)}
    factors = {'L0_attn_virtual_k': 64.0,
     'L0_ffn_w1': 7.209,
     'L0_ffn_w2': 7.134,
     'L1_attn_u_bias': 23.128,
     'L1_attn_v_bias': 41.204}
    for name, (base, spread) in spreads.items():
        noise = np.random.default_rng([zlib.crc32(name.encode()), seed]).standard_normal(out[name].shape)
        drawn = base * np.exp(spread * noise) if base else spread * noise
        out[name] = jnp.asarray(drawn.astype(out[name].dtype))
    for name, factor in factors.items():
        out[name] = (out[name] * factor).astype(out[name].dtype)
    return out
```

```python
from contextlib import ExitStack

import numpy as np

import concourse.bass as bass
from concourse import mybir

ALU = mybir.AluOpType
ACT = mybir.ActivationFunctionType
AX = mybir.AxisListType
F32 = mybir.dt.float32
F32R = mybir.dt.float32r
BF16 = mybir.dt.bfloat16
I32 = mybir.dt.int32

P = 128
B, N, D = 4, 512, 128
NT = N // P
TT = B * NT
EPS = 1e-5
BIG = -1e30

AH, AD, AR, AV = 32, 32, 8, 16
GH = P // AD
AG = AH // GH
KN = N + AV
PITCH = N + AV
NB = 2


class Chain:

    def __init__(self, eng, sem):
        self.eng, self.sem, self.n = eng, sem, 0

    def add(self, ins):
        self.n += 1
        ins.then_inc(self.sem, 1)

    def wait(self):
        self.eng.wait_ge(self.sem, self.n)

    def step(self, ins):
        self.add(ins)
        self.wait()


class Store:

    def __init__(self, nc, ctx, tag):
        self.nc, self.ctx, self.tag = nc, ctx, tag

    def sb(self, name, shape, dt=F32):
        return self.ctx.enter_context(self.nc.sbuf_tensor(f"{self.tag}_{name}", shape, dt))

    def sem(self, name):
        return self.ctx.enter_context(self.nc.semaphore(f"{self.tag}_{name}"))

    def sems(self, *names):
        return [self.sem(n) for n in names]


def clear(nc, sems):
    nums = sorted(s.num for s in sems)
    assert nums == list(range(nums[0], nums[-1] + 1))
    nc.all_engine_barrier(sems_to_clear=range(nums[0], nums[-1] + 1))


def causal_attention(nc, X, Z, ps, c, d):
    with ExitStack() as ctx:
        s = Store(nc, ctx, "a")
        xnT = s.sb("xnT", [P, B * N])
        V = s.sb("V", [P, B, NT, AH * AR])
        Vrem = s.sb("Vrem", [P, B, AH, NT, AR])
        W = s.sb("W", [P, 4, P])
        bias = s.sb("bias", [P, 4])
        vk = s.sb("vk", [P, AV])
        with ExitStack() as ctx0:
            s0 = Store(nc, ctx0, "a0")
            xn = s0.sb("xn", [P, 2, D])
            xrem = s0.sb("xrem", [P, B, NT - 1, 32])
            st = s0.sb("st", [P, TT, 6])
            mv = s0.sb("mv", [P, TT, 2])
            rstd = s0.sb("rstd", [P, TT])
            wv = s0.sb("wv", [P, AH * AR])
            bv = s0.sb("bv", [P, AH * AR])
            x_in, w_in, stats, stats_done, pow_done, xn_done, xt_done, xt_used, v_ready, v_done, zeroed, vv_in, rem_used = s0.sems(
                "x_in", "w_in", "stats", "stats_done", "pow_done", "xn_done", "xt_done", "xt_used", "v_ready", "v_done", "zeroed", "vv_in", "rem_used")
            with nc.Block() as block:
                @block.sync
                def _(sp):
                    sp.dma_start(X[:], d["x"].rearrange("b (t p) d -> p (b t) d", p=P)).then_inc(x_in, 16)
                    sp.dma_start(wv[:], d["a_wv"]).then_inc(w_in, 16)
                    sp.dma_start(bv[:], d["a_bv"]).then_inc(w_in, 16)
                    sp.dma_start(W[:], d["a_w"][0]).then_inc(w_in, 16)
                    sp.dma_start(bias[:], d["a_b"][0]).then_inc(w_in, 16)
                    sp.dma_start(vk[:], d["a_vk"][0]).then_inc(w_in, 16)
                    sp.wait_ge(zeroed, 1)
                    for b in range(B):
                        sp.dma_start(Vrem[96:96 + AV, b, :, NT - 1, :], d["a_vv"]).then_inc(vv_in, 16)
                    sp.wait_ge(w_in, 80)
                    sp.wait_ge(vv_in, 16 * B)

                @block.gpsimd
                def _(pool):
                    nc.gpsimd.memset(Vrem[:], 0.0).then_inc(zeroed, 1)
                    pool.wait_ge(stats_done, 1)
                    nc.gpsimd.tensor_tensor(rstd[:], mv[:, :, 1], c["mhalf"][:, 0:TT], ALU.pow).then_inc(pow_done, 1)

                @block.vector
                def _(v):
                    link = Chain(v, stats)
                    v.wait_ge(x_in, 16)
                    for t in range(TT):
                        nc.vector.bn_stats(st[:, t, :], X[:, t, :]).then_inc(stats, 1)
                    link.n = TT
                    v.wait_ge(stats, TT)
                    for t in range(TT):
                        nc.vector.bn_aggr(mv[:, t, :], st[:, t, :]).then_inc(stats, 1)
                    link.n = 2 * TT
                    v.wait_ge(stats, 2 * TT)
                    nc.vector.tensor_scalar(mv[:, :, 1], mv[:, :, 1], EPS, None, ALU.add).then_inc(stats_done, 1)
                    v.wait_ge(pow_done, 1)
                    for t in range(TT):
                        if t >= 2:
                            v.wait_ge(xt_done, t - 1)
                        nc.vector.tensor_scalar(xn[:, t % 2, :], X[:, t, :], mv[:, t, 0:1], rstd[:, t:t + 1],
                                                ALU.subtract, ALU.mult).then_inc(xn_done, 1)
                    v.wait_ge(w_in, 80)
                    v.wait_ge(zeroed, 1)
                    for n in range(TT + B):
                        v.wait_ge(v_ready, n + 1)
                        if n < TT:
                            nc.vector.tensor_tensor(V[:, n // NT, n % NT, :], ps[:, 4 + n % 2, 0:AH * AR], bv[:],
                                                    ALU.add).then_inc(v_done, 1)
                        else:
                            for qt in range(NT - 1):
                                r = slice(32 * qt, 32 * qt + 32)
                                ins = nc.vector.tensor_tensor(
                                    Vrem[r, n - TT, :, qt, :],
                                    ps[r, 4 + n % 2, 0:AH * AR].rearrange("p (h r) -> p h r", r=AR),
                                    bv[r].rearrange("p (h r) -> p h r", r=AR), ALU.add)
                                ins.then_inc(v_done, 1)

                @block.tensor
                def _(pe):
                    for t in range(TT):
                        pe.wait_ge(xn_done, t + 1)
                        if t >= 4:
                            pe.wait_ge(xt_used, t - 3)
                        nc.tensor.transpose(ps[:, t % 4, 0:P], xn[:, t % 2, :], c["ident"][:]).then_inc(xt_done, 1)
                    pe.wait_ge(xt_used, TT)
                    pe.wait_ge(rem_used, B * (NT - 1))
                    pe.wait_ge(w_in, 80)
                    for n in range(TT + B):
                        if n >= 2:
                            pe.wait_ge(v_done, n - 1 if n - 2 < TT else TT + (NT - 1) * (n - 1 - TT))
                        if n < TT:
                            nc.tensor.matmul(ps[:, 4 + n % 2, 0:AH * AR], xnT[:, P * n:P * n + P], wv[:],
                                             start=True, stop=True).then_inc(v_ready, 1)
                        else:
                            lhs = xrem[:, n - TT].rearrange("p t k -> p (t k)")
                            nc.tensor.matmul(ps[0:96, 4 + n % 2, 0:AH * AR], lhs, wv[:],
                                             start=True, stop=True).then_inc(v_ready, 1)

                @block.scalar
                def _(act):
                    for t in range(TT):
                        act.wait_ge(xt_done, t + 1)
                        if t % NT:
                            nc.scalar.copy(xrem[:, t // NT, t % NT - 1, :], ps[:, t % 4, 0:32]).then_inc(rem_used, 1)
                        nc.scalar.copy(xnT[:, P * t:P * t + P], ps[:, t % 4, 0:P]).then_inc(xt_used, 1)
        clear(nc, [x_in, w_in, stats, stats_done, pow_done, xn_done, xt_done, xt_used, v_ready, v_done, zeroed, vv_in, rem_used])
        attention_groups(nc, s, Z, ps, c, d, xnT, V, Vrem, W, bias, vk)


def attention_groups(nc, s, Z, ps, c, d, xnT, V, Vrem, W, bias, vk):
    Qst = [s.sb(f"Qst{i}", [P, GH, NB, N], F32R) for i in range(2)]
    Kst = [s.sb(f"Kst{i}", [P, GH, NB, KN], F32R) for i in range(2)]
    qh = s.sb("qh", [P, NB, N], F32R)
    ql = s.sb("ql", [P, NB, N], F32R)
    kh = s.sb("kh", [P, NB, KN], F32R)
    kl = s.sb("kl", [P, NB, KN], F32R)
    rot = s.sb("rot", [P, 4, N])
    full = s.sb("full", [P, 2, N])
    Pm = s.sb("Pm", [P, 2, NT, PITCH])
    PT = s.sb("PT", [P, 2, 11, P])
    Prem = s.sb("Prem", [P, 2, NT, 32])
    tab = s.sb("tab", [P, 4, N])
    nm = s.sb("nm", [P, 2, NT])
    sums = s.sb("sums", [P, NB, NT, GH])
    rs = s.sb("rs", [P, NB, NT, GH])
    (w_in, pj_ready, stt_done, added, hi_done, lo_done, stk0, stk1, s_ready, nm_ready, exp_done,
     t_done, evd, eva, pv_done, o_rs, o_done, tab_in, pad_done, rem_done) = names = s.sems(
        "w_in", "pj_ready", "stt_done", "added", "hi_done", "lo_done", "stk0", "stk1", "s_ready", "nm_ready",
        "exp_done", "t_done", "evd", "eva", "pv_done", "o_rs", "o_done", "tab_in", "pad_done", "rem_done")
    stk = [stk0, stk1]
    PJ, O, SA, SC, TB = 0, 1, 2, 4, 5
    S_of = {3: 0, 2: 528, 1: 1024, 0: 1296}
    S = ps[:, SA:SC + 1, :].rearrange("p a n -> p (a n)")
    width = lambda qt: P * (qt + 1) + AV
    Ob = ps[:, O, 0:P].rearrange("p (t h r) -> p t h r", t=NT, h=GH)
    TBANK = [[(2, 0), (2, 1), (2, 2), (0, 0)], [(3, 0), (3, 1), (3, 2), (3, 3)], [(1, 0), (1, 1), "rem"]]
    SLOT = {}
    for k, blocks in enumerate(TBANK):
        for j, x in enumerate(blocks):
            SLOT[x] = (k, j, (0, 4, 8)[k] + j)

    def project(pe, s_, n, b):
        k = 8 * s_ + n
        if k >= 1:
            pe.wait_ge(stt_done, k)
        if s_ == 1 and n == 0:
            pe.wait_ge(w_in, 48)
        nc.tensor.matmul(ps[:, PJ, :], W[:, n % 4, :], xnT[:, b * N:(b + 1) * N], start=True, stop=True)\
            .then_inc(pj_ready, 1)

    def rotate_half(v, s_, n):
        k = 8 * s_ + n
        v.wait_ge(pj_ready, k + 1)
        if k >= 4:
            v.wait_ge(added, (k - 4) // 2 + 1)
        nc.vector.scalar_tensor_tensor(rot[:, n % 4, :], ps[:, PJ, :], bias[:, n % 4:n % 4 + 1], tab[:, n % 4, :],
                                       ALU.add, ALU.mult).then_inc(stt_done, 1)

    def add_pair(pool, s_, m):
        k = 4 * s_ + m
        pool.wait_ge(stt_done, 2 * k + 2)
        if k >= 2:
            pool.wait_ge(lo_done, k - 1)
        nc.gpsimd.tensor_tensor(full[:, m % 2, :], rot[:, 2 * (m % 2), :], rot[:, 2 * (m % 2) + 1, :],
                                ALU.add).then_inc(added, 1)

    def split_lo(pool, s_, m):
        k = 4 * s_ + m
        pool.wait_ge(hi_done, k + 1)
        hi, lo = ((qh, ql), (kh, kl))[m % 2]
        ins = nc.gpsimd.tensor_tensor(lo[:, m // 2, 0:N], full[:, m % 2, :], hi[:, m // 2, 0:N].bitcast(F32), ALU.subtract)
        if m % 2:
            ins = nc.gpsimd.tensor_tensor(kl[:, m // 2, N:KN], vk[:], kh[:, m // 2, N:KN].bitcast(F32), ALU.subtract)
        ins.then_inc(lo_done, 1)

    def split_hi(act, s_, m):
        k = 4 * s_ + m
        act.wait_ge(added, k + 1)
        if s_ == 1 and m == 0:
            act.wait_ge(stk[1], 512)
        hi = (qh, kh)[m % 2]
        if m % 2:
            if s_ == 1:
                act.wait_ge(w_in, 48)
            nc.scalar.copy(kh[:, m // 2, N:KN], vk[:])
        nc.scalar.copy(hi[:, m // 2, 0:N], full[:, m % 2, :]).then_inc(hi_done, 1)

    def stack(sp, s_, buf):
        sp.wait_ge(hi_done, 4 * s_ + 4)
        sp.wait_ge(lo_done, 4 * s_ + 4)
        for h in range(GH):
            r = slice(32 * h, 32 * h + 32)
            for dst, halves in ((Qst, (qh, ql, qh, ql)), (Kst, (kh, kh, kl, kl))):
                for k, src in enumerate(halves):
                    sp.dma_start(dst[buf][32 * k:32 * k + 32, h].bitcast(F32), src[r].bitcast(F32)).then_inc(stk[buf], 16)

    with nc.Block() as block:
        @block.sync
        def _(sp):
            sp.dma_start(tab[:], d["a_tab"]).then_inc(tab_in, 16)
            stack(sp, 0, 0)
            sp.wait_ge(stk[0], 512)

        @block.tensor
        def _(pe):
            for n in range(8):
                project(pe, 0, n, n // 4)

        @block.vector
        def _(v):
            v.wait_ge(tab_in, 16)
            for n in range(8):
                rotate_half(v, 0, n)

        @block.gpsimd
        def _(pool):
            nc.gpsimd.memset(Prem[:], 0.0).then_inc(pad_done, 1)
            for m in range(4):
                add_pair(pool, 0, m)
                split_lo(pool, 0, m)
            pool.wait_ge(pad_done, 1)

        @block.scalar
        def _(act):
            for m in range(4):
                split_hi(act, 0, m)
    clear(nc, names)

    U = NB * GH
    with nc.Fori(0, AG) as g:
        with nc.Block() as block:
            @block.sync
            def _(sp):
                stack(sp, 0, 1)
                sp.wait_ge(stt_done, 8)
                sp.dma_start(W[:], d["a_w"][bass.ds(g + 1, 1)].rearrange("g p c n -> p (g c) n")).then_inc(w_in, 16)
                sp.dma_start(bias[:], d["a_b"][bass.ds(g + 1, 1)].rearrange("g p c -> p (g c)")).then_inc(w_in, 16)
                sp.dma_start(vk[:], d["a_vk"][bass.ds(g + 1, 1)].rearrange("g p c -> p (g c)")).then_inc(w_in, 16)
                sp.wait_ge(s_ready, 2 * U)
                stack(sp, 1, 0)
                sp.wait_ge(stk[0], 512)

            @block.gpsimd
            def _(pool):
                def remainder(u):
                    pool.wait_ge(exp_done, 4 * u + 4)
                    if u >= 2:
                        pool.wait_ge(t_done, 3 * (u - 1))
                    for qt in range(NT):
                        lo = P * (qt + 1)
                        ins = nc.gpsimd.tensor_copy(Prem[:, u % 2, qt, 0:AV], Pm[:, u % 2, qt, lo:lo + AV])
                        ins.then_inc(rem_done, 1)

                for k in range(2 * U):
                    if k % 2 == 1:
                        add_pair(pool, k // U, k % U // 2)
                    remainder(k)
                    if k % 2 == 1:
                        split_lo(pool, k // U, k % U // 2)

            @block.tensor
            def _(pe):
                def scores(u, part):
                    q, k = Qst[u // U], Kst[u // U]
                    i, h = u % U // GH, u % GH
                    if u == U and part == 0:
                        pe.wait_ge(stk[1], 512)
                    if part == 0:
                        if u >= 1:
                            pe.wait_ge(exp_done, 4 * u - 2)
                        todo = [(1, [(0, 272)]), (0, [(0, 144)])]
                        last = 0
                    else:
                        if u >= 1:
                            pe.wait_ge(exp_done, 4 * u)
                        todo = [(3, [(0, 512), (512, 16)]), (2, [(0, 400)])]
                        last = 2
                    opened = set()
                    for qt, pieces in todo:
                        for at, w in pieces:
                            lo = S_of[qt] + at
                            nc.tensor.matmul(S[:, lo:lo + w], q[:, h, i, P * qt:P * qt + P], k[:, h, i, at:at + w],
                                             start=lo // 512 not in opened, stop=False)
                            opened.add(lo // 512)
                        edge = width(qt) - P
                        cuts = [(0, P)] if qt != 3 else [(0, 512 - edge), (512 - edge, P)]
                        for a, z in cuts:
                            lo = S_of[qt] + edge + a
                            end = (part == 0 and qt == 0) or (part == 1 and (qt == 2 or a == 0))
                            ins = nc.tensor.matmul(S[:, lo:lo + z - a], c["identb"][:], c["trib"][:, a:z],
                                                   start=False, stop=end)
                    ins.then_inc(s_ready, 1)

                def transposes(u):
                    pe.wait_ge(exp_done, 4 * u + 4)
                    for k in range(3):
                        if u >= 1:
                            if k != 1:
                                pe.wait_ge(eva, 2 * u - 1 + k // 2)
                            else:
                                pe.wait_ge(evd, u)
                        for j, x in enumerate(TBANK[k]):
                            if x == "rem":
                                pe.wait_ge(rem_done, NT * (u + 1))
                                src = Prem[:, u % 2].rearrange("p t n -> p (t n)")
                            else:
                                src = Pm[:, u % 2, x[0], P * x[1]:P * x[1] + P]
                            ins = nc.tensor.transpose(ps[:, TB + k, P * j:P * j + P], src, c["ident"][:])
                        ins.then_inc(t_done, 1)

                def values(u):
                    s_, i, h = u // U, u % U // GH, u % GH
                    pe.wait_ge(eva, 2 * u + 2)
                    pe.wait_ge(evd, u + 1)
                    if h == 0 and u >= GH:
                        pe.wait_ge(o_done, u // GH)
                    b, gh = NB * s_ + i, g * GH * AR
                    for qt in range(NT):
                        for kt in range(qt + 1):
                            nc.tensor.matmul(Ob[:, qt, h, :], PT[:, u % 2, SLOT[qt, kt][2], :],
                                             V[:, b, kt, bass.ds(gh + AR * h, AR)],
                                             start=(h == 0 and qt == 0 and kt == 0), stop=False)
                    nc.tensor.matmul(Ob[:, :, h, :], PT[:, u % 2, SLOT["rem"][2], :],
                                     Vrem[:, b, bass.ds(g * GH + h, 1), :, :].rearrange("p a t r -> p (a t) r"),
                                     start=False, stop=(h == GH - 1)).then_inc(pv_done, 1)

                for k in range(2 * U + 2):
                    if k < 2 * U:
                        scores(k, 0)
                        step, n = k // U, k % U
                        project(pe, step, n, (NB * (1 - step)) + n // 4)
                        scores(k, 1)
                    if 1 <= k <= 2 * U:
                        transposes(k - 1)
                    if k >= 2:
                        values(k - 2)

            @block.vector
            def _(v):
                def maxima(u):
                    for part, tiles in ((0, (1, 0)), (1, (3, 2))):
                        v.wait_ge(s_ready, 2 * u + part + 1)
                        for qt in tiles:
                            nc.vector.tensor_reduce(nm[:, u % 2, qt:qt + 1], S[:, S_of[qt]:S_of[qt] + width(qt)],
                                                    AX.X, ALU.max, negate=True).then_inc(nm_ready, 1)

                def evacuate(u):
                    v.wait_ge(t_done, 3 * u + 2)
                    if u >= 2:
                        v.wait_ge(pv_done, u - 1)
                    nc.vector.tensor_copy(PT[:, u % 2, 4:8, :].rearrange("p j n -> p (j n)"), ps[:, TB + 1, :])\
                        .then_inc(evd, 1)

                def finish(u):
                    s_, i = u // U, u % U // GH
                    v.wait_ge(exp_done, 4 * u + 4)
                    if u >= GH:
                        v.wait_ge(o_done, u // GH)
                    nc.vector.reciprocal(rs[:, i].rearrange("p t h -> p (t h)"), sums[:, i].rearrange("p t h -> p (t h)"))\
                        .then_inc(o_rs, 1)
                    v.wait_ge(o_rs, u // GH + 1)
                    v.wait_ge(pv_done, u + 1)
                    t0 = (NB * s_ + i) * NT
                    out = Z[:, t0:t0 + NT, bass.ds(g * GH * AR, GH * AR)].rearrange("p t (h r) -> p t h r", r=AR)
                    for qt in range(NT):
                        ins = nc.vector.tensor_tensor(
                            out[:, qt], Ob[:, qt],
                            rs[:, i, qt, :].rearrange("p (h o) -> p h o", o=1).to_broadcast([P, GH, AR]), ALU.mult)
                    ins.then_inc(o_done, 1)

                for k in range(2 * U + 3):
                    if k < 2 * U:
                        maxima(k)
                        rotate_half(v, k // U, k % U)
                    if 1 <= k <= 2 * U:
                        evacuate(k - 1)
                    if k >= 2 + GH and (k - 2) % GH == 0:
                        finish(k - 3)

            @block.scalar
            def _(act):
                def exps(u):
                    i, h = u % U // GH, u % GH
                    if u >= 2:
                        act.wait_ge(t_done, 3 * (u - 1))
                        act.wait_ge(rem_done, NT * (u - 1))
                    if u >= U and h == 0:
                        act.wait_ge(o_rs, i + 1)
                    for part, tiles in ((0, (1, 0)), (1, (3, 2))):
                        act.wait_ge(nm_ready, 4 * u + 2 * part + 2)
                        for qt in tiles:
                            nc.scalar.activation(Pm[:, u % 2, qt, 0:width(qt)], S[:, S_of[qt]:S_of[qt] + width(qt)],
                                                 ACT.Exp, bias=nm[:, u % 2, qt:qt + 1],
                                                 accum_out=sums[:, i, qt, h:h + 1]).then_inc(exp_done, 1)

                def evacuate(u):
                    if u >= 2:
                        act.wait_ge(pv_done, u - 1)
                    for k, a, z in ((0, 0, 4), (2, 8, 11)):
                        act.wait_ge(t_done, 3 * u + k + 1)
                        nc.scalar.copy(PT[:, u % 2, a:z, :].rearrange("p j n -> p (j n)"), ps[:, TB + k, 0:P * (z - a)])\
                            .then_inc(eva, 1)

                for k in range(2 * U + 1):
                    if k < 2 * U:
                        exps(k)
                    if k >= 1:
                        evacuate(k - 1)
                    if k % 2 == 1 and k < 2 * U:
                        split_hi(act, k // U, k % U // 2)
        clear(nc, names)


def rope_tables():
    freq = (np.float32(10000.0) ** (np.arange(AD // 2, dtype=np.float32) / np.float32(AD / 2))).astype(np.float32)
    freq = np.concatenate([freq, freq])
    ang = (np.arange(N, dtype=np.float32)[:, None] / freq[None, :]).astype(np.float32)
    sign = np.where(np.arange(AD) < AD // 2, -1.0, 1.0)
    cos, sin = np.cos(ang).T, np.sin(ang).T * sign[:, None]
    q = AD ** -0.5
    t = np.stack([cos * q, sin * q, cos, sin], axis=1)
    return np.tile(t, (GH, 1, 1)).astype(np.float32)


def by_group(w):
    w = w.reshape(AG, GH, w.shape[1], w.shape[2]).transpose(0, 2, 1, 3)
    w = w.reshape(AG, w.shape[1], -1)
    return np.concatenate([w, w[:1]])


def swap(w):
    return np.roll(w, w.shape[-1] // 2, axis=-1)


def arrays_of(i):
    a = {"x": i["L0_attn_resid"]}
    wq, wk, bq, bk = i["L0_attn_W_Q"], i["L0_attn_W_K"], i["L0_attn_b_Q"], i["L0_attn_b_K"]
    a["a_w"] = np.stack([by_group(w) for w in (wq, swap(wq), wk, swap(wk))], axis=2)
    a["a_b"] = np.stack([by_group(b[:, None, :])[:, 0] for b in (bq, swap(bq), bk, swap(bk))], axis=2)
    a["a_vk"] = by_group(i["L0_attn_virtual_k"].transpose(1, 0, 2)).reshape(AG + 1, AV, P).transpose(0, 2, 1)
    a["a_vv"] = i["L0_attn_virtual_v"].reshape(AV, AH, AR)
    a["a_wv"] = i["L0_attn_W_V"].reshape(AH * AR, D).T
    a["a_bv"] = np.broadcast_to(i["L0_attn_b_V"].reshape(1, AH * AR), (P, AH * AR))
    a["a_wo"] = i["L0_attn_W_O"].reshape(2, P, D).transpose(1, 0, 2)
    a["a_tab"] = rope_tables()
    a["ident"] = np.eye(P, dtype=np.float32)
    kk = np.arange(P)
    a["tri"] = np.where(kk[None, :] > kk[:, None], BIG, 0.0).astype(np.float32)
    return a


def output_and_residual(nc, X, Z, ps, c, d):
    with ExitStack() as ctx:
        s = Store(nc, ctx, "o")
        wo = s.sb("wo", [P, 2, D])
        zT = s.sb("zT", [P, 2, 4, P])
        nrm = Norm(s, "on")
        names = w_in, t_done, t_used, y_done, link_, pow_, var_ = s.sems("w_in", "t_done", "t_used", "y_done", "link", "pow", "var")
        with nc.Block() as block:
            @block.sync
            def _(sp):
                sp.dma_start(wo[:], d["a_wo"]).then_inc(w_in, 16)
                sp.wait_ge(w_in, 16)

            @block.tensor
            def _(pe):
                pe.wait_ge(w_in, 16)

                def turn(n):
                    if n >= 2:
                        pe.wait_ge(t_used, n - 1)
                    for j in range(4):
                        ins = nc.tensor.transpose(ps[:, n % 2, P * j:P * j + P],
                                                  Z[:, 2 * n + j // 2, P * (j % 2):P * (j % 2) + P], c["ident"][:])
                    ins.then_inc(t_done, 1)

                turn(0)
                for n in range(TT // 2):
                    if n + 1 < TT // 2:
                        turn(n + 1)
                    pe.wait_ge(t_used, n + 1)
                    if n % 2 == 0 and n >= 4:
                        pe.wait_ge(var_, 2 * (n // 2 - 2) + 2)
                    for t in range(2):
                        for j in range(2):
                            ins = nc.tensor.matmul(ps[:, 2 + n // 2 % 2, P * (2 * (n % 2) + t):P * (2 * (n % 2) + t) + P],
                                                   zT[:, n % 2, 2 * t + j, :], wo[:, j, :], start=(j == 0), stop=(j == 1))
                    ins.then_inc(y_done, 1)

            @block.scalar
            def _(act):
                for n in range(TT // 2):
                    act.wait_ge(t_done, n + 1)
                    if n >= 2:
                        act.wait_ge(y_done, n - 1)
                    nc.scalar.copy(zT[:, n % 2].rearrange("p j n -> p (j n)"), ps[:, n % 2, :]).then_inc(t_used, 1)

            @block.gpsimd
            def _(pool):
                for b in range(B):
                    pool.wait_ge(var_, 2 * b + 1)
                    nrm.power(nc, c).then_inc(pow_, 1)

            @block.vector
            def _(v):
                link = Chain(v, link_)
                for b in range(B):
                    v.wait_ge(y_done, 2 * b + 2)
                    y = ps[:, 2 + b % 2, :].rearrange("p (t n) -> p t n", n=D)
                    nrm.variance(nc, link, y, EPS).then_inc(var_, 1)
                    v.wait_ge(pow_, b + 1)
                    nrm.apply(nc, link, nrm.out, y)
                    nc.vector.tensor_tensor(X[:, NT * b:NT * b + NT, :], X[:, NT * b:NT * b + NT, :], nrm.out[:],
                                            ALU.add).then_inc(var_, 1)
                    v.wait_ge(var_, 2 * b + 2)
        clear(nc, names)


class Norm:

    def __init__(self, s, name):
        self.st = s.sb(name + "_st", [P, NT, 6])
        self.mv = s.sb(name + "_mv", [P, NT, 2])
        self.rstd = s.sb(name + "_rstd", [P, NT])
        self.out = s.sb(name + "_out", [P, NT, D])

    def variance(self, nc, link, x, eps):
        for t in range(NT):
            link.add(nc.vector.bn_stats(self.st[:, t, :], x[:, t, :]))
        link.wait()
        for t in range(NT):
            link.add(nc.vector.bn_aggr(self.mv[:, t, :], self.st[:, t, :]))
        link.wait()
        return nc.vector.tensor_scalar(self.mv[:, :, 1], self.mv[:, :, 1], eps, None, ALU.add)

    def power(self, nc, c):
        return nc.gpsimd.tensor_tensor(self.rstd[:], self.mv[:, :, 1], c["mhalf"][:, 0:NT], ALU.pow)

    def apply(self, nc, link, out, x):
        for t in range(NT):
            link.add(nc.vector.tensor_scalar(out[:, t, :], x[:, t, :], self.mv[:, t, 0:1], self.rstd[:, t:t + 1],
                                             ALU.subtract, ALU.mult))
        link.wait()


FL, FH, FD = 2, 8, 64
FI = FH * FD
FW = 64
HID = int(D * 4 * 2 / 3)
HC = [(0, P), (P, 2 * P), (2 * P, HID)]


def local_layers(nc, X, ps, c, d):
    with ExitStack() as ctx:
        s = Store(nc, ctx, "f")
        wqkv = s.sb("wqkv", [P, FL, 3 * FI])
        wo = s.sb("wo", [P, FL, 4, D])
        w1 = s.sb("w1", [P, FL, 2 * HID])
        w2 = s.sb("w2", [P, FL, 3, D])
        b1 = s.sb("b1", [P, FL, 2 * HID])
        b2 = s.sb("b2", [P, FL, D])
        lgb = s.sb("lgb", [P, FL, 2])
        tab = s.sb("tab", [P, FL, 2, 2, NT, FD])
        band = s.sb("band", [P, 2, 2 * P])
        hs = s.sb("hs", [P, NT, D])
        kz = s.sb("kz", [P, FH, N + P])
        with ExitStack() as ctx0:
            s0 = Store(nc, ctx0, "f0")
            base = s0.sb("base", [P, 2, 2, NT, FD])
            sc = s0.sb("sc", [P, FL, 2, 2, FD])
            names = w_in, sc_in, done = s0.sems("w_in", "sc_in", "done")
            with nc.Block() as block:
                @block.sync
                def _(sp):
                    for dst, src in ((base, "f_base"), (sc, "f_sc")):
                        sp.dma_start(dst[:], d[src]).then_inc(sc_in, 16)
                    for dst, src in ((wqkv, "f_wqkv"), (wo, "f_wo"), (w1, "f_w1"), (b1, "f_b1"), (b2, "f_b2"),
                                     (lgb, "f_lgb"), (band, "f_band")):
                        sp.dma_start(dst[:], d[src]).then_inc(w_in, 16)
                    for k, (a, z) in enumerate(HC):
                        sp.dma_start(w2[0:z - a, :, k, :], d["f_w2"][a:z]).then_inc(w_in, 16)
                    sp.wait_ge(w_in, 160)

                @block.gpsimd
                def _(pool):
                    nc.gpsimd.memset(kz[:], 0.0).then_inc(done, 1)
                    nc.gpsimd.memset(hs[:], 0.0).then_inc(done, 1)

                @block.vector
                def _(v):
                    v.wait_ge(sc_in, 32)
                    for l in range(FL):
                        for cs in range(2):
                            for t in range(NT):
                                nc.vector.tensor_tensor(tab[:, l, cs, :, t, :], base[:, cs, :, t, :], sc[:, l, cs, :, :],
                                                        ALU.mult).then_inc(done, 1)
                    v.wait_ge(done, 2 + FL * 2 * NT)
            clear(nc, names)
        xb = s.sb("xb", [P, NT, D])
        hT = s.sb("hT", [P, N])
        QK = s.sb("QK", [P, 2, 2 * FI])
        R1 = s.sb("R1", [P, 2, 2 * FI])
        R2 = s.sb("R2", [P, 2 * FI])
        ss = s.sb("ss", [P, 2, 2 * FH])
        rr = s.sb("rr", [P, 2, 2 * FH])
        Vb = s.sb("Vb", [P, NT, FI])
        qT = s.sb("qT", [P, 4, N])
        Sm = s.sb("Sm", [P, 2, 2, 2 * P])
        nb = s.sb("nb", [P, 2, 2])
        Pe = s.sb("Pe", [P, 2, 2, 2 * P])
        PT = s.sb("PT", [P, 2, 4, P])
        sums = s.sb("sums", [P, NT, FH])
        rs = s.sb("rs", [P, NT, FH])
        on = s.sb("on", [P, 2, FI])
        oT = s.sb("oT", [P, 2, 4, P])
        UG = s.sb("UG", [P, 2, HID])
        UA = s.sb("UA", [P, 2, HID])
        G = s.sb("G", [P, 2, HID])
        HT = s.sb("HT", [P, 2, 3, P])
        yb = s.sb("yb", [P, 2, D])
        nrm = Norm(s, "fn")
        names = (xb_ready, sh_copy, sh_dma, tr, hT_done, hn_done, qkv_ready, qk_ev, v_ev, sq_done, ss_done, rr_done,
                 rot_done, qkT_ready, qT_ev, kT_ev, s_ready, sm_done, exp_done, pt_ready, pt_ev, pv_done, on_done,
                 oT_ready, oT_ev, y_ready, y_used, up_ready, ug_done, gelu_done, ua_done, h_done, hT2_ready, hT2_ev,
                 y2_ready, y2_used, link_, var_, pow_) = s.sems(
            *("xb_ready sh_copy sh_dma tr hT_done hn_done qkv_ready qk_ev v_ev sq_done ss_done rr_done rot_done "
              "qkT_ready qT_ev kT_ev s_ready sm_done exp_done pt_ready pt_ev pv_done on_done oT_ready oT_ev y_ready "
              "y_used up_ready ug_done gelu_done ua_done h_done hT2_ready hT2_ev y2_ready y2_used link var pow").split())
        HP = FH // 2
        UL = NT * HP
        qkv_bank = lambda T: 1 + 3 * (T % 2)
        with nc.Fori(0, B) as b:
            with nc.Block() as block:
                @block.sync
                def _(sp):
                    for j in range(2 * FL):
                        sp.wait_ge(xb_ready, j + 1)
                        sp.dma_start(hs[1:P, :, FW:D], xb[0:P - 1, :, FW:D]).then_inc(sh_dma, 16)
                        sp.dma_start(hs[0:1, 1:NT, FW:D], xb[P - 1:P, 0:NT - 1, FW:D]).then_inc(sh_dma, 16)
                    sp.wait_ge(sh_dma, 32 * 2 * FL)

                @block.gpsimd
                def _(pool):
                    def shift(j):
                        pool.wait_ge(xb_ready, j + 1)
                        nc.gpsimd.tensor_copy(hs[:, :, 0:FW], xb[:, :, 0:FW]).then_inc(sh_copy, 1)

                    pool.wait_ge(var_, 1)
                    nrm.power(nc, c).then_inc(pow_, 1)
                    for l in range(FL):
                        shift(2 * l)
                        for t in range(NT):
                            T = NT * l + t
                            pool.wait_ge(ss_done, T + 1)
                            if T >= 2:
                                pool.wait_ge(rot_done, T - 1)
                            nc.gpsimd.tensor_tensor(rr[:, T % 2, :], ss[:, T % 2, :], c["mhalf"][:, 0:2 * FH],
                                                    ALU.pow).then_inc(rr_done, 1)
                        shift(2 * l + 1)
                        pool.wait_ge(var_, 2 + l)
                        nrm.power(nc, c).then_inc(pow_, 1)
                    pool.wait_ge(var_, 2 + FL)
                    nrm.power(nc, c).then_inc(pow_, 1)

                @block.scalar
                def _(act):
                    for l in range(FL):
                        act.wait_ge(tr, 2 * l + 1)
                        nc.scalar.copy(hT[:], ps[:, 0, :]).then_inc(hT_done, 1)
                        for t in range(NT + 1):
                            if t < NT:
                                T = NT * l + t
                                act.wait_ge(qkv_ready, T + 1)
                                if T >= 2:
                                    act.wait_ge(rot_done, T - 1)
                                k = qkv_bank(T)
                                nc.scalar.copy(QK[:, T % 2, :], ps[:, k:k + 2, :].rearrange("p a n -> p (a n)")).then_inc(qk_ev, 1)
                                if l and t == 0:
                                    act.wait_ge(pv_done, UL * l)
                                nc.scalar.copy(Vb[:, t, :], ps[:, k + 2, :]).then_inc(v_ev, 1)
                            if t >= 1:
                                T = NT * l + t - 1
                                act.wait_ge(qkT_ready, T + 1)
                                nc.scalar.copy(qT[:, :, P * (t - 1):P * t], ps[:, 7, :].rearrange("p (h n) -> p h n", n=P))\
                                    .then_inc(qT_ev, 1)

                        def out_turn(t):
                            T = NT * l + t
                            act.wait_ge(oT_ready, T + 1)
                            if T >= 2:
                                act.wait_ge(y_ready, T - 1)
                            nc.scalar.copy(oT[:, T % 2].rearrange("p h n -> p (h n)"), ps[:, 0, :]).then_inc(oT_ev, 1)

                        for k in range(UL):
                            u = UL * l + k
                            t, hp = k // HP, k % HP
                            if u >= 2:
                                act.wait_ge(pt_ready, u - 1)
                            if l and k == 0:
                                act.wait_ge(on_done, NT * l)
                            for j in range(2):
                                act.wait_ge(sm_done, 2 * u + j + 1)
                                nc.scalar.activation(Pe[:, u % 2, j, :], Sm[:, u % 2, j, :], ACT.Exp, scale=-1.0,
                                                     bias=nb[:, u % 2, j:j + 1],
                                                     accum_out=sums[:, t, 2 * hp + j:2 * hp + j + 1]).then_inc(exp_done, 1)
                            if hp == 2 and t >= 1:
                                out_turn(t - 1)
                        out_turn(NT - 1)
                        act.wait_ge(tr, 2 * l + 2)
                        nc.scalar.activation(hT[:], ps[:, 0, :], ACT.Identity, scale=lgb[:, l, 0:1],
                                             bias=lgb[:, l, 1:2]).then_inc(hT_done, 1)
                        for t in range(NT + 1):
                            if t < NT:
                                T = NT * l + t
                                act.wait_ge(ug_done, T + 1)
                                if T >= 2:
                                    act.wait_ge(h_done, T - 1)
                                nc.scalar.activation(G[:, T % 2, :], UG[:, T % 2, :], ACT.Gelu).then_inc(gelu_done, 1)
                            if t >= 1:
                                T = NT * l + t - 1
                                act.wait_ge(hT2_ready, T + 1)
                                if T >= 2:
                                    act.wait_ge(y2_ready, T - 1)
                                for k, (a, z) in enumerate(HC):
                                    ins = nc.scalar.copy(HT[0:z - a, T % 2, k, :], ps[0:z - a, 5 + T % 2, P * k:P * k + P])
                                    ins.then_inc(hT2_ev, 1)

                @block.tensor
                def _(pe):
                    def turn(src, bank, n):
                        for j in range(n):
                            ins = nc.tensor.transpose(ps[:, bank, P * j:P * j + P], src(j), c["ident"][:])
                        return ins

                    for l in range(FL):
                        pe.wait_ge(sh_copy, 2 * l + 1)
                        pe.wait_ge(sh_dma, 32 * (2 * l + 1))
                        turn(lambda j: hs[:, j, :], 0, NT).then_inc(tr, 1)
                        pe.wait_ge(hT_done, 2 * l + 1)
                        for t in range(NT + 1):
                            if t < NT:
                                T = NT * l + t
                                if T >= 2:
                                    pe.wait_ge(v_ev, T - 1)
                                if l and t == 0:
                                    pe.wait_ge(y2_used, 2 * NT * l)
                                for j in range(3):
                                    ins = nc.tensor.matmul(ps[:, qkv_bank(T) + j, :], hT[:, P * t:P * t + P],
                                                           wqkv[:, l, FI * j:FI * j + FI], start=True, stop=True)
                                ins.then_inc(qkv_ready, 1)
                            if t >= 1:
                                T = NT * l + t - 1
                                pe.wait_ge(rot_done, T + 1)
                                if t >= 2:
                                    pe.wait_ge(qT_ev, T)
                                    pe.wait_ge(kT_ev, 2 * T)
                                turn(lambda j: R1[:, T % 2, P * j:P * j + P], 7, 4)
                                turn(lambda j: R1[:, T % 2, FI + P * j:FI + P * j + P], 0, 4).then_inc(qkT_ready, 1)

                        def scores(k):
                            u = UL * l + k
                            t, hp = k // HP, k % HP
                            if k == 0:
                                pe.wait_ge(qT_ev, NT * (l + 1))
                                pe.wait_ge(kT_ev, 2 * NT * (l + 1))
                                pe.wait_ge(v_ev, NT * (l + 1))
                            if u >= 2:
                                pe.wait_ge(sm_done, 2 * (u - 1))
                            for j in range(2):
                                ins = nc.tensor.matmul(ps[:, 1 + u % 2, 2 * P * j:2 * P * j + 2 * P],
                                                       qT[:, hp, P * t:P * t + P], kz[:, 2 * hp + j, P * t:P * t + 2 * P],
                                                       start=True, stop=True)
                            ins.then_inc(s_ready, 1)

                        def p_turn(k):
                            u = UL * l + k
                            pe.wait_ge(exp_done, 2 * u + 2)
                            if u >= 2:
                                pe.wait_ge(pt_ev, u - 1)
                            turn(lambda j: Pe[:, u % 2, j // 2, P * (j % 2):P * (j % 2) + P], 3 + u % 2, 4).then_inc(pt_ready, 1)

                        def values(k):
                            u = UL * l + k
                            t, hp = k // HP, k % HP
                            T = NT * l + t
                            pe.wait_ge(pt_ev, u + 1)
                            if hp == 0 and T >= 2:
                                pe.wait_ge(on_done, T - 1)
                            for j in range(2):
                                h = 2 * hp + j
                                kts = [0, 1] if t else [1]
                                for i in kts:
                                    ins = nc.tensor.matmul(ps[:, 5 + T % 2, FD * h:FD * h + FD], PT[:, u % 2, 2 * j + i, :],
                                                           Vb[:, t - 1 + i, FD * h:FD * h + FD], start=(i == kts[0]), stop=(i == 1))
                            ins.then_inc(pv_done, 1)

                        def out(t):
                            T = NT * l + t
                            pe.wait_ge(on_done, T + 1)
                            if T >= 1:
                                pe.wait_ge(oT_ev, T)
                            turn(lambda j: on[:, T % 2, P * j:P * j + P], 0, 4).then_inc(oT_ready, 1)
                            pe.wait_ge(oT_ev, T + 1)
                            if T >= 1 and t >= 1:
                                pe.wait_ge(y_used, T)
                            for j in range(4):
                                ins = nc.tensor.matmul(ps[:, 7, 0:D], oT[:, T % 2, j, :], wo[:, l, j, :],
                                                       start=(j == 0), stop=(j == 3))
                            ins.then_inc(y_ready, 1)

                        for k in range(UL + 2):
                            if k < UL:
                                scores(k)
                            if 1 <= k <= UL:
                                p_turn(k - 1)
                            if k >= 2:
                                values(k - 2)
                                if (k - 2) % HP == 1 and k - 2 > HP:
                                    out((k - 2) // HP - 1)
                        out(NT - 1)
                        pe.wait_ge(hn_done, l + 1)
                        turn(lambda j: nrm.out[:, j, :], 0, NT).then_inc(tr, 1)
                        pe.wait_ge(hT_done, 2 * l + 2)
                        for t in range(NT + 1):
                            if t < NT:
                                T = NT * l + t
                                if t >= 2:
                                    pe.wait_ge(ua_done, T - 1)
                                for j in range(2):
                                    ins = nc.tensor.matmul(ps[:, 1 + 2 * (T % 2) + j, 0:HID], hT[:, P * t:P * t + P],
                                                           w1[:, l, HID * j:HID * j + HID], start=True, stop=True)
                                ins.then_inc(up_ready, 1)
                            if t >= 1:
                                T = NT * l + t - 1
                                pe.wait_ge(h_done, T + 1)
                                if T >= 2:
                                    pe.wait_ge(hT2_ev, 3 * (T - 1))
                                for k, (a, z) in enumerate(HC):
                                    ins = nc.tensor.transpose(ps[0:z - a, 5 + T % 2, P * k:P * k + P], UA[:, T % 2, a:z],
                                                              c["ident"][:])
                                ins.then_inc(hT2_ready, 1)
                                pe.wait_ge(hT2_ev, 3 * (T + 1))
                                if T >= 1:
                                    pe.wait_ge(y2_used, 2 * T)
                                for k, (a, z) in enumerate(HC):
                                    ins = nc.tensor.matmul(ps[:, 7, 0:D], HT[0:z - a, T % 2, k, :], w2[0:z - a, l, k, :],
                                                           start=(k == 0), stop=(k == 2))
                                ins.then_inc(y2_ready, 1)

                @block.vector
                def _(v):
                    link = Chain(v, link_)
                    xs = X[:, bass.ds(b * NT, NT), :]

                    def norm(out, x, eps, n):
                        nrm.variance(nc, link, x, eps).then_inc(var_, 1)
                        v.wait_ge(pow_, n)
                        nrm.apply(nc, link, out, x)

                    norm(xb, xs, EPS, 1)
                    nc.vector.tensor_copy(yb[:, 0, 0:1], xb[:, 0, 0:1]).then_inc(xb_ready, 1)
                    for l in range(FL):
                        def rotate(t):
                            T = NT * l + t
                            v.wait_ge(qk_ev, T + 1)
                            q4 = QK[:, T % 2].rearrange("p (k h e) -> p k h e", k=2, e=FD)
                            r4 = R1[:, T % 2].rearrange("p (k h e) -> p k h e", k=2, e=FD)
                            s4 = R2[:].rearrange("p (k h e) -> p k h e", k=2, e=FD)
                            if T >= 2:
                                v.wait_ge(qkT_ready, T - 1)
                            link.step(nc.vector.tensor_tensor(R2[:], QK[:, T % 2], QK[:, T % 2], ALU.mult))
                            link.step(nc.vector.tensor_reduce(ss[:, T % 2, :], R2[:].rearrange("p (h e) -> p h e", e=FD),
                                                              AX.X, ALU.add))
                            nc.vector.tensor_scalar(ss[:, T % 2, :], ss[:, T % 2, :], 1e-24, None, ALU.max).then_inc(ss_done, 1)
                            for k in range(2):
                                cos = tab[:, l, 0, k, t, :].rearrange("p (h e) -> p h e", h=1).to_broadcast([P, FH, FD])
                                link.add(nc.vector.tensor_tensor(r4[:, k], q4[:, k], cos, ALU.mult))
                                for z in range(2):
                                    e, f = slice(32 * z, 32 * z + 32), slice(32 - 32 * z, 64 - 32 * z)
                                    sin = tab[:, l, 1, k, t, e].rearrange("p (h e) -> p h e", h=1).to_broadcast([P, FH, FD // 2])
                                    link.add(nc.vector.tensor_tensor(s4[:, k, :, e], q4[:, k, :, f], sin, ALU.mult))
                            link.wait()
                            link.step(nc.vector.tensor_tensor(R1[:, T % 2], R1[:, T % 2], R2[:], ALU.add))
                            v.wait_ge(rr_done, T + 1)
                            nc.vector.tensor_tensor(
                                R1[:, T % 2].rearrange("p (h e) -> p h e", e=FD), R1[:, T % 2].rearrange("p (h e) -> p h e", e=FD),
                                rr[:, T % 2, :].rearrange("p (h o) -> p h o", o=1).to_broadcast([P, 2 * FH, FD]),
                                ALU.mult).then_inc(rot_done, 1)

                        def key_turn(t):
                            T = NT * l + t
                            v.wait_ge(qkT_ready, T + 1)
                            for z in range(2):
                                r = slice(64 * z, 64 * z + 64)
                                ins = nc.vector.tensor_copy(kz[r, z:FH:2, P * (t + 1):P * (t + 2)],
                                                            ps[r, 0, :].rearrange("p (h n) -> p h n", n=P))
                                ins.then_inc(kT_ev, 1)

                        def mask(k):
                            u = UL * l + k
                            t = k // HP
                            v.wait_ge(s_ready, u + 1)
                            if u >= 2:
                                v.wait_ge(exp_done, 2 * (u - 1))
                            for j in range(2):
                                nc.vector.tensor_tensor_reduce(
                                    out=Sm[:, u % 2, j, :], in0=ps[:, 1 + u % 2, 2 * P * j:2 * P * j + 2 * P],
                                    in1=band[:, min(t, 1), :], scale=-8.0, scalar=-8 * BIG, op0=ALU.add, op1=ALU.min,
                                    accum_out=nb[:, u % 2, j:j + 1]).then_inc(sm_done, 1)

                        def p_evac(k):
                            u = UL * l + k
                            v.wait_ge(pt_ready, u + 1)
                            if u >= 2:
                                v.wait_ge(pv_done, u - 1)
                            nc.vector.tensor_copy(PT[:, u % 2].rearrange("p j n -> p (j n)"), ps[:, 3 + u % 2, :]).then_inc(pt_ev, 1)

                        def divide(t):
                            T = NT * l + t
                            v.wait_ge(exp_done, 2 * (UL * l + HP * (t + 1)))
                            link.step(nc.vector.reciprocal(rs[:, t, :], sums[:, t, :]))
                            v.wait_ge(pv_done, UL * l + HP * (t + 1))
                            if T >= 2:
                                v.wait_ge(oT_ready, T - 1)
                            nc.vector.tensor_tensor(
                                on[:, T % 2].rearrange("p (h e) -> p h e", e=FD), ps[:, 5 + T % 2, :].rearrange("p (h e) -> p h e", e=FD),
                                rs[:, t, :].rearrange("p (h o) -> p h o", o=1).to_broadcast([P, FH, FD]), ALU.mult).then_inc(on_done, 1)

                        def attention_residual(t):
                            T = NT * l + t
                            v.wait_ge(y_ready, T + 1)
                            ins = nc.vector.tensor_tensor(xb[:, t, :], xb[:, t, :], ps[:, 7, 0:D], ALU.add)
                            ins.then_inc(y_used, 1)

                        for t in range(NT + 1):
                            if t < NT:
                                rotate(t)
                            if t >= 1:
                                key_turn(t - 1)
                        for k in range(UL + 4):
                            if k < UL:
                                mask(k)
                            if 1 <= k <= UL:
                                p_evac(k - 1)
                            if k >= 3 and (k - 3) % HP == HP - 1:
                                divide((k - 3) // HP)
                            if k >= 2 + HP and (k - 2) % HP == 2 and (k - 2) // HP - 1 < NT - 1:
                                attention_residual((k - 2) // HP - 1)
                        attention_residual(NT - 1)
                        v.wait_ge(y_used, NT * (l + 1))
                        nc.vector.tensor_copy(yb[:, 1, 0:1], xb[:, 0, 0:1]).then_inc(xb_ready, 1)
                        v.wait_ge(sh_copy, 2 * l + 2)
                        v.wait_ge(sh_dma, 32 * (2 * l + 2))
                        norm(nrm.out, hs, EPS, 2 + l)
                        nc.vector.tensor_copy(yb[:, 0, 1:2], nrm.out[:, 0, 0:1]).then_inc(hn_done, 1)
                        for t in range(NT + 1):
                            if t < NT:
                                T = NT * l + t
                                k = 1 + 2 * (T % 2)
                                v.wait_ge(up_ready, T + 1)
                                if T >= 2:
                                    v.wait_ge(gelu_done, T - 1)
                                nc.vector.tensor_tensor(UG[:, T % 2, :], ps[:, k + 1, 0:HID], b1[:, l, HID:2 * HID],
                                                        ALU.add).then_inc(ug_done, 1)
                                if T >= 2:
                                    v.wait_ge(hT2_ready, T - 1)
                                nc.vector.tensor_tensor(UA[:, T % 2, :], ps[:, k, 0:HID], b1[:, l, 0:HID],
                                                        ALU.add).then_inc(ua_done, 1)
                                v.wait_ge(ua_done, T + 1)
                                v.wait_ge(gelu_done, T + 1)
                                nc.vector.tensor_tensor(UA[:, T % 2, :], UA[:, T % 2, :], G[:, T % 2, :], ALU.mult).then_inc(h_done, 1)
                            if t >= 1:
                                T = NT * l + t - 1
                                v.wait_ge(y2_ready, T + 1)
                                if T >= 2:
                                    v.wait_ge(y2_used, 2 * (T - 1))
                                nc.vector.tensor_tensor(yb[:, T % 2, :], ps[:, 7, 0:D], b2[:, l, :], ALU.add).then_inc(y2_used, 1)
                                v.wait_ge(y2_used, 2 * T + 1)
                                nc.vector.tensor_tensor(xb[:, t - 1, :], xb[:, t - 1, :], yb[:, T % 2, :], ALU.add).then_inc(y2_used, 1)
                        v.wait_ge(y2_used, 2 * NT * (l + 1))
                        if l + 1 < FL:
                            nc.vector.tensor_copy(yb[:, 0, 0:1], xb[:, 0, 0:1]).then_inc(xb_ready, 1)
                            v.wait_ge(xb_ready, 2 * l + 3)
                    norm(nrm.out, xb, EPS, 2 + FL)
                    link.step(nc.vector.tensor_tensor(xs, xs, nrm.out[:], ALU.add))
            clear(nc, names)


def xpos_tables():
    half = np.arange(0, FD, 2, dtype=np.float32)
    inv = (1.0 / 10000.0 ** (half / FD)).astype(np.float32)
    t = np.arange(N, dtype=np.float32)
    fr = (t[:, None] * inv[None, :]).astype(np.float32)
    fr = np.concatenate([fr, fr], axis=-1)
    base = ((half + 0.4 * FD) / (1.4 * FD)).astype(np.float32)
    power = ((t - N // 2) / float(FW // 2)).astype(np.float32)
    scale = (base[None, :] ** power[:, None]).astype(np.float32)
    scale = np.concatenate([scale, scale], axis=-1)
    sign = np.where(np.arange(FD) < FD // 2, -1.0, 1.0)
    cos, sin = np.cos(fr), np.sin(fr) * sign
    a = np.stack([np.stack([cos * scale, cos / scale]), np.stack([sin * scale, sin / scale])])
    return a.reshape(2, 2, NT, P, FD).transpose(3, 0, 1, 2, 4).astype(np.float32)


def band_masks():
    q, k = np.arange(P)[:, None], np.arange(2 * P)[None, :]
    ok = (k <= q + P) & (k >= q + P - FW)
    return np.stack([np.where(ok & (k >= P), 0.0, BIG), np.where(ok, 0.0, BIG)], axis=1).astype(np.float32)


def rows(v):
    return np.broadcast_to(v[None], (P,) + v.shape)


def arrays_of_layers(i):
    qs, ks = i["L0_ffn_q_scale"], i["L0_ffn_k_scale"]
    return {
        "f_wqkv": i["L0_ffn_wqkv"].transpose(1, 0, 2),
        "f_wo": i["L0_ffn_wo"].reshape(FL, 4, P, D).transpose(2, 0, 1, 3),
        "f_w1": i["L0_ffn_w1"].transpose(1, 0, 2),
        "f_w2": i["L0_ffn_w2"].transpose(1, 0, 2),
        "f_b1": rows(i["L0_ffn_b1"]),
        "f_b2": rows(i["L0_ffn_b2"]),
        "f_lgb": np.stack([i["L0_ffn_ln_g"], i["L0_ffn_ln_b"]], axis=-1).transpose(1, 0, 2),
        "f_sc": rows(np.stack([np.stack([qs, ks], 1), np.stack([swap(qs), swap(ks)], 1)], 1)),
        "f_base": xpos_tables(),
        "f_band": band_masks(),
    }


RH, RD = 16, 8
RG = 4
RW = 2 * N
BW = N + P
MAX_LEN = 625


def relative_attention(nc, X, ps, c, d):
    with ExitStack() as ctx:
        s = Store(nc, ctx, "r")
        Qu = s.sb("Qu", [P, RG, B * N], F32R)
        Qv = s.sb("Qv", [P, RG, B * N], F32R)
        Kst = s.sb("Kst", [P, RG, B * N], F32R)
        Rst = s.sb("Rst", [P, RG, RW], F32R)
        V = s.sb("V", [P, B, NT, P])
        wo = s.sb("wo", [P, D])
        bo = s.sb("bo", [P, D])
        hm = s.sb("hm", [P, RG])
        sel = s.sb("sel", [RH, P])
        with ExitStack() as ctx0:
            make_stacks(nc, Store(nc, ctx0, "r0"), X, ps, c, d, Qu, Qv, Kst, Rst, V, wo, bo, hm, sel)
        relative_heads(nc, s, X, ps, c, d, Qu, Qv, Kst, Rst, V, wo, bo, hm, sel)


def make_stacks(nc, s, X, ps, c, d, Qu, Qv, Kst, Rst, V, wo, bo, hm, sel):
    w = s.sb("w", [P, 4, P])
    gb = s.sb("gb", [P, 2])
    uv = s.sb("uv", [P, 2])
    emb = s.sb("emb", [P, RW])
    xT = s.sb("xT", [P, N])
    full = s.sb("full", [P, 3, N])
    hi = s.sb("hi", [P, 3, B * N], F32R)
    lo = s.sb("lo", [P, 3, B * N], F32R)
    rhi = s.sb("rhi", [P, RW], F32R)
    rlo = s.sb("rlo", [P, RW], F32R)
    n1, n2 = Norm(s, "n1"), Norm(s, "n2")
    names = (w_in, r_ready, rhi_done, rlo_done, norm_done, tr, xT_done, p_ready, full_done, v_ev, hi_done, lo_done,
             stacked, link_, var_, pow_) = s.sems(
        *"w_in r_ready rhi_done rlo_done norm_done tr xT_done p_ready full_done v_ev hi_done lo_done stacked link var pow".split())

    def stack(sp, dst, halves):
        for g in range(RG):
            for k, src in enumerate(halves):
                sp.dma_start(dst[32 * k:32 * k + 32, g].bitcast(F32), src[32 * g:32 * g + 32].bitcast(F32)).then_inc(stacked, 16)

    with nc.Block() as block:
        @block.sync
        def _(sp):
            for dst, src in ((w, "r_w"), (gb, "r_gb"), (uv, "r_uv"), (emb, "r_emb"), (wo, "r_wo"), (bo, "r_bo"), (hm, "r_hm"), (sel, "r_sel")):
                sp.dma_start(dst[:], d[src]).then_inc(w_in, 16)
            sp.wait_ge(rhi_done, 1)
            sp.wait_ge(rlo_done, 2)
            stack(sp, Rst, (rhi, rhi, rlo, rlo))
            sp.wait_ge(stacked, 256)

        @block.tensor
        def _(pe):
            pe.wait_ge(w_in, 128)
            for k in range(2):
                ins = nc.tensor.matmul(ps[:, k, :], w[:, 3, :], emb[:, N * k:N * k + N], start=True, stop=True)
            ins.then_inc(r_ready, 1)

        @block.scalar
        def _(act):
            act.wait_ge(r_ready, 1)
            nc.scalar.copy(rhi[:], ps[:, 0:2, :].rearrange("p a n -> p (a n)")).then_inc(rhi_done, 1)

        @block.vector
        def _(v):
            v.wait_ge(rhi_done, 1)
            for k in range(2):
                nc.vector.tensor_tensor(rlo[:, N * k:N * k + N], ps[:, k, :], rhi[:, N * k:N * k + N].bitcast(F32),
                                        ALU.subtract).then_inc(rlo_done, 1)
    clear(nc, names)

    with nc.Fori(0, B) as b:
        with nc.Block() as block:
            @block.gpsimd
            def _(pool):
                for k, n in enumerate((n1, n2)):
                    pool.wait_ge(var_, k + 1)
                    n.power(nc, c).then_inc(pow_, 1)

            @block.tensor
            def _(pe):
                pe.wait_ge(norm_done, 1)
                for t in range(NT):
                    ins = nc.tensor.transpose(ps[:, 0, P * t:P * t + P], n2.out[:, t, :], c["ident"][:])
                ins.then_inc(tr, 1)
                pe.wait_ge(xT_done, 1)
                for j in range(2):
                    nc.tensor.matmul(ps[:, 1 + j, :], w[:, j, :], xT[:], start=True, stop=True).then_inc(p_ready, 1)
                for t in range(NT):
                    ins = nc.tensor.matmul(ps[:, 3, P * t:P * t + P], xT[:, P * t:P * t + P], w[:, 2, :],
                                           start=True, stop=True)
                ins.then_inc(p_ready, 1)

            @block.scalar
            def _(act):
                act.wait_ge(tr, 1)
                nc.scalar.activation(xT[:], ps[:, 0, :], ACT.Identity, scale=gb[:, 0:1], bias=gb[:, 1:2]).then_inc(xT_done, 1)
                act.wait_ge(p_ready, 3)
                nc.scalar.copy(V[:, bass.ds(b, 1)].rearrange("p b t n -> p (b t n)"), ps[:, 3, :]).then_inc(v_ev, 1)
                for j in range(3):
                    act.wait_ge(full_done, j + 1)
                    nc.scalar.copy(hi[:, j, bass.ds(b * N, N)], full[:, j, :]).then_inc(hi_done, 1)

            @block.vector
            def _(v):
                link = Chain(v, link_)
                n1.variance(nc, link, X[:, bass.ds(b * NT, NT), :], EPS).then_inc(var_, 1)
                v.wait_ge(pow_, 1)
                n1.apply(nc, link, n1.out, X[:, bass.ds(b * NT, NT), :])
                n2.variance(nc, link, n1.out, 1e-6).then_inc(var_, 1)
                v.wait_ge(pow_, 2)
                n2.apply(nc, link, n2.out, n1.out)
                nc.vector.tensor_copy(n1.rstd[:, 0:1], n2.out[:, 0, 0:1]).then_inc(norm_done, 1)
                v.wait_ge(p_ready, 1)
                for j in range(2):
                    nc.vector.tensor_scalar(full[:, j, :], ps[:, 1, :], uv[:, j:j + 1], None, ALU.add).then_inc(full_done, 1)
                v.wait_ge(p_ready, 2)
                nc.vector.tensor_copy(full[:, 2, :], ps[:, 2, :]).then_inc(full_done, 1)
                for j in range(3):
                    v.wait_ge(full_done, j + 1)
                    v.wait_ge(hi_done, j + 1)
                    nc.vector.tensor_tensor(lo[:, j, bass.ds(b * N, N)], full[:, j, :], hi[:, j, bass.ds(b * N, N)].bitcast(F32),
                                            ALU.subtract).then_inc(lo_done, 1)
        clear(nc, names)

    with nc.Block() as block:
        @block.sync
        def _(sp):
            stack(sp, Qu, (hi[:, 0], lo[:, 0], hi[:, 0], lo[:, 0]))
            stack(sp, Qv, (hi[:, 1], lo[:, 1], hi[:, 1], lo[:, 1]))
            stack(sp, Kst, (hi[:, 2], hi[:, 2], lo[:, 2], lo[:, 2]))
            sp.wait_ge(stacked, 768)
    clear(nc, names)


def relative_heads(nc, s, X, ps, c, d, Qu, Qv, Kst, Rst, V, wo, bo, hm, sel):
    STEPS = RH * NT
    PAIRS = STEPS // 2
    BUFS, SCRATCH = 3, 5
    LAG = 8
    spill = [nc.dram_tensor(f"spill{k}", (2, P, BW), F32, kind="Internal").ap() for k in range(SCRATCH)]
    qu = s.sb("qu", [P, 2, N], F32R)
    qv = s.sb("qv", [P, 2, N], F32R)
    BD = s.sb("BD", [P, BUFS, 2, BW])
    Sx = s.sb("Sx", [P, SCRATCH, 2, N])
    PT = s.sb("PT", [P, 2, NT, N])
    Vm = s.sb("Vm", [P, NT, RG, P])
    nb = s.sb("nb", [P, 2, NT])
    sums = s.sb("sums", [P, NT, RH])
    rs = s.sb("rs", [P, NT, RH])
    rsT = s.sb("rsT", [RH, N])
    oT = s.sb("oT", [P, N])
    yb = s.sb("yb", [P, NT, D])
    nrm = Norm(s, "n")
    names = (qv_done, qu_done, bd_ready, bd_ev, wr0, wr1, wr2, rd0, rd1, rd2, rd3, rd4, ac_ready, sx_done, exp_done, t_ready,
             t_ev, pv_done, rs_done, on_done, zeroed, vm_done, rs_tr, rs_ev, rs_ready, o_ev, y_ready, y_done, link_, var_, pow_) = s.sems(
        *("qv_done qu_done bd_ready bd_ev wr0 wr1 wr2 rd0 rd1 rd2 rd3 rd4 ac_ready sx_done exp_done t_ready t_ev pv_done rs_done "
          "on_done zeroed vm_done rs_tr rs_ev rs_ready o_ev y_ready y_done link var pow").split())
    wr, rd = (wr0, wr1, wr2), (rd0, rd1, rd2, rd3, rd4)
    assert len(rd) == SCRATCH and len(wr) == BUFS
    BDB = (0, 1, 7)
    HW = BW // 2
    SCALE = RD ** -0.5
    with nc.Fori(0, B) as b:
        with nc.Block() as block:
            @block.sync
            def _(sp):
                for k in range(PAIRS + 1):
                    if k < PAIRS:
                        sp.wait_ge(bd_ev, 4 * (k + 1))
                        if k >= SCRATCH:
                            sp.wait_ge(rd[k % SCRATCH], 16 * (k // SCRATCH))
                        sp.dma_start(spill[k % SCRATCH].rearrange("t p n -> p t n"), BD[:, k % BUFS])\
                            .then_inc(wr[k % BUFS], 16)
                    if k >= 1:
                        m = k - 1
                        sp.wait_ge(wr[m % BUFS], 16 * (m // BUFS + 1))
                        if m >= SCRATCH:
                            sp.wait_ge(t_ready, 2 * (m - SCRATCH + 1))
                        a = spill[m % SCRATCH]
                        skew = bass.AP(tensor=a.tensor, offset=P - 1, ap=[[BW - 1, P], [P * BW, 2], [1, N]])
                        sp.dma_start(Sx[:, m % SCRATCH], skew).then_inc(rd[m % SCRATCH], 16)
                for k in range(SCRATCH):
                    sp.wait_ge(rd[k], 16 * len(range(k, PAIRS, SCRATCH)))

            @block.gpsimd
            def _(pool):
                nc.gpsimd.memset(Vm[:], 0.0).then_inc(zeroed, 1)
                pool.wait_ge(var_, 1)
                nrm.power(nc, c).then_inc(pow_, 1)

            @block.tensor
            def _(pe):
                def relative(n):
                    h, lt = n // NT, n % NT
                    pe.wait_ge(qv_done, h + 1)
                    for j in range(2):
                        m = 2 * n + j
                        if m >= 3:
                            pe.wait_ge(bd_ev, m - 2)
                        r0 = N - P - P * lt + HW * j
                        nc.tensor.matmul(ps[:, BDB[m % 3], 0:HW], qv[:, h % 2, P * lt:P * lt + P],
                                         Rst[:, h // RG, r0:r0 + HW], start=True, stop=True).then_inc(bd_ready, 1)

                def content(n):
                    h, lt = n // NT, n % NT
                    pe.wait_ge(qu_done, h + 1)
                    if n >= 2:
                        pe.wait_ge(sx_done, n - 1)
                    nc.tensor.matmul(ps[:, 2 + n % 2, :], qu[:, h % 2, P * lt:P * lt + P], Kst[:, h // RG, bass.ds(b * N, N)],
                                     start=True, stop=True).then_inc(ac_ready, 1)

                def turn(n):
                    pe.wait_ge(exp_done, n + 1)
                    if n >= 2:
                        pe.wait_ge(t_ev, n - 1)
                    for j in range(NT):
                        ins = nc.tensor.transpose(ps[:, 4 + n % 2, P * j:P * j + P],
                                                  Sx[:, n // 2 % SCRATCH, n % 2, P * j:P * j + P], c["ident"][:])
                    ins.then_inc(t_ready, 1)

                def values(n):
                    h, kt = n // NT, n % NT
                    if kt == 0:
                        pe.wait_ge(t_ev, NT * (h + 1))
                    if n == 0:
                        pe.wait_ge(vm_done, RG)
                    r = 32 * (h // RG)
                    nc.tensor.matmul(ps[r:r + 32, 6, :], Vm[:, kt, h // RG, 32 * (h % RG):32 * (h % RG) + 32],
                                     PT[:, h % 2, kt, :], start=(h % RG == 0 and kt == 0),
                                     stop=(h % RG == RG - 1 and kt == NT - 1)).then_inc(pv_done, 1)

                for k in range(STEPS + LAG + 6):
                    if k < STEPS:
                        relative(k)
                    for part, late in ((content, LAG), (turn, LAG + 2), (values, LAG + 6)):
                        if 0 <= k - late < STEPS:
                            part(k - late)
                pe.wait_ge(rs_done, 1)
                for t in range(NT):
                    ins = nc.tensor.transpose(ps[0:RH, 0, P * t:P * t + P], rs[:, t, :], c["ident"][:])
                ins.then_inc(rs_tr, 1)
                pe.wait_ge(rs_ev, 1)
                nc.tensor.matmul(ps[:, 1, :], sel[:], rsT[:], start=True, stop=True).then_inc(rs_ready, 1)
                pe.wait_ge(on_done, 1)
                for t in range(NT):
                    ins = nc.tensor.matmul(ps[:, 0, P * t:P * t + P], oT[:, P * t:P * t + P], wo[:], start=True, stop=True)
                ins.then_inc(y_ready, 1)

            @block.scalar
            def _(act):
                def relative(n):
                    if n % 2 == 0 and n // 2 >= BUFS:
                        act.wait_ge(wr[n // 2 % BUFS], 16 * (n // 2 // BUFS))
                    for j in range(2):
                        m = 2 * n + j
                        act.wait_ge(bd_ready, m + 1)
                        nc.scalar.copy(BD[:, n // 2 % BUFS, n % 2, HW * j:HW * j + HW], ps[:, BDB[m % 3], 0:HW])\
                            .then_inc(bd_ev, 1)

                def exps(n):
                    h, lt = n // NT, n % NT
                    act.wait_ge(sx_done, n + 1)
                    row = Sx[:, n // 2 % SCRATCH, n % 2, :]
                    nc.scalar.activation(row, row, ACT.Exp, scale=-1.0, bias=nb[:, h % 2, lt:lt + 1],
                                         accum_out=sums[:, lt, h:h + 1]).then_inc(exp_done, 1)

                act.wait_ge(zeroed, 1)
                for k in range(STEPS + LAG):
                    if k < STEPS:
                        relative(k)
                    if 1 <= k <= RG:
                        r = k - 1
                        nc.scalar.copy(Vm[:, :, :, 40 * r:40 * r + RD],
                                       V[:, bass.ds(b, 1)].rearrange("p b t (g e) -> p (b t) g e", g=RG)
                                       [:, :, :, RD * r:RD * r + RD]).then_inc(vm_done, 1)
                    if k >= LAG:
                        exps(k - LAG)
                act.wait_ge(rs_tr, 1)
                nc.scalar.copy(rsT[:], ps[0:RH, 0, :]).then_inc(rs_ev, 1)
                act.wait_ge(pv_done, STEPS)
                nc.scalar.copy(oT[:], ps[:, 6, :]).then_inc(o_ev, 1)

            @block.vector
            def _(v):
                def mask(dst, src, h, done, free, per):
                    if h >= 2:
                        v.wait_ge(free, per * (h - 1))
                    nc.vector.tensor_scalar(dst[:, h % 2, :], src[:, h // RG, bass.ds(b * N, N)].bitcast(F32),
                                            hm[:, h % RG:h % RG + 1], None, ALU.mult).then_inc(done, 1)

                def add(n):
                    h, lt, m = n // NT, n % NT, n // 2
                    v.wait_ge(ac_ready, n + 1)
                    v.wait_ge(rd[m % SCRATCH], 16 * (m // SCRATCH + 1))
                    if n >= 2 * NT:
                        v.wait_ge(exp_done, n - 2 * NT + 1)
                    row = Sx[:, m % SCRATCH, n % 2, :]
                    nc.vector.tensor_tensor_reduce(
                        out=row, in0=ps[:, 2 + n % 2, :], in1=row, scale=-SCALE,
                        scalar=-BIG, op0=ALU.add, op1=ALU.min, accum_out=nb[:, h % 2, lt:lt + 1]).then_inc(sx_done, 1)

                def evacuate(n):
                    v.wait_ge(t_ready, n + 1)
                    h, lt = n // NT, n % NT
                    if h >= 2:
                        v.wait_ge(pv_done, NT * (h - 1))
                    nc.vector.tensor_copy(PT[:, h % 2, :, P * lt:P * lt + P],
                                          ps[:, 4 + n % 2, :].rearrange("p (j n) -> p j n", j=NT)).then_inc(t_ev, 1)

                for k in range(STEPS + LAG + 2):
                    if k % NT == 0 and k // NT < RH:
                        mask(qv, Qv, k // NT, qv_done, bd_ready, 2 * NT)
                    if k >= LAG - 2 and (k - LAG + 2) % NT == 0 and (k - LAG + 2) // NT < RH:
                        mask(qu, Qu, (k - LAG + 2) // NT, qu_done, ac_ready, NT)
                    if 0 <= k - LAG < STEPS:
                        add(k - LAG)
                    if 0 <= k - LAG - 2 < STEPS:
                        evacuate(k - LAG - 2)
                link = Chain(v, link_)
                v.wait_ge(exp_done, NT * RH)
                nc.vector.reciprocal(rs[:], sums[:]).then_inc(rs_done, 1)
                v.wait_ge(rs_ready, 1)
                v.wait_ge(o_ev, 1)
                nc.vector.tensor_tensor(oT[:], oT[:], ps[:, 1, :], ALU.mult).then_inc(on_done, 1)
                v.wait_ge(y_ready, 1)
                for t in range(NT):
                    link.add(nc.vector.tensor_tensor(yb[:, t, :], ps[:, 0, P * t:P * t + P], bo[:], ALU.add))
                link.wait()
                nrm.variance(nc, link, yb, EPS).then_inc(var_, 1)
                v.wait_ge(pow_, 1)
                nrm.apply(nc, link, nrm.out, yb)
                xs = X[:, bass.ds(b * NT, NT), :]
                link.step(nc.vector.tensor_tensor(xs, xs, nrm.out[:], ALU.add))
        clear(nc, names)


GHID = 384
GC = GHID // P
QSCALE = 1.0 / 127.0


def gated_feed_forward(nc, X, ps, c, d):
    with ExitStack() as ctx:
        s = Store(nc, ctx, "g")
        wgu = s.sb("wgu", [P, 2, GHID])
        wd = s.sb("wd", [P, GC, D])
        with ExitStack() as ctx0:
            s0 = Store(nc, ctx0, "g0")
            gui = s0.sb("gui", [P, 2, GHID], I32)
            di = s0.sb("di", [P, GC, D], I32)
            names = w_in, done = s0.sems("w_in", "done")
            with nc.Block() as block:
                @block.sync
                def _(sp):
                    sp.dma_start(gui[:], d["g_wgu"]).then_inc(w_in, 16)
                    sp.dma_start(di[:], d["g_wd"]).then_inc(w_in, 16)

                @block.vector
                def _(v):
                    v.wait_ge(w_in, 32)
                    nc.vector.tensor_scalar(wgu[:], gui[:], QSCALE, None, ALU.mult).then_inc(done, 1)
                    nc.vector.tensor_scalar(wd[:], di[:], QSCALE, None, ALU.mult).then_inc(done, 1)
                    v.wait_ge(done, 2)
            clear(nc, names)
        xT = s.sb("xT", [P, N])
        G = s.sb("G", [P, 2, GHID])
        H = s.sb("H", [P, 2, GHID])
        HT = s.sb("HT", [P, 2, GC, P])
        nrm = Norm(s, "n")
        names = (norm_done, tr, xT_done, up_ready, g_done, h_done, hT_ready, hT_ev, y_ready, link_, var_, pow_) = s.sems(
            *"norm_done tr xT_done up_ready g_done h_done hT_ready hT_ev y_ready link var pow".split())
        with nc.Fori(0, B) as b:
            with nc.Block() as block:
                @block.gpsimd
                def _(pool):
                    for k in range(2):
                        pool.wait_ge(var_, k + 1)
                        nrm.power(nc, c).then_inc(pow_, 1)

                @block.tensor
                def _(pe):
                    pe.wait_ge(norm_done, 1)
                    for t in range(NT):
                        ins = nc.tensor.transpose(ps[:, 0, P * t:P * t + P], nrm.out[:, t, :], c["ident"][:])
                    ins.then_inc(tr, 1)
                    pe.wait_ge(xT_done, 1)
                    for t in range(NT + 1):
                        if t < NT:
                            if t >= 2:
                                pe.wait_ge(h_done, t - 1)
                            for j in range(2):
                                ins = nc.tensor.matmul(ps[:, 1 + 2 * (t % 2) + j, 0:GHID], xT[:, P * t:P * t + P], wgu[:, j, :],
                                                       start=True, stop=True)
                            ins.then_inc(up_ready, 1)
                        if t >= 1:
                            n = t - 1
                            pe.wait_ge(h_done, n + 1)
                            if n >= 2:
                                pe.wait_ge(hT_ev, n - 1)
                            for k in range(GC):
                                ins = nc.tensor.transpose(ps[:, 5 + n % 2, P * k:P * k + P], H[:, n % 2, P * k:P * k + P],
                                                          c["ident"][:])
                            ins.then_inc(hT_ready, 1)
                            pe.wait_ge(hT_ev, n + 1)
                            for k in range(GC):
                                ins = nc.tensor.matmul(ps[:, 7, P * n:P * n + P], HT[:, n % 2, k, :], wd[:, k, :],
                                                       start=(k == 0), stop=(k == GC - 1))
                            ins.then_inc(y_ready, 1)

                @block.scalar
                def _(act):
                    act.wait_ge(tr, 1)
                    nc.scalar.copy(xT[:], ps[:, 0, :]).then_inc(xT_done, 1)
                    for t in range(NT + 1):
                        if t < NT:
                            act.wait_ge(up_ready, t + 1)
                            if t >= 2:
                                act.wait_ge(h_done, t - 1)
                            nc.scalar.activation(G[:, t % 2, :], ps[:, 1 + 2 * (t % 2), 0:GHID], ACT.Silu).then_inc(g_done, 1)
                        if t >= 1:
                            n = t - 1
                            act.wait_ge(hT_ready, n + 1)
                            if n >= 2:
                                act.wait_ge(y_ready, n - 1)
                            nc.scalar.copy(HT[:, n % 2].rearrange("p k n -> p (k n)"), ps[:, 5 + n % 2, 0:GHID]).then_inc(hT_ev, 1)

                @block.vector
                def _(v):
                    link = Chain(v, link_)
                    xs = X[:, bass.ds(b * NT, NT), :]
                    nrm.variance(nc, link, xs, EPS).then_inc(var_, 1)
                    v.wait_ge(pow_, 1)
                    nrm.apply(nc, link, nrm.out, xs)
                    nc.vector.tensor_copy(nrm.st[:, 0, 0:1], nrm.out[:, 0, 0:1]).then_inc(norm_done, 1)
                    for t in range(NT):
                        v.wait_ge(g_done, t + 1)
                        if t >= 2:
                            v.wait_ge(hT_ready, t - 1)
                        nc.vector.tensor_tensor(H[:, t % 2, :], ps[:, 2 + 2 * (t % 2), 0:GHID], G[:, t % 2, :],
                                                ALU.mult).then_inc(h_done, 1)
                    v.wait_ge(y_ready, NT)
                    y = ps[:, 7, :].rearrange("p (t n) -> p t n", n=D)
                    v.wait_ge(norm_done, 1)
                    nrm.variance(nc, link, y, EPS).then_inc(var_, 1)
                    v.wait_ge(pow_, 2)
                    nrm.apply(nc, link, nrm.out, y)
                    link.step(nc.vector.tensor_tensor(xs, xs, nrm.out[:], ALU.add))
            clear(nc, names)


def arrays_of_rest(i):
    emb = i["L1_attn_rel_pos_emb"][MAX_LEN - (N - 1):MAX_LEN - (N - 1) + RW]
    p = np.arange(P)
    return {
        "r_w": np.stack([i["L1_attn_Wq"], i["L1_attn_Wk"], i["L1_attn_Wv"], i["L1_attn_Wr"]], axis=1),
        "r_gb": np.stack([i["L1_attn_gamma"], i["L1_attn_beta"]], axis=1),
        "r_uv": np.stack([i["L1_attn_u_bias"].reshape(P), i["L1_attn_v_bias"].reshape(P)], axis=1),
        "r_emb": emb.T,
        "r_wo": i["L1_attn_Wo"],
        "r_bo": rows(i["L1_attn_bo"]),
        "r_sel": (np.arange(P)[None, :] // RD == np.arange(RH)[:, None]).astype(np.float32),
        "r_hm": ((p[:, None] % 32) // RD == np.arange(RG)[None, :]).astype(np.float32),
        "g_wgu": np.stack([i["L1_ffn_w_gate"].T, i["L1_ffn_w_up"].T], axis=1),
        "g_wd": i["L1_ffn_w_down"].T.reshape(GC, P, D).transpose(1, 0, 2),
    }


def program(nc, d, out):
    with ExitStack() as ctx:
        s = Store(nc, ctx, "m")
        X = s.sb("X", [P, TT, D])
        c = {"ident": s.sb("ident", [P, P]), "identb": s.sb("identb", [P, P], BF16), "trib": s.sb("trib", [P, P], BF16),
             "mhalf": s.sb("mhalf", [P, 16])}
        ps = ctx.enter_context(nc.psum_tensor("ps", [P, 8, 512], F32))
        names = c_in, c_tri, c_done, done = s.sems("c_in", "c_tri", "c_done", "done")
        with ExitStack() as ctx0:
            tri = Store(nc, ctx0, "m0").sb("tri", [P, P])
            with nc.Block() as block:
                @block.sync
                def _(sp):
                    sp.dma_start(c["ident"][:], d["ident"]).then_inc(c_in, 16)
                    sp.dma_start(tri[:], d["tri"]).then_inc(c_tri, 16)

                @block.vector
                def _(v):
                    v.wait_ge(c_in, 16)
                    nc.vector.tensor_copy(c["identb"][:], c["ident"][:]).then_inc(c_done, 1)
                    v.wait_ge(c_tri, 16)
                    nc.vector.tensor_copy(c["trib"][:], tri[:]).then_inc(c_done, 1)
                    nc.vector.memset(c["mhalf"][:], -0.5).then_inc(c_done, 1)
                    v.wait_ge(c_done, 3)
        clear(nc, names)
        with ExitStack() as ctxz:
            Z = Store(nc, ctxz, "z").sb("Z", [P, TT, AH * AR])
            causal_attention(nc, X, Z, ps, c, d)
            output_and_residual(nc, X, Z, ps, c, d)
        local_layers(nc, X, ps, c, d)
        relative_attention(nc, X, ps, c, d)
        gated_feed_forward(nc, X, ps, c, d)

        with nc.Block() as block:
            @block.sync
            def _(sp):
                sp.dma_start(out.rearrange("b (t p) d -> p (b t) d", p=P), X[:]).then_inc(done, 16)
                sp.wait_ge(done, 16)


def kernel(**inputs):
    import concourse.bacc as bacc
    from concourse.bass_utils import run_bass_kernel_spmd

    i = {k: np.asarray(v) for k, v in inputs.items()}
    arrays = {"in_" + k: np.ascontiguousarray(v) for k, v in (arrays_of(i) | arrays_of_layers(i) | arrays_of_rest(i)).items()}
    nc = bacc.Bacc("TRN2", target_bir_lowering=False, num_devices=1)
    d = {k[3:]: nc.dram_tensor(k, v.shape, mybir.dt.from_np(v.dtype), kind="ExternalInput").ap() for k, v in arrays.items()}
    out = nc.dram_tensor("out", (B, N, D), F32, kind="ExternalOutput").ap()
    program(nc, d, out)
    r = run_bass_kernel_spmd(nc, [arrays], core_ids=[0])
    return r.results[0]["out"]
```

```python
from contextlib import ExitStack

import numpy as np

import concourse.bass as bass
from concourse import mybir

ALU = mybir.AluOpType
ACT = mybir.ActivationFunctionType
AX = mybir.AxisListType
F32 = mybir.dt.float32
F32R = mybir.dt.float32r
BF16 = mybir.dt.bfloat16
I32 = mybir.dt.int32

P = 128
B, N, D = 4, 512, 128
NT = N // P
TT = B * NT
EPS = 1e-5
BIG = -1e30

AH, AD, AR, AV = 32, 32, 8, 16
GH = P // AD
AG = AH // GH
KN = N + AV
PITCH = N + AV
NB = 2


class Chain:

    def __init__(self, eng, sem):
        self.eng, self.sem, self.n = eng, sem, 0

    def add(self, ins):
        self.n += 1
        ins.then_inc(self.sem, 1)

    def wait(self):
        self.eng.wait_ge(self.sem, self.n)

    def step(self, ins):
        self.add(ins)
        self.wait()


class Store:

    def __init__(self, nc, ctx, tag):
        self.nc, self.ctx, self.tag = nc, ctx, tag

    def sb(self, name, shape, dt=F32):
        return self.ctx.enter_context(self.nc.sbuf_tensor(f"{self.tag}_{name}", shape, dt))

    def sem(self, name):
        return self.ctx.enter_context(self.nc.semaphore(f"{self.tag}_{name}"))

    def sems(self, *names):
        return [self.sem(n) for n in names]


def clear(nc, sems):
    nums = sorted(s.num for s in sems)
    starts = [n for n in nums if n - 1 not in nums]
    ends = [n + 1 for n in nums if n + 1 not in nums]
    for first, end in zip(starts, ends):
        nc.all_engine_barrier(sems_to_clear=range(first, end))


def causal_attention(nc, X, RS, zd, ps, c, d):
    with ExitStack() as ctx:
        s = Store(nc, ctx, "a")
        xnT = s.sb("xnT", [P, B * N])
        V = s.sb("V", [P, B, NT, AH * AR])
        V0 = s.sb("V0", [P, B, AG, GH * AR])
        W = s.sb("W", [P, 2, 4, P])
        bias = s.sb("bias", [P, 2, 4])
        vk = s.sb("vk", [P, 2, AV])
        with ExitStack() as ctx0:
            s0 = Store(nc, ctx0, "a0")
            xn = s0.sb("xn", [P, 2, D])
            x0 = s0.sb("x0", [P, B, GH, 32])
            st = s0.sb("st", [P, TT, 6])
            mv = s0.sb("mv", [P, TT, 2])
            rstd = s0.sb("rstd", [P, TT])
            wv = s0.sb("wv", [P, AH * AR])
            bv = s0.sb("bv", [P, AH * AR])
            x_in, w_in, stats, stats_done, pow_done, xn_done, xt_done, xt_used, v_ready, v_done, zeroed, vv_in, x0_done = s0.sems(
                "x_in", "w_in", "stats", "stats_done", "pow_done", "xn_done", "xt_done", "xt_used", "v_ready", "v_done", "zeroed", "vv_in", "x0_done")
            with nc.Block() as block:
                @block.sync
                def _(sp):
                    sp.dma_start(X[:], d["x"].rearrange("b (t p) d -> p (b t) d", p=P)).then_inc(x_in, 16)
                    sp.dma_start(wv[:], d["a_wv"]).then_inc(w_in, 16)
                    sp.dma_start(bv[:], d["a_bv"]).then_inc(w_in, 16)
                    sp.dma_start(W[:, 0], d["a_w"][0]).then_inc(w_in, 16)
                    sp.dma_start(bias[:, 0], d["a_b"][0]).then_inc(w_in, 16)
                    sp.dma_start(vk[:, 0], d["a_vk"][0]).then_inc(w_in, 16)
                    for b in range(B):
                        sp.dma_start(V[P - AV:P, b, NT - 1, :], d["a_vv"]).then_inc(vv_in, 16)
                    sp.wait_ge(w_in, 80)
                    sp.wait_ge(vv_in, 16 * B)

                @block.gpsimd
                def _(pool):
                    nc.gpsimd.memset(V0[:], 0.0).then_inc(zeroed, 1)
                    nc.gpsimd.memset(x0[:], 0.0).then_inc(zeroed, 1)
                    pool.wait_ge(stats_done, 1)
                    nc.gpsimd.tensor_tensor(rstd[:], mv[:, :, 1], c["mhalf"][:, 0:TT], ALU.pow).then_inc(pow_done, 1)

                @block.vector
                def _(v):
                    link = Chain(v, stats)
                    v.wait_ge(x_in, 16)
                    for t in range(TT):
                        nc.vector.bn_stats(st[:, t, :], X[:, t, :]).then_inc(stats, 1)
                    link.n = TT
                    v.wait_ge(stats, TT)
                    for t in range(TT):
                        nc.vector.bn_aggr(mv[:, t, :], st[:, t, :]).then_inc(stats, 1)
                    link.n = 2 * TT
                    v.wait_ge(stats, 2 * TT)
                    nc.vector.tensor_scalar(mv[:, :, 1], mv[:, :, 1], EPS, None, ALU.add).then_inc(stats_done, 1)
                    v.wait_ge(pow_done, 1)
                    for t in range(TT):
                        if t >= 2:
                            v.wait_ge(xt_done, t - 1)
                        nc.vector.tensor_scalar(xn[:, t % 2, :], X[:, t, :], mv[:, t, 0:1], rstd[:, t:t + 1],
                                                ALU.subtract, ALU.mult).then_inc(xn_done, 1)
                    v.wait_ge(w_in, 80)
                    v.wait_ge(zeroed, 2)
                    for n in range(TT + B):
                        v.wait_ge(v_ready, n + 1)
                        if n < TT:
                            r = P - AV if n % NT == NT - 1 else P
                            nc.vector.tensor_tensor(V[0:r, n // NT, n % NT, :], ps[0:r, 4 + n % 2, 0:AH * AR], bv[0:r],
                                                    ALU.add).then_inc(v_done, 1)
                        else:
                            for h in range(GH):
                                r = slice(32 * h, 32 * h + 32)
                                own = slice(AR * h, AR * h + AR)
                                nc.vector.tensor_tensor(
                                    V0[r, n - TT, :, own],
                                    ps[r, 4 + n % 2, 0:AH * AR].rearrange("p (g c) -> p g c", g=AG)[:, :, own],
                                    bv[r].rearrange("p (g c) -> p g c", g=AG)[:, :, own], ALU.add).then_inc(v_done, 1)

                @block.tensor
                def _(pe):
                    for t in range(TT):
                        pe.wait_ge(xn_done, t + 1)
                        if t >= 4:
                            pe.wait_ge(xt_used, t - 3)
                        nc.tensor.transpose(ps[:, t % 4, 0:P], xn[:, t % 2, :], c["ident"][:]).then_inc(xt_done, 1)
                    pe.wait_ge(xt_used, TT)
                    pe.wait_ge(x0_done, B)
                    pe.wait_ge(w_in, 80)
                    for n in range(TT + B):
                        if n >= 2:
                            pe.wait_ge(v_done, n - 1 if n - 2 < TT else TT + GH * (n - 1 - TT))
                        if n < TT:
                            r = P - AV if n % NT == NT - 1 else P
                            nc.tensor.matmul(ps[0:r, 4 + n % 2, 0:AH * AR], xnT[:, P * n + AV:P * n + AV + r], wv[:],
                                             start=True, stop=True).then_inc(v_ready, 1)
                        else:
                            lhs = x0[:, n - TT].rearrange("p h k -> p (h k)")
                            nc.tensor.matmul(ps[:, 4 + n % 2, 0:AH * AR], lhs, wv[:],
                                             start=True, stop=True).then_inc(v_ready, 1)

                @block.scalar
                def _(act):
                    act.wait_ge(zeroed, 2)
                    for t in range(TT):
                        act.wait_ge(xt_done, t + 1)
                        if t % NT == 0:
                            first = ps[:, t % 4, 0:AV].rearrange("p (o k) -> p o k", o=1).to_broadcast([P, GH, AV])
                            nc.scalar.copy(x0[:, t // NT, :, 0:AV], first).then_inc(x0_done, 1)
                        nc.scalar.copy(xnT[:, P * t:P * t + P], ps[:, t % 4, 0:P]).then_inc(xt_used, 1)
        clear(nc, [x_in, w_in, stats, stats_done, pow_done, xn_done, xt_done, xt_used, v_ready, v_done, zeroed, vv_in, x0_done])
        attention_groups(nc, s, RS, zd, ps, c, d, xnT, V, V0, W, bias, vk)


def attention_groups(nc, s, RS, zd, ps, c, d, xnT, V, V0, W, bias, vk):
    Qst = [s.sb(f"Qst{i}", [P, GH, NB, N], F32R) for i in range(2)]
    Kst = [s.sb(f"Kst{i}", [P, GH, NB, KN], F32R) for i in range(2)]
    qh = s.sb("qh", [P, NB, N], F32R)
    ql = s.sb("ql", [P, NB, N], F32R)
    kh = s.sb("kh", [P, NB, KN], F32R)
    kl = s.sb("kl", [P, NB, KN], F32R)
    rot = s.sb("rot", [P, 4, N])
    full = s.sb("full", [P, 2, N])
    Pm = s.sb("Pm", [P, 2, NT, PITCH])
    PT = s.sb("PT", [P, 2, 10, P])
    P0 = s.sb("P0", [P, 2, NT, GH * 32])
    P0T = s.sb("P0T", [P, N])
    Vm = s.sb("Vm", [P, 2, NT, GH * 40])
    V0m = s.sb("V0m", [P, 2, GH * AR])
    zs = s.sb("zs", [P, N])
    tab = s.sb("tab", [P, 4, N])
    nm = s.sb("nm", [P, 2, NT])
    sums = s.sb("sums", [P, NB, NT, GH])
    names = (w_in, pj_ready, stt_done, added, hi_done, lo_done, s_ready, nm_ready, exp_done, t_done, evd, eva, pv_done, o_rs,
             tab_in, pad_done, p0_done, p0_tr, p0_ev, vm_done, z_ready, z_ev, z_out, bounced) = s.sems(
        *("w_in pj_ready stt_done added hi_done lo_done s_ready nm_ready exp_done t_done evd eva pv_done o_rs "
          "tab_in pad_done p0_done p0_tr p0_ev vm_done z_ready z_ev z_out bounced").split())
    bounce = [[nc.dram_tensor(f"bounce{k}{m}", (2, P, KN), F32, kind="Internal").ap() for m in range(4)] for k in range(2)]
    stk = [s.sems(f"stk{k}0", f"stk{k}1") for k in range(2)]
    STK = 16 * 2 * 4
    PJ, O, SA, SC, TB = 0, 1, 2, 4, 5
    S_of = {3: 0, 2: 528, 1: 1024, 0: 1296}
    S = ps[:, SA:SC + 1, :].rearrange("p a n -> p (a n)")
    width = lambda qt: P * (qt + 1) + AV
    TBANK = [[(qt, 0) for qt in range(NT)], [(qt, 1) for qt in range(1, NT)], [(2, 2), (3, 2), (3, 3)]]
    AT = (0, 4, 7)
    KEYS = ((0, 4), (4, 7), (7, 9), (9, 10))

    def project(pe, s_, n, b):
        k = 8 * s_ + n
        if k >= 1:
            pe.wait_ge(stt_done, k)
        if s_ == 1 and n == 0:
            pe.wait_ge(w_in, 48)
        nc.tensor.matmul(ps[:, PJ, :], W[:, s_, n % 4, :], xnT[:, b * N:(b + 1) * N], start=True, stop=True)\
            .then_inc(pj_ready, 1)

    def rotate_half(v, s_, n):
        k = 8 * s_ + n
        v.wait_ge(pj_ready, k + 1)
        if k >= 4:
            v.wait_ge(added, (k - 4) // 2 + 1)
        nc.vector.scalar_tensor_tensor(rot[:, n % 4, :], ps[:, PJ, :], bias[:, s_, n % 4:n % 4 + 1], tab[:, n % 4, :],
                                       ALU.add, ALU.mult).then_inc(stt_done, 1)

    def add_pair(pool, s_, m):
        k = 4 * s_ + m
        pool.wait_ge(stt_done, 2 * k + 2)
        if k >= 2:
            pool.wait_ge(lo_done, k - 1)
        nc.gpsimd.tensor_tensor(full[:, m % 2, :], rot[:, 2 * (m % 2), :], rot[:, 2 * (m % 2) + 1, :],
                                ALU.add).then_inc(added, 1)

    def split_lo(pool, s_, m):
        k = 4 * s_ + m
        pool.wait_ge(hi_done, k + 1)
        hi, lo = ((qh, ql), (kh, kl))[m % 2]
        ins = nc.gpsimd.tensor_tensor(lo[:, m // 2, 0:N], full[:, m % 2, :], hi[:, m // 2, 0:N].bitcast(F32), ALU.subtract)
        if m % 2:
            ins = nc.gpsimd.tensor_tensor(kl[:, m // 2, N:KN], vk[:, s_, :], kh[:, m // 2, N:KN].bitcast(F32), ALU.subtract)
        ins.then_inc(lo_done, 1)

    def split_hi(act, s_, m, n=None):
        k = 4 * s_ + m
        act.wait_ge(added, k + 1)
        if n is not None:
            act.wait_ge(stk[s_][m // 2], n)
        hi = (qh, kh)[m % 2]
        if m % 2:
            if s_ == 1:
                act.wait_ge(w_in, 48)
            nc.scalar.copy(kh[:, m // 2, N:KN], vk[:, s_, :])
        nc.scalar.copy(hi[:, m // 2, 0:N], full[:, m % 2, :]).then_inc(hi_done, 1)

    def stack(sp, s_, m, buf):
        i, k = m // 2, 4 * s_ + m
        width_ = (N, KN)[m % 2]
        dst, halves = ((Qst, (qh, ql)), (Kst, (kh, kl)))[m % 2]
        for j, (src, made) in enumerate(zip(halves, (hi_done, lo_done))):
            sp.wait_ge(made, k + 1)
            sp.dma_start(bounce[s_][m][j, :, 0:width_], src[:, i].bitcast(F32)).then_inc(bounced, 16)
        sp.wait_ge(bounced, 32 * (k + 1))
        for block, j in enumerate(((0, 1, 0, 1), (0, 0, 1, 1))[m % 2]):
            sp.dma_start(dst[buf][32 * block:32 * block + 32, :, i].bitcast(F32),
                         bounce[s_][m][j, :, 0:width_].rearrange("(h c) n -> c h n", h=GH)).then_inc(stk[buf][i], 16)

    with nc.Block() as block:
        @block.sync
        def _(sp):
            sp.dma_start(tab[:], d["a_tab"]).then_inc(tab_in, 16)
            for m in range(4):
                stack(sp, 0, m, 0)

        @block.tensor
        def _(pe):
            for n in range(8):
                project(pe, 0, n, n // 4)

        @block.vector
        def _(v):
            v.wait_ge(tab_in, 16)
            for n in range(8):
                rotate_half(v, 0, n)

        @block.gpsimd
        def _(pool):
            for pad in (P0, Vm):
                nc.gpsimd.memset(pad[:], 0.0).then_inc(pad_done, 1)
            for m in range(4):
                add_pair(pool, 0, m)
                split_lo(pool, 0, m)
            pool.wait_ge(pad_done, 2)

        @block.scalar
        def _(act):
            for m in range(4):
                split_hi(act, 0, m)
    clear(nc, names)

    U = NB * GH
    with nc.Fori(0, AG) as g:
        with nc.Block() as block:
            @block.sync
            def _(sp):
                def store(b):
                    sp.wait_ge(z_ev, b + 1)
                    sp.dma_start(zd[b, bass.ds(g * 32, 32), :], zs[32 * b:32 * b + 32, :]).then_inc(z_out, 16)

                def weights(k):
                    sp.dma_start(W[:, k], d["a_w"][bass.ds(g + 1, 1)].rearrange("g p c n -> p (g c) n")).then_inc(w_in, 16)
                    sp.dma_start(bias[:, k], d["a_b"][bass.ds(g + 1, 1)].rearrange("g p c -> p (g c)")).then_inc(w_in, 16)
                    sp.dma_start(vk[:, k], d["a_vk"][bass.ds(g + 1, 1)].rearrange("g p c -> p (g c)")).then_inc(w_in, 16)

                weights(1)
                sp.wait_ge(w_in, 48)
                for m in range(4):
                    stack(sp, 0, m, 1)
                    if m == 2:
                        store(0)
                sp.wait_ge(stt_done, 8)
                weights(0)
                for m in range(4):
                    sp.wait_ge(s_ready, 2 * GH * (m // 2 + 1))
                    stack(sp, 1, m, 0)
                    if m % 2 == 0:
                        store(1 + m // 2)
                store(3)
                sp.wait_ge(z_out, 16 * B)
                sp.wait_ge(w_in, 96)

            @block.gpsimd
            def _(pool):
                def first_keys(u):
                    bb, h = u // GH, u % GH
                    pool.wait_ge(exp_done, 4 * u + 4)
                    if h == 0 and bb >= 2:
                        pool.wait_ge(p0_tr, bb - 1)
                    nc.gpsimd.tensor_copy(P0[:, bb % 2, :, 32 * h:32 * h + AV], Pm[:, u % 2, :, 0:AV]).then_inc(p0_done, 1)

                for k in range(2 * U):
                    if k % 2 == 1:
                        add_pair(pool, k // U, k % U // 2)
                    first_keys(k)
                    if k % 2 == 1:
                        split_lo(pool, k // U, k % U // 2)

            @block.tensor
            def _(pe):
                def scores(u, part):
                    q, k = Qst[u // U], Kst[u // U]
                    i, h = u % U // GH, u % GH
                    if h == 0 and part == 0:
                        pe.wait_ge(stk[u // U][i], g * STK + STK)
                    if part == 0:
                        if u >= 1:
                            pe.wait_ge(exp_done, 4 * u - 2)
                        todo = [(1, [(0, 272)]), (0, [(0, 144)])]
                        last = 0
                    else:
                        if u >= 1:
                            pe.wait_ge(exp_done, 4 * u)
                        todo = [(3, [(0, 512), (512, 16)]), (2, [(0, 400)])]
                        last = 2
                    opened = set()
                    for qt, pieces in todo:
                        for at, w in pieces:
                            lo = S_of[qt] + at
                            nc.tensor.matmul(S[:, lo:lo + w], q[:, h, i, P * qt:P * qt + P], k[:, h, i, at:at + w],
                                             start=lo // 512 not in opened, stop=False)
                            opened.add(lo // 512)
                        edge = width(qt) - P
                        cuts = [(0, P)] if qt != 3 else [(0, 512 - edge), (512 - edge, P)]
                        for a, z in cuts:
                            lo = S_of[qt] + edge + a
                            end = (part == 0 and qt == 0) or (part == 1 and (qt == 2 or a == 0))
                            ins = nc.tensor.matmul(S[:, lo:lo + z - a], c["identb"][:], c["trib"][:, a:z],
                                                   start=False, stop=end)
                    ins.then_inc(s_ready, 1)

                def transposes(u):
                    pe.wait_ge(exp_done, 4 * u + 4)
                    for k in range(3):
                        if u >= 1:
                            if k != 1:
                                pe.wait_ge(eva, 2 * u - 1 + k // 2)
                            else:
                                pe.wait_ge(evd, u)
                        if k == 0 and u >= GH and u % GH == 0:
                            pe.wait_ge(p0_ev, u // GH)
                        for j, (qt, kt) in enumerate(TBANK[k]):
                            at = AV + P * kt
                            ins = nc.tensor.transpose(ps[:, TB + k, P * j:P * j + P], Pm[:, u % 2, qt, at:at + P],
                                                      c["ident"][:])
                        ins.then_inc(t_done, 1)

                def first_transposes(bb):
                    pe.wait_ge(p0_done, GH * (bb + 1))
                    pe.wait_ge(eva, 2 * GH * (bb + 1) - 1)
                    for qt in range(NT):
                        ins = nc.tensor.transpose(ps[:, TB, P * qt:P * qt + P], P0[:, bb % 2, qt, :], c["ident"][:])
                    ins.then_inc(p0_tr, 1)

                def values(u):
                    bb, h = u // GH, u % GH
                    out = ps[32 * bb:32 * bb + 32, O, :]
                    pe.wait_ge(eva, 2 * u + 2)
                    pe.wait_ge(evd, u + 1)
                    if h == 0:
                        pe.wait_ge(vm_done, 2 * bb + 2)
                    for kt in range(NT):
                        a, z = KEYS[kt]
                        ins = nc.tensor.matmul(out[:, P * kt:N], Vm[:, bb % 2, kt, 32 * h:32 * h + 32],
                                               PT[:, u % 2, a:z, :].rearrange("p j n -> p (j n)"),
                                               start=(h == 0 and kt == 0), stop=False)
                    ins.then_inc(pv_done, 1)
                    if h == GH - 1:
                        pe.wait_ge(p0_ev, bb + 1)
                        nc.tensor.matmul(out, V0m[:, bb % 2, :], P0T[:], start=False, stop=True).then_inc(z_ready, 1)

                for k in range(2 * U + 2):
                    if k < 2 * U:
                        scores(k, 0)
                        step, n = k // U, k % U
                        project(pe, step, n, (NB * (1 - step)) + n // 4)
                        scores(k, 1)
                    if 1 <= k <= 2 * U:
                        transposes(k - 1)
                        if k % GH == 0:
                            first_transposes(k // GH - 1)
                    if k >= 2:
                        values(k - 2)

            @block.vector
            def _(v):
                def maxima(u):
                    for part, tiles in ((0, (1, 0)), (1, (3, 2))):
                        v.wait_ge(s_ready, 2 * u + part + 1)
                        for qt in tiles:
                            nc.vector.tensor_reduce(nm[:, u % 2, qt:qt + 1], S[:, S_of[qt]:S_of[qt] + width(qt)],
                                                    AX.X, ALU.max, negate=True).then_inc(nm_ready, 1)

                def evacuate(u):
                    v.wait_ge(t_done, 3 * u + 2)
                    if u >= 2:
                        v.wait_ge(pv_done, u - 1)
                    nc.vector.tensor_copy(PT[:, u % 2, 4:7, :].rearrange("p j n -> p (j n)"), ps[:, TB + 1, 0:3 * P])\
                        .then_inc(evd, 1)

                def first_evacuate(bb):
                    v.wait_ge(p0_tr, bb + 1)
                    if bb >= 1:
                        v.wait_ge(z_ready, bb)
                    nc.vector.tensor_copy(P0T[:], ps[:, TB, :]).then_inc(p0_ev, 1)

                def group_values(bb):
                    if bb >= 2:
                        v.wait_ge(z_ready, bb - 1)
                    nc.vector.tensor_copy(
                        Vm[:, bb % 2].rearrange("p t (h x) -> p t h x", h=GH)[:, :, :, 0:AR],
                        V[:, bb, :, bass.ds(g * GH * AR, GH * AR)].rearrange("p t (h r) -> p t h r", h=GH)).then_inc(vm_done, 1)
                    nc.vector.tensor_copy(V0m[:, bb % 2, :], V0[:, bb, bass.ds(g, 1), :].rearrange("p g c -> p (g c)"))\
                        .then_inc(vm_done, 1)

                def reciprocals(bb):
                    v.wait_ge(exp_done, 4 * GH * (bb + 1))
                    nc.vector.reciprocal(RS[:, NT * bb:NT * bb + NT, bass.ds(g * GH, GH)], sums[:, bb % NB]).then_inc(o_rs, 1)

                def outputs(bb):
                    v.wait_ge(z_ready, bb + 1)
                    nc.vector.tensor_copy(zs[32 * bb:32 * bb + 32, :], ps[32 * bb:32 * bb + 32, O, :]).then_inc(z_ev, 1)

                for k in range(2 * U + 3):
                    if k < 2 * U:
                        maxima(k)
                        rotate_half(v, k // U, k % U)
                        if k % GH == 0:
                            group_values(k // GH)
                    if 1 <= k <= 2 * U:
                        evacuate(k - 1)
                        if k % GH == 0:
                            reciprocals(k // GH - 1)
                            first_evacuate(k // GH - 1)
                    if k >= GH + 2 and (k - 2) % GH == 0:
                        outputs(k // GH - 1)

            @block.scalar
            def _(act):
                def exps(u):
                    i, h = u % U // GH, u % GH
                    if u >= 2:
                        act.wait_ge(t_done, 3 * (u - 1))
                        act.wait_ge(p0_done, u - 1)
                    if u >= U and h == 0:
                        act.wait_ge(o_rs, i + 1)
                    for part, tiles in ((0, (1, 0)), (1, (3, 2))):
                        act.wait_ge(nm_ready, 4 * u + 2 * part + 2)
                        for qt in tiles:
                            nc.scalar.activation(Pm[:, u % 2, qt, 0:width(qt)], S[:, S_of[qt]:S_of[qt] + width(qt)],
                                                 ACT.Exp, bias=nm[:, u % 2, qt:qt + 1],
                                                 accum_out=sums[:, i, qt, h:h + 1]).then_inc(exp_done, 1)

                def evacuate(u):
                    if u >= 2:
                        act.wait_ge(pv_done, u - 1)
                    for k, a, z in ((0, 0, 4), (2, 7, 10)):
                        act.wait_ge(t_done, 3 * u + k + 1)
                        nc.scalar.copy(PT[:, u % 2, a:z, :].rearrange("p j n -> p (j n)"), ps[:, TB + k, 0:P * (z - a)])\
                            .then_inc(eva, 1)

                for k in range(2 * U + 1):
                    if k < 2 * U:
                        exps(k)
                    if k >= 1:
                        evacuate(k - 1)
                    if k % 2 == 1 and k < 2 * U:
                        split_hi(act, k // U, k % U // 2, g * STK + STK)
        clear(nc, names)
    with nc.Block() as block:
        @block.sync
        def _(sp):
            for i in range(NB):
                sp.wait_ge(stk[0][i], STK * (AG + 1))
    clear(nc, [*names, *stk[0], *stk[1]])


def rope_tables():
    freq = (np.float32(10000.0) ** (np.arange(AD // 2, dtype=np.float32) / np.float32(AD / 2))).astype(np.float32)
    freq = np.concatenate([freq, freq])
    ang = (np.arange(N, dtype=np.float32)[:, None] / freq[None, :]).astype(np.float32)
    sign = np.where(np.arange(AD) < AD // 2, -1.0, 1.0)
    cos, sin = np.cos(ang).T, np.sin(ang).T * sign[:, None]
    q = AD ** -0.5
    t = np.stack([cos * q, sin * q, cos, sin], axis=1)
    return np.tile(t, (GH, 1, 1)).astype(np.float32)


def by_group(w):
    w = w.reshape(AG, GH, w.shape[1], w.shape[2]).transpose(0, 2, 1, 3)
    w = w.reshape(AG, w.shape[1], -1)
    return np.concatenate([w, w[:1]])


def swap(w):
    return np.roll(w, w.shape[-1] // 2, axis=-1)


def arrays_of(i):
    a = {"x": i["L0_attn_resid"]}
    wq, wk, bq, bk = i["L0_attn_W_Q"], i["L0_attn_W_K"], i["L0_attn_b_Q"], i["L0_attn_b_K"]
    a["a_w"] = np.stack([by_group(w) for w in (wq, swap(wq), wk, swap(wk))], axis=2)
    a["a_b"] = np.stack([by_group(b[:, None, :])[:, 0] for b in (bq, swap(bq), bk, swap(bk))], axis=2)
    a["a_vk"] = by_group(i["L0_attn_virtual_k"].transpose(1, 0, 2)).reshape(AG + 1, AV, P).transpose(0, 2, 1)
    a["a_vv"] = i["L0_attn_virtual_v"].reshape(AV, AH * AR)
    a["a_wv"] = i["L0_attn_W_V"].reshape(AH * AR, D).T
    a["a_bv"] = np.broadcast_to(i["L0_attn_b_V"].reshape(1, AH * AR), (P, AH * AR))
    a["a_wo"] = i["L0_attn_W_O"].reshape(2, P, D).transpose(1, 0, 2)
    a["a_sel"] = np.repeat(np.eye(AH, dtype=np.float32), AR, axis=1).reshape(AH, 2, P)
    a["a_tab"] = rope_tables()
    a["ident"] = np.eye(P, dtype=np.float32)
    kk = np.arange(P)
    a["tri"] = np.where(kk[None, :] > kk[:, None], BIG, 0.0).astype(np.float32)
    return a


def output_and_residual(nc, X, RS, zd, ps, c, d):
    with ExitStack() as ctx:
        s = Store(nc, ctx, "o")
        wo = s.sb("wo", [P, 2, D])
        sel = s.sb("sel", [AH, 2, P])
        z = s.sb("z", [P, B, 2, N])
        rsT = s.sb("rsT", [AH, 2, N])
        nrm = Norm(s, "on")
        names = w_in, z_in, r_tr, r_ev, r_ready, z_done, y_done, link_, pow_, var_ = s.sems(
            *"w_in z_in r_tr r_ev r_ready z_done y_done link pow var".split())
        with nc.Block() as block:
            @block.sync
            def _(sp):
                for b in range(B):
                    sp.dma_start(z[:, b], zd[b].rearrange("(j p) n -> p j n", p=P)).then_inc(z_in, 16)
                sp.dma_start(wo[:], d["a_wo"]).then_inc(w_in, 16)
                sp.dma_start(sel[:], d["a_sel"]).then_inc(w_in, 16)
                sp.wait_ge(w_in, 32)

            @block.tensor
            def _(pe):
                def spread(b):
                    if b >= 1:
                        pe.wait_ge(r_ev, b)
                    for t in range(NT):
                        ins = nc.tensor.transpose(ps[0:AH, 0, P * t:P * t + P], RS[:, NT * b + t, :], c["ident"][:])
                    ins.then_inc(r_tr, 1)
                    pe.wait_ge(r_ev, b + 1)
                    for j in range(2):
                        if b >= 1:
                            pe.wait_ge(z_done, 2 * b - 1 + j)
                        nc.tensor.matmul(ps[:, 1 + j, :], sel[:, j, :], rsT[:, b % 2, :], start=True, stop=True)\
                            .then_inc(r_ready, 1)

                pe.wait_ge(w_in, 32)
                spread(0)
                for b in range(B):
                    if b + 1 < B:
                        spread(b + 1)
                    pe.wait_ge(z_done, 2 * b + 2)
                    if b >= 2:
                        pe.wait_ge(var_, 2 * (b - 2) + 2)
                    for t in range(NT):
                        for j in range(2):
                            ins = nc.tensor.matmul(ps[:, 3 + b % 2, P * t:P * t + P], z[:, b, j, P * t:P * t + P], wo[:, j, :],
                                                   start=(j == 0), stop=(j == 1))
                    ins.then_inc(y_done, 1)

            @block.scalar
            def _(act):
                for b in range(B):
                    act.wait_ge(r_tr, b + 1)
                    if b >= 2:
                        act.wait_ge(r_ready, 2 * (b - 1))
                    nc.scalar.copy(rsT[:, b % 2, :], ps[0:AH, 0, :]).then_inc(r_ev, 1)

            @block.gpsimd
            def _(pool):
                for b in range(B):
                    pool.wait_ge(var_, 2 * b + 1)
                    nrm.power(nc, c).then_inc(pow_, 1)

            @block.vector
            def _(v):
                link = Chain(v, link_)
                v.wait_ge(z_in, 16 * B)

                def scale(b):
                    for j in range(2):
                        v.wait_ge(r_ready, 2 * b + j + 1)
                        nc.vector.tensor_tensor(z[:, b, j, :], z[:, b, j, :], ps[:, 1 + j, :], ALU.mult).then_inc(z_done, 1)

                scale(0)
                for b in range(B):
                    if b + 1 < B:
                        scale(b + 1)
                    v.wait_ge(y_done, b + 1)
                    y = ps[:, 3 + b % 2, :].rearrange("p (t n) -> p t n", n=D)
                    nrm.variance(nc, link, y, EPS).then_inc(var_, 1)
                    v.wait_ge(pow_, b + 1)
                    nrm.apply(nc, link, nrm.out, y)
                    nc.vector.tensor_tensor(X[:, NT * b:NT * b + NT, :], X[:, NT * b:NT * b + NT, :], nrm.out[:],
                                            ALU.add).then_inc(var_, 1)
                    v.wait_ge(var_, 2 * b + 2)
        clear(nc, names)


class Norm:

    def __init__(self, s, name):
        self.st = s.sb(name + "_st", [P, NT, 6])
        self.mv = s.sb(name + "_mv", [P, NT, 2])
        self.rstd = s.sb(name + "_rstd", [P, NT])
        self.out = s.sb(name + "_out", [P, NT, D])

    def variance(self, nc, link, x, eps):
        for t in range(NT):
            link.add(nc.vector.bn_stats(self.st[:, t, :], x[:, t, :]))
        link.wait()
        for t in range(NT):
            link.add(nc.vector.bn_aggr(self.mv[:, t, :], self.st[:, t, :]))
        link.wait()
        return nc.vector.tensor_scalar(self.mv[:, :, 1], self.mv[:, :, 1], eps, None, ALU.add)

    def power(self, nc, c):
        return nc.gpsimd.tensor_tensor(self.rstd[:], self.mv[:, :, 1], c["mhalf"][:, 0:NT], ALU.pow)

    def apply(self, nc, link, out, x):
        for t in range(NT):
            link.add(nc.vector.tensor_scalar(out[:, t, :], x[:, t, :], self.mv[:, t, 0:1], self.rstd[:, t:t + 1],
                                             ALU.subtract, ALU.mult))
        link.wait()


FL, FH, FD = 2, 8, 64
FI = FH * FD
FW = 64
HID = int(D * 4 * 2 / 3)
HC = [(0, P), (P, 2 * P), (2 * P, HID)]


def local_layers(nc, X, ps, c, d):
    with ExitStack() as ctx:
        s = Store(nc, ctx, "f")
        wqkv = s.sb("wqkv", [P, FL, 3 * FI])
        wo = s.sb("wo", [P, FL, 4, D])
        w1 = s.sb("w1", [P, FL, 2 * HID])
        w2 = s.sb("w2", [P, FL, 3, D])
        b1 = s.sb("b1", [P, FL, 2 * HID])
        b2 = s.sb("b2", [P, FL, D])
        lgb = s.sb("lgb", [P, FL, 2])
        tab = s.sb("tab", [P, FL, 2, 2, NT, FD])
        band = s.sb("band", [P, 2, 2 * P])
        hs = s.sb("hs", [P, NT, D])
        kz = s.sb("kz", [P, FH, N + P])
        with ExitStack() as ctx0:
            s0 = Store(nc, ctx0, "f0")
            base = s0.sb("base", [P, 2, 2, NT, FD])
            sc = s0.sb("sc", [P, FL, 2, 2, FD])
            names = w_in, sc_in, done = s0.sems("w_in", "sc_in", "done")
            with nc.Block() as block:
                @block.sync
                def _(sp):
                    for dst, src in ((base, "f_base"), (sc, "f_sc")):
                        sp.dma_start(dst[:], d[src]).then_inc(sc_in, 16)
                    for dst, src in ((wqkv, "f_wqkv"), (wo, "f_wo"), (w1, "f_w1"), (b1, "f_b1"), (b2, "f_b2"),
                                     (lgb, "f_lgb"), (band, "f_band")):
                        sp.dma_start(dst[:], d[src]).then_inc(w_in, 16)
                    for k, (a, z) in enumerate(HC):
                        sp.dma_start(w2[0:z - a, :, k, :], d["f_w2"][a:z]).then_inc(w_in, 16)
                    sp.wait_ge(w_in, 160)

                @block.gpsimd
                def _(pool):
                    nc.gpsimd.memset(kz[:], 0.0).then_inc(done, 1)
                    nc.gpsimd.memset(hs[:], 0.0).then_inc(done, 1)

                @block.vector
                def _(v):
                    v.wait_ge(sc_in, 32)
                    for l in range(FL):
                        for cs in range(2):
                            for t in range(NT):
                                nc.vector.tensor_tensor(tab[:, l, cs, :, t, :], base[:, cs, :, t, :], sc[:, l, cs, :, :],
                                                        ALU.mult).then_inc(done, 1)
                    v.wait_ge(done, 2 + FL * 2 * NT)
            clear(nc, names)
        xb = s.sb("xb", [P, NT, D])
        hT = s.sb("hT", [P, N])
        QK = s.sb("QK", [P, 2, 2 * FI])
        R1 = s.sb("R1", [P, 2, 2 * FI])
        R2 = s.sb("R2", [P, 2 * FI])
        ss = s.sb("ss", [P, 2, 2 * FH])
        rr = s.sb("rr", [P, 2, 2 * FH])
        Vb = s.sb("Vb", [P, NT, FI])
        qT = s.sb("qT", [P, 4, N])
        Sm = s.sb("Sm", [P, 2, 2, 2 * P])
        nb = s.sb("nb", [P, 2, 2])
        Pe = s.sb("Pe", [P, 2, 2, 2 * P])
        PT = s.sb("PT", [P, 2, 4, P])
        sums = s.sb("sums", [P, NT, FH])
        rs = s.sb("rs", [P, NT, FH])
        on = s.sb("on", [P, 2, FI])
        oT = s.sb("oT", [P, 2, 4, P])
        UG = s.sb("UG", [P, 2, HID])
        UA = s.sb("UA", [P, 2, HID])
        G = s.sb("G", [P, 2, HID])
        HT = s.sb("HT", [P, 2, 3, P])
        yb = s.sb("yb", [P, 2, D])
        nrm = Norm(s, "fn")
        names = (xb_ready, sh_copy, sh_dma, tr, hT_done, hn_done, qkv_ready, qk_ev, v_ev, sq_done, ss_done, rr_done,
                 rot_done, qkT_ready, qT_ev, kT_ev, s_ready, sm_done, exp_done, pt_ready, pt_ev, pv_done, on_done,
                 oT_ready, oT_ev, y_ready, y_used, up_ready, ug_done, gelu_done, ua_done, h_done, hT2_ready, hT2_ev,
                 y2_ready, y2_used, link_, var_, pow_) = s.sems(
            *("xb_ready sh_copy sh_dma tr hT_done hn_done qkv_ready qk_ev v_ev sq_done ss_done rr_done rot_done "
              "qkT_ready qT_ev kT_ev s_ready sm_done exp_done pt_ready pt_ev pv_done on_done oT_ready oT_ev y_ready "
              "y_used up_ready ug_done gelu_done ua_done h_done hT2_ready hT2_ev y2_ready y2_used link var pow").split())
        HP = FH // 2
        UL = NT * HP
        qkv_bank = lambda T: 1 + 3 * (T % 2)
        with nc.Fori(0, B) as b:
            with nc.Block() as block:
                @block.sync
                def _(sp):
                    for j in range(2 * FL):
                        sp.wait_ge(xb_ready, j + 1)
                        sp.dma_start(hs[1:P, :, FW:D], xb[0:P - 1, :, FW:D]).then_inc(sh_dma, 16)
                        sp.dma_start(hs[0:1, 1:NT, FW:D], xb[P - 1:P, 0:NT - 1, FW:D]).then_inc(sh_dma, 16)
                    sp.wait_ge(sh_dma, 32 * 2 * FL)

                @block.gpsimd
                def _(pool):
                    def shift(j):
                        pool.wait_ge(xb_ready, j + 1)
                        nc.gpsimd.tensor_copy(hs[:, :, 0:FW], xb[:, :, 0:FW]).then_inc(sh_copy, 1)

                    pool.wait_ge(var_, 1)
                    nrm.power(nc, c).then_inc(pow_, 1)
                    for l in range(FL):
                        shift(2 * l)
                        for t in range(NT):
                            T = NT * l + t
                            pool.wait_ge(ss_done, T + 1)
                            if T >= 2:
                                pool.wait_ge(rot_done, T - 1)
                            nc.gpsimd.tensor_tensor(rr[:, T % 2, :], ss[:, T % 2, :], c["mhalf"][:, 0:2 * FH],
                                                    ALU.pow).then_inc(rr_done, 1)
                        shift(2 * l + 1)
                        pool.wait_ge(var_, 2 + l)
                        nrm.power(nc, c).then_inc(pow_, 1)
                    pool.wait_ge(var_, 2 + FL)
                    nrm.power(nc, c).then_inc(pow_, 1)

                @block.scalar
                def _(act):
                    for l in range(FL):
                        act.wait_ge(tr, 2 * l + 1)
                        nc.scalar.copy(hT[:], ps[:, 0, :]).then_inc(hT_done, 1)
                        for t in range(NT + 1):
                            if t < NT:
                                T = NT * l + t
                                act.wait_ge(qkv_ready, T + 1)
                                if T >= 2:
                                    act.wait_ge(rot_done, T - 1)
                                k = qkv_bank(T)
                                nc.scalar.copy(QK[:, T % 2, :], ps[:, k:k + 2, :].rearrange("p a n -> p (a n)")).then_inc(qk_ev, 1)
                                if l and t == 0:
                                    act.wait_ge(pv_done, UL * l)
                                nc.scalar.copy(Vb[:, t, :], ps[:, k + 2, :]).then_inc(v_ev, 1)
                            if t >= 1:
                                T = NT * l + t - 1
                                act.wait_ge(qkT_ready, T + 1)
                                nc.scalar.copy(qT[:, :, P * (t - 1):P * t], ps[:, 7, :].rearrange("p (h n) -> p h n", n=P))\
                                    .then_inc(qT_ev, 1)

                        def out_turn(t):
                            T = NT * l + t
                            act.wait_ge(oT_ready, T + 1)
                            if T >= 2:
                                act.wait_ge(y_ready, T - 1)
                            nc.scalar.copy(oT[:, T % 2].rearrange("p h n -> p (h n)"), ps[:, 0, :]).then_inc(oT_ev, 1)

                        for k in range(UL):
                            u = UL * l + k
                            t, hp = k // HP, k % HP
                            if u >= 2:
                                act.wait_ge(pt_ready, u - 1)
                            if l and k == 0:
                                act.wait_ge(on_done, NT * l)
                            for j in range(2):
                                act.wait_ge(sm_done, 2 * u + j + 1)
                                nc.scalar.activation(Pe[:, u % 2, j, :], Sm[:, u % 2, j, :], ACT.Exp, scale=-1.0,
                                                     bias=nb[:, u % 2, j:j + 1],
                                                     accum_out=sums[:, t, 2 * hp + j:2 * hp + j + 1]).then_inc(exp_done, 1)
                            if hp == 2 and t >= 1:
                                out_turn(t - 1)
                        out_turn(NT - 1)
                        act.wait_ge(tr, 2 * l + 2)
                        nc.scalar.activation(hT[:], ps[:, 0, :], ACT.Identity, scale=lgb[:, l, 0:1],
                                             bias=lgb[:, l, 1:2]).then_inc(hT_done, 1)
                        for t in range(NT + 1):
                            if t < NT:
                                T = NT * l + t
                                act.wait_ge(ug_done, T + 1)
                                if T >= 2:
                                    act.wait_ge(h_done, T - 1)
                                nc.scalar.activation(G[:, T % 2, :], UG[:, T % 2, :], ACT.Gelu).then_inc(gelu_done, 1)
                            if t >= 1:
                                T = NT * l + t - 1
                                act.wait_ge(hT2_ready, T + 1)
                                if T >= 2:
                                    act.wait_ge(y2_ready, T - 1)
                                for k, (a, z) in enumerate(HC):
                                    ins = nc.scalar.copy(HT[0:z - a, T % 2, k, :], ps[0:z - a, 5 + T % 2, P * k:P * k + P])
                                    ins.then_inc(hT2_ev, 1)

                @block.tensor
                def _(pe):
                    def turn(src, bank, n):
                        for j in range(n):
                            ins = nc.tensor.transpose(ps[:, bank, P * j:P * j + P], src(j), c["ident"][:])
                        return ins

                    for l in range(FL):
                        pe.wait_ge(sh_copy, 2 * l + 1)
                        pe.wait_ge(sh_dma, 32 * (2 * l + 1))
                        turn(lambda j: hs[:, j, :], 0, NT).then_inc(tr, 1)
                        pe.wait_ge(hT_done, 2 * l + 1)
                        for t in range(NT + 1):
                            if t < NT:
                                T = NT * l + t
                                if T >= 2:
                                    pe.wait_ge(v_ev, T - 1)
                                if l and t == 0:
                                    pe.wait_ge(y2_used, 2 * NT * l)
                                for j in range(3):
                                    ins = nc.tensor.matmul(ps[:, qkv_bank(T) + j, :], hT[:, P * t:P * t + P],
                                                           wqkv[:, l, FI * j:FI * j + FI], start=True, stop=True)
                                ins.then_inc(qkv_ready, 1)
                            if t >= 1:
                                T = NT * l + t - 1
                                pe.wait_ge(rot_done, T + 1)
                                if t >= 2:
                                    pe.wait_ge(qT_ev, T)
                                    pe.wait_ge(kT_ev, 2 * T)
                                turn(lambda j: R1[:, T % 2, P * j:P * j + P], 7, 4)
                                turn(lambda j: R1[:, T % 2, FI + P * j:FI + P * j + P], 0, 4).then_inc(qkT_ready, 1)

                        def scores(k):
                            u = UL * l + k
                            t, hp = k // HP, k % HP
                            if k == 0:
                                pe.wait_ge(qT_ev, NT * (l + 1))
                                pe.wait_ge(kT_ev, 2 * NT * (l + 1))
                                pe.wait_ge(v_ev, NT * (l + 1))
                            if u >= 2:
                                pe.wait_ge(sm_done, 2 * (u - 1))
                            for j in range(2):
                                ins = nc.tensor.matmul(ps[:, 1 + u % 2, 2 * P * j:2 * P * j + 2 * P],
                                                       qT[:, hp, P * t:P * t + P], kz[:, 2 * hp + j, P * t:P * t + 2 * P],
                                                       start=True, stop=True)
                            ins.then_inc(s_ready, 1)

                        def p_turn(k):
                            u = UL * l + k
                            pe.wait_ge(exp_done, 2 * u + 2)
                            if u >= 2:
                                pe.wait_ge(pt_ev, u - 1)
                            turn(lambda j: Pe[:, u % 2, j // 2, P * (j % 2):P * (j % 2) + P], 3 + u % 2, 4).then_inc(pt_ready, 1)

                        def values(k):
                            u = UL * l + k
                            t, hp = k // HP, k % HP
                            T = NT * l + t
                            pe.wait_ge(pt_ev, u + 1)
                            if hp == 0 and T >= 2:
                                pe.wait_ge(on_done, T - 1)
                            for j in range(2):
                                h = 2 * hp + j
                                kts = [0, 1] if t else [1]
                                for i in kts:
                                    ins = nc.tensor.matmul(ps[:, 5 + T % 2, FD * h:FD * h + FD], PT[:, u % 2, 2 * j + i, :],
                                                           Vb[:, t - 1 + i, FD * h:FD * h + FD], start=(i == kts[0]), stop=(i == 1))
                            ins.then_inc(pv_done, 1)

                        def out(t):
                            T = NT * l + t
                            pe.wait_ge(on_done, T + 1)
                            if T >= 1:
                                pe.wait_ge(oT_ev, T)
                            turn(lambda j: on[:, T % 2, P * j:P * j + P], 0, 4).then_inc(oT_ready, 1)
                            pe.wait_ge(oT_ev, T + 1)
                            if T >= 1 and t >= 1:
                                pe.wait_ge(y_used, T)
                            for j in range(4):
                                ins = nc.tensor.matmul(ps[:, 7, 0:D], oT[:, T % 2, j, :], wo[:, l, j, :],
                                                       start=(j == 0), stop=(j == 3))
                            ins.then_inc(y_ready, 1)

                        for k in range(UL + 2):
                            if k < UL:
                                scores(k)
                            if 1 <= k <= UL:
                                p_turn(k - 1)
                            if k >= 2:
                                values(k - 2)
                                if (k - 2) % HP == 1 and k - 2 > HP:
                                    out((k - 2) // HP - 1)
                        out(NT - 1)
                        pe.wait_ge(hn_done, l + 1)
                        turn(lambda j: nrm.out[:, j, :], 0, NT).then_inc(tr, 1)
                        pe.wait_ge(hT_done, 2 * l + 2)
                        for t in range(NT + 1):
                            if t < NT:
                                T = NT * l + t
                                if t >= 2:
                                    pe.wait_ge(ua_done, T - 1)
                                for j in range(2):
                                    ins = nc.tensor.matmul(ps[:, 1 + 2 * (T % 2) + j, 0:HID], hT[:, P * t:P * t + P],
                                                           w1[:, l, HID * j:HID * j + HID], start=True, stop=True)
                                ins.then_inc(up_ready, 1)
                            if t >= 1:
                                T = NT * l + t - 1
                                pe.wait_ge(h_done, T + 1)
                                if T >= 2:
                                    pe.wait_ge(hT2_ev, 3 * (T - 1))
                                for k, (a, z) in enumerate(HC):
                                    ins = nc.tensor.transpose(ps[0:z - a, 5 + T % 2, P * k:P * k + P], UA[:, T % 2, a:z],
                                                              c["ident"][:])
                                ins.then_inc(hT2_ready, 1)
                                pe.wait_ge(hT2_ev, 3 * (T + 1))
                                if T >= 1:
                                    pe.wait_ge(y2_used, 2 * T)
                                for k, (a, z) in enumerate(HC):
                                    ins = nc.tensor.matmul(ps[:, 7, 0:D], HT[0:z - a, T % 2, k, :], w2[0:z - a, l, k, :],
                                                           start=(k == 0), stop=(k == 2))
                                ins.then_inc(y2_ready, 1)

                @block.vector
                def _(v):
                    link = Chain(v, link_)
                    xs = X[:, bass.ds(b * NT, NT), :]

                    def norm(out, x, eps, n):
                        nrm.variance(nc, link, x, eps).then_inc(var_, 1)
                        v.wait_ge(pow_, n)
                        nrm.apply(nc, link, out, x)

                    norm(xb, xs, EPS, 1)
                    nc.vector.tensor_copy(yb[:, 0, 0:1], xb[:, 0, 0:1]).then_inc(xb_ready, 1)
                    for l in range(FL):
                        def rotate(t):
                            T = NT * l + t
                            v.wait_ge(qk_ev, T + 1)
                            q4 = QK[:, T % 2].rearrange("p (k h e) -> p k h e", k=2, e=FD)
                            r4 = R1[:, T % 2].rearrange("p (k h e) -> p k h e", k=2, e=FD)
                            s4 = R2[:].rearrange("p (k h e) -> p k h e", k=2, e=FD)
                            if T >= 2:
                                v.wait_ge(qkT_ready, T - 1)
                            link.step(nc.vector.tensor_tensor(R2[:], QK[:, T % 2], QK[:, T % 2], ALU.mult))
                            link.step(nc.vector.tensor_reduce(ss[:, T % 2, :], R2[:].rearrange("p (h e) -> p h e", e=FD),
                                                              AX.X, ALU.add))
                            nc.vector.tensor_scalar(ss[:, T % 2, :], ss[:, T % 2, :], 1e-24, None, ALU.max).then_inc(ss_done, 1)
                            for k in range(2):
                                cos = tab[:, l, 0, k, t, :].rearrange("p (h e) -> p h e", h=1).to_broadcast([P, FH, FD])
                                link.add(nc.vector.tensor_tensor(r4[:, k], q4[:, k], cos, ALU.mult))
                                for z in range(2):
                                    e, f = slice(32 * z, 32 * z + 32), slice(32 - 32 * z, 64 - 32 * z)
                                    sin = tab[:, l, 1, k, t, e].rearrange("p (h e) -> p h e", h=1).to_broadcast([P, FH, FD // 2])
                                    link.add(nc.vector.tensor_tensor(s4[:, k, :, e], q4[:, k, :, f], sin, ALU.mult))
                            link.wait()
                            link.step(nc.vector.tensor_tensor(R1[:, T % 2], R1[:, T % 2], R2[:], ALU.add))
                            v.wait_ge(rr_done, T + 1)
                            nc.vector.tensor_tensor(
                                R1[:, T % 2].rearrange("p (h e) -> p h e", e=FD), R1[:, T % 2].rearrange("p (h e) -> p h e", e=FD),
                                rr[:, T % 2, :].rearrange("p (h o) -> p h o", o=1).to_broadcast([P, 2 * FH, FD]),
                                ALU.mult).then_inc(rot_done, 1)

                        def key_turn(t):
                            T = NT * l + t
                            v.wait_ge(qkT_ready, T + 1)
                            for z in range(2):
                                r = slice(64 * z, 64 * z + 64)
                                ins = nc.vector.tensor_copy(kz[r, z:FH:2, P * (t + 1):P * (t + 2)],
                                                            ps[r, 0, :].rearrange("p (h n) -> p h n", n=P))
                                ins.then_inc(kT_ev, 1)

                        def mask(k):
                            u = UL * l + k
                            t = k // HP
                            v.wait_ge(s_ready, u + 1)
                            if u >= 2:
                                v.wait_ge(exp_done, 2 * (u - 1))
                            for j in range(2):
                                nc.vector.tensor_tensor_reduce(
                                    out=Sm[:, u % 2, j, :], in0=ps[:, 1 + u % 2, 2 * P * j:2 * P * j + 2 * P],
                                    in1=band[:, min(t, 1), :], scale=-8.0, scalar=-8 * BIG, op0=ALU.add, op1=ALU.min,
                                    accum_out=nb[:, u % 2, j:j + 1]).then_inc(sm_done, 1)

                        def p_evac(k):
                            u = UL * l + k
                            v.wait_ge(pt_ready, u + 1)
                            if u >= 2:
                                v.wait_ge(pv_done, u - 1)
                            nc.vector.tensor_copy(PT[:, u % 2].rearrange("p j n -> p (j n)"), ps[:, 3 + u % 2, :]).then_inc(pt_ev, 1)

                        def divide(t):
                            T = NT * l + t
                            v.wait_ge(exp_done, 2 * (UL * l + HP * (t + 1)))
                            link.step(nc.vector.reciprocal(rs[:, t, :], sums[:, t, :]))
                            v.wait_ge(pv_done, UL * l + HP * (t + 1))
                            if T >= 2:
                                v.wait_ge(oT_ready, T - 1)
                            nc.vector.tensor_tensor(
                                on[:, T % 2].rearrange("p (h e) -> p h e", e=FD), ps[:, 5 + T % 2, :].rearrange("p (h e) -> p h e", e=FD),
                                rs[:, t, :].rearrange("p (h o) -> p h o", o=1).to_broadcast([P, FH, FD]), ALU.mult).then_inc(on_done, 1)

                        def attention_residual(t):
                            T = NT * l + t
                            v.wait_ge(y_ready, T + 1)
                            ins = nc.vector.tensor_tensor(xb[:, t, :], xb[:, t, :], ps[:, 7, 0:D], ALU.add)
                            ins.then_inc(y_used, 1)

                        for t in range(NT + 1):
                            if t < NT:
                                rotate(t)
                            if t >= 1:
                                key_turn(t - 1)
                        for k in range(UL + 4):
                            if k < UL:
                                mask(k)
                            if 1 <= k <= UL:
                                p_evac(k - 1)
                            if k >= 3 and (k - 3) % HP == HP - 1:
                                divide((k - 3) // HP)
                            if k >= 2 + HP and (k - 2) % HP == 2 and (k - 2) // HP - 1 < NT - 1:
                                attention_residual((k - 2) // HP - 1)
                        attention_residual(NT - 1)
                        v.wait_ge(y_used, NT * (l + 1))
                        nc.vector.tensor_copy(yb[:, 1, 0:1], xb[:, 0, 0:1]).then_inc(xb_ready, 1)
                        v.wait_ge(sh_copy, 2 * l + 2)
                        v.wait_ge(sh_dma, 32 * (2 * l + 2))
                        norm(nrm.out, hs, EPS, 2 + l)
                        nc.vector.tensor_copy(yb[:, 0, 1:2], nrm.out[:, 0, 0:1]).then_inc(hn_done, 1)
                        for t in range(NT + 1):
                            if t < NT:
                                T = NT * l + t
                                k = 1 + 2 * (T % 2)
                                v.wait_ge(up_ready, T + 1)
                                if T >= 2:
                                    v.wait_ge(gelu_done, T - 1)
                                nc.vector.tensor_tensor(UG[:, T % 2, :], ps[:, k + 1, 0:HID], b1[:, l, HID:2 * HID],
                                                        ALU.add).then_inc(ug_done, 1)
                                if T >= 2:
                                    v.wait_ge(hT2_ready, T - 1)
                                nc.vector.tensor_tensor(UA[:, T % 2, :], ps[:, k, 0:HID], b1[:, l, 0:HID],
                                                        ALU.add).then_inc(ua_done, 1)
                                v.wait_ge(ua_done, T + 1)
                                v.wait_ge(gelu_done, T + 1)
                                nc.vector.tensor_tensor(UA[:, T % 2, :], UA[:, T % 2, :], G[:, T % 2, :], ALU.mult).then_inc(h_done, 1)
                            if t >= 1:
                                T = NT * l + t - 1
                                v.wait_ge(y2_ready, T + 1)
                                if T >= 2:
                                    v.wait_ge(y2_used, 2 * (T - 1))
                                nc.vector.tensor_tensor(yb[:, T % 2, :], ps[:, 7, 0:D], b2[:, l, :], ALU.add).then_inc(y2_used, 1)
                                v.wait_ge(y2_used, 2 * T + 1)
                                nc.vector.tensor_tensor(xb[:, t - 1, :], xb[:, t - 1, :], yb[:, T % 2, :], ALU.add).then_inc(y2_used, 1)
                        v.wait_ge(y2_used, 2 * NT * (l + 1))
                        if l + 1 < FL:
                            nc.vector.tensor_copy(yb[:, 0, 0:1], xb[:, 0, 0:1]).then_inc(xb_ready, 1)
                            v.wait_ge(xb_ready, 2 * l + 3)
                    norm(nrm.out, xb, EPS, 2 + FL)
                    link.step(nc.vector.tensor_tensor(xs, xs, nrm.out[:], ALU.add))
            clear(nc, names)


def xpos_tables():
    half = np.arange(0, FD, 2, dtype=np.float32)
    inv = (1.0 / 10000.0 ** (half / FD)).astype(np.float32)
    t = np.arange(N, dtype=np.float32)
    fr = (t[:, None] * inv[None, :]).astype(np.float32)
    fr = np.concatenate([fr, fr], axis=-1)
    base = ((half + 0.4 * FD) / (1.4 * FD)).astype(np.float32)
    power = ((t - N // 2) / float(FW // 2)).astype(np.float32)
    scale = (base[None, :] ** power[:, None]).astype(np.float32)
    scale = np.concatenate([scale, scale], axis=-1)
    sign = np.where(np.arange(FD) < FD // 2, -1.0, 1.0)
    cos, sin = np.cos(fr), np.sin(fr) * sign
    a = np.stack([np.stack([cos * scale, cos / scale]), np.stack([sin * scale, sin / scale])])
    return a.reshape(2, 2, NT, P, FD).transpose(3, 0, 1, 2, 4).astype(np.float32)


def band_masks():
    q, k = np.arange(P)[:, None], np.arange(2 * P)[None, :]
    ok = (k <= q + P) & (k >= q + P - FW)
    return np.stack([np.where(ok & (k >= P), 0.0, BIG), np.where(ok, 0.0, BIG)], axis=1).astype(np.float32)


def rows(v):
    return np.broadcast_to(v[None], (P,) + v.shape)


def arrays_of_layers(i):
    qs, ks = i["L0_ffn_q_scale"], i["L0_ffn_k_scale"]
    return {
        "f_wqkv": i["L0_ffn_wqkv"].transpose(1, 0, 2),
        "f_wo": i["L0_ffn_wo"].reshape(FL, 4, P, D).transpose(2, 0, 1, 3),
        "f_w1": i["L0_ffn_w1"].transpose(1, 0, 2),
        "f_w2": i["L0_ffn_w2"].transpose(1, 0, 2),
        "f_b1": rows(i["L0_ffn_b1"]),
        "f_b2": rows(i["L0_ffn_b2"]),
        "f_lgb": np.stack([i["L0_ffn_ln_g"], i["L0_ffn_ln_b"]], axis=-1).transpose(1, 0, 2),
        "f_sc": rows(np.stack([np.stack([qs, ks], 1), np.stack([swap(qs), swap(ks)], 1)], 1)),
        "f_base": xpos_tables(),
        "f_band": band_masks(),
    }


RH, RD = 16, 8
RG = 4
RW = 2 * N
BW = N + P
MAX_LEN = 625


def relative_attention(nc, X, ps, c, d):
    with ExitStack() as ctx:
        s = Store(nc, ctx, "r")
        Qu = s.sb("Qu", [P, RG, B * N], F32R)
        Qv = s.sb("Qv", [P, RG, B * N], F32R)
        Kst = s.sb("Kst", [P, RG, B * N], F32R)
        Rst = s.sb("Rst", [P, RG, RW], F32R)
        V = s.sb("V", [P, B, NT, P])
        wo = s.sb("wo", [P, D])
        bo = s.sb("bo", [P, D])
        hm = s.sb("hm", [P, RG])
        sel = s.sb("sel", [RH, P])
        with ExitStack() as ctx0:
            make_stacks(nc, Store(nc, ctx0, "r0"), X, ps, c, d, Qu, Qv, Kst, Rst, V, wo, bo, hm, sel)
        relative_heads(nc, s, X, ps, c, d, Qu, Qv, Kst, Rst, V, wo, bo, hm, sel)


def make_stacks(nc, s, X, ps, c, d, Qu, Qv, Kst, Rst, V, wo, bo, hm, sel):
    w = s.sb("w", [P, 4, P])
    gb = s.sb("gb", [P, 2])
    uv = s.sb("uv", [P, 2])
    emb = s.sb("emb", [P, RW])
    xT = s.sb("xT", [P, N])
    full = s.sb("full", [P, 3, N])
    hi = s.sb("hi", [P, 3, B * N], F32R)
    lo = s.sb("lo", [P, 3, B * N], F32R)
    rhi = s.sb("rhi", [P, RW], F32R)
    rlo = s.sb("rlo", [P, RW], F32R)
    n1, n2 = Norm(s, "n1"), Norm(s, "n2")
    names = (w_in, r_ready, rhi_done, rlo_done, norm_done, tr, xT_done, p_ready, full_done, v_ev, hi_done, lo_done,
             stacked, link_, var_, pow_) = s.sems(
        *"w_in r_ready rhi_done rlo_done norm_done tr xT_done p_ready full_done v_ev hi_done lo_done stacked link var pow".split())

    def stack(sp, dst, halves):
        for g in range(RG):
            for k, src in enumerate(halves):
                sp.dma_start(dst[32 * k:32 * k + 32, g].bitcast(F32), src[32 * g:32 * g + 32].bitcast(F32)).then_inc(stacked, 16)

    with nc.Block() as block:
        @block.sync
        def _(sp):
            for dst, src in ((w, "r_w"), (gb, "r_gb"), (uv, "r_uv"), (emb, "r_emb"), (wo, "r_wo"), (bo, "r_bo"), (hm, "r_hm"), (sel, "r_sel")):
                sp.dma_start(dst[:], d[src]).then_inc(w_in, 16)
            sp.wait_ge(rhi_done, 1)
            sp.wait_ge(rlo_done, 2)
            stack(sp, Rst, (rhi, rhi, rlo, rlo))
            sp.wait_ge(stacked, 256)

        @block.tensor
        def _(pe):
            pe.wait_ge(w_in, 128)
            for k in range(2):
                ins = nc.tensor.matmul(ps[:, k, :], w[:, 3, :], emb[:, N * k:N * k + N], start=True, stop=True)
            ins.then_inc(r_ready, 1)

        @block.scalar
        def _(act):
            act.wait_ge(r_ready, 1)
            nc.scalar.copy(rhi[:], ps[:, 0:2, :].rearrange("p a n -> p (a n)")).then_inc(rhi_done, 1)

        @block.vector
        def _(v):
            v.wait_ge(rhi_done, 1)
            for k in range(2):
                nc.vector.tensor_tensor(rlo[:, N * k:N * k + N], ps[:, k, :], rhi[:, N * k:N * k + N].bitcast(F32),
                                        ALU.subtract).then_inc(rlo_done, 1)
    clear(nc, names)

    with nc.Fori(0, B) as b:
        with nc.Block() as block:
            @block.gpsimd
            def _(pool):
                for k, n in enumerate((n1, n2)):
                    pool.wait_ge(var_, k + 1)
                    n.power(nc, c).then_inc(pow_, 1)

            @block.tensor
            def _(pe):
                pe.wait_ge(norm_done, 1)
                for t in range(NT):
                    ins = nc.tensor.transpose(ps[:, 0, P * t:P * t + P], n2.out[:, t, :], c["ident"][:])
                ins.then_inc(tr, 1)
                pe.wait_ge(xT_done, 1)
                for j in range(2):
                    nc.tensor.matmul(ps[:, 1 + j, :], w[:, j, :], xT[:], start=True, stop=True).then_inc(p_ready, 1)
                for t in range(NT):
                    ins = nc.tensor.matmul(ps[:, 3, P * t:P * t + P], xT[:, P * t:P * t + P], w[:, 2, :],
                                           start=True, stop=True)
                ins.then_inc(p_ready, 1)

            @block.scalar
            def _(act):
                act.wait_ge(tr, 1)
                nc.scalar.activation(xT[:], ps[:, 0, :], ACT.Identity, scale=gb[:, 0:1], bias=gb[:, 1:2]).then_inc(xT_done, 1)
                act.wait_ge(p_ready, 3)
                nc.scalar.copy(V[:, bass.ds(b, 1)].rearrange("p b t n -> p (b t n)"), ps[:, 3, :]).then_inc(v_ev, 1)
                for j in range(3):
                    act.wait_ge(full_done, j + 1)
                    nc.scalar.copy(hi[:, j, bass.ds(b * N, N)], full[:, j, :]).then_inc(hi_done, 1)

            @block.vector
            def _(v):
                link = Chain(v, link_)
                n1.variance(nc, link, X[:, bass.ds(b * NT, NT), :], EPS).then_inc(var_, 1)
                v.wait_ge(pow_, 1)
                n1.apply(nc, link, n1.out, X[:, bass.ds(b * NT, NT), :])
                n2.variance(nc, link, n1.out, 1e-6).then_inc(var_, 1)
                v.wait_ge(pow_, 2)
                n2.apply(nc, link, n2.out, n1.out)
                nc.vector.tensor_copy(n1.rstd[:, 0:1], n2.out[:, 0, 0:1]).then_inc(norm_done, 1)
                v.wait_ge(p_ready, 1)
                for j in range(2):
                    nc.vector.tensor_scalar(full[:, j, :], ps[:, 1, :], uv[:, j:j + 1], None, ALU.add).then_inc(full_done, 1)
                v.wait_ge(p_ready, 2)
                nc.vector.tensor_copy(full[:, 2, :], ps[:, 2, :]).then_inc(full_done, 1)
                for j in range(3):
                    v.wait_ge(full_done, j + 1)
                    v.wait_ge(hi_done, j + 1)
                    nc.vector.tensor_tensor(lo[:, j, bass.ds(b * N, N)], full[:, j, :], hi[:, j, bass.ds(b * N, N)].bitcast(F32),
                                            ALU.subtract).then_inc(lo_done, 1)
        clear(nc, names)

    with nc.Block() as block:
        @block.sync
        def _(sp):
            stack(sp, Qu, (hi[:, 0], lo[:, 0], hi[:, 0], lo[:, 0]))
            stack(sp, Qv, (hi[:, 1], lo[:, 1], hi[:, 1], lo[:, 1]))
            stack(sp, Kst, (hi[:, 2], hi[:, 2], lo[:, 2], lo[:, 2]))
            sp.wait_ge(stacked, 768)
    clear(nc, names)


def relative_heads(nc, s, X, ps, c, d, Qu, Qv, Kst, Rst, V, wo, bo, hm, sel):
    STEPS = RH * NT
    PAIRS = STEPS // 2
    BUFS, SCRATCH = 3, 5
    LAG = 8
    spill = [nc.dram_tensor(f"spill{k}", (2, P, BW), F32, kind="Internal").ap() for k in range(SCRATCH)]
    qu = s.sb("qu", [P, 2, N], F32R)
    qv = s.sb("qv", [P, 2, N], F32R)
    BD = s.sb("BD", [P, BUFS, 2, BW])
    Sx = s.sb("Sx", [P, SCRATCH, 2, N])
    PT = s.sb("PT", [P, 2, NT, N])
    Vm = s.sb("Vm", [P, NT, RG, P])
    nb = s.sb("nb", [P, 2, NT])
    sums = s.sb("sums", [P, NT, RH])
    rs = s.sb("rs", [P, NT, RH])
    rsT = s.sb("rsT", [RH, N])
    oT = s.sb("oT", [P, N])
    yb = s.sb("yb", [P, NT, D])
    nrm = Norm(s, "n")
    names = (qv_done, qu_done, bd_ready, bd_ev, wr0, wr1, wr2, rd0, rd1, rd2, rd3, rd4, ac_ready, sx_done, exp_done, t_ready,
             t_ev, pv_done, rs_done, on_done, zeroed, vm_done, rs_tr, rs_ev, rs_ready, o_ev, y_ready, y_done, link_, var_, pow_) = s.sems(
        *("qv_done qu_done bd_ready bd_ev wr0 wr1 wr2 rd0 rd1 rd2 rd3 rd4 ac_ready sx_done exp_done t_ready t_ev pv_done rs_done "
          "on_done zeroed vm_done rs_tr rs_ev rs_ready o_ev y_ready y_done link var pow").split())
    wr, rd = (wr0, wr1, wr2), (rd0, rd1, rd2, rd3, rd4)
    assert len(rd) == SCRATCH and len(wr) == BUFS
    BDB = (0, 1, 7)
    HW = BW // 2
    SCALE = RD ** -0.5
    with nc.Fori(0, B) as b:
        with nc.Block() as block:
            @block.sync
            def _(sp):
                for k in range(PAIRS + 1):
                    if k < PAIRS:
                        sp.wait_ge(bd_ev, 4 * (k + 1))
                        if k >= SCRATCH:
                            sp.wait_ge(rd[k % SCRATCH], 16 * (k // SCRATCH))
                        sp.dma_start(spill[k % SCRATCH].rearrange("t p n -> p t n"), BD[:, k % BUFS])\
                            .then_inc(wr[k % BUFS], 16)
                    if k >= 1:
                        m = k - 1
                        sp.wait_ge(wr[m % BUFS], 16 * (m // BUFS + 1))
                        if m >= SCRATCH:
                            sp.wait_ge(t_ready, 2 * (m - SCRATCH + 1))
                        a = spill[m % SCRATCH]
                        skew = bass.AP(tensor=a.tensor, offset=P - 1, ap=[[BW - 1, P], [P * BW, 2], [1, N]])
                        sp.dma_start(Sx[:, m % SCRATCH], skew).then_inc(rd[m % SCRATCH], 16)
                for k in range(SCRATCH):
                    sp.wait_ge(rd[k], 16 * len(range(k, PAIRS, SCRATCH)))

            @block.gpsimd
            def _(pool):
                nc.gpsimd.memset(Vm[:], 0.0).then_inc(zeroed, 1)
                pool.wait_ge(var_, 1)
                nrm.power(nc, c).then_inc(pow_, 1)

            @block.tensor
            def _(pe):
                def relative(n):
                    h, lt = n // NT, n % NT
                    pe.wait_ge(qv_done, h + 1)
                    for j in range(2):
                        m = 2 * n + j
                        if m >= 3:
                            pe.wait_ge(bd_ev, m - 2)
                        r0 = N - P - P * lt + HW * j
                        nc.tensor.matmul(ps[:, BDB[m % 3], 0:HW], qv[:, h % 2, P * lt:P * lt + P],
                                         Rst[:, h // RG, r0:r0 + HW], start=True, stop=True).then_inc(bd_ready, 1)

                def content(n):
                    h, lt = n // NT, n % NT
                    pe.wait_ge(qu_done, h + 1)
                    if n >= 2:
                        pe.wait_ge(sx_done, n - 1)
                    nc.tensor.matmul(ps[:, 2 + n % 2, :], qu[:, h % 2, P * lt:P * lt + P], Kst[:, h // RG, bass.ds(b * N, N)],
                                     start=True, stop=True).then_inc(ac_ready, 1)

                def turn(n):
                    pe.wait_ge(exp_done, n + 1)
                    if n >= 2:
                        pe.wait_ge(t_ev, n - 1)
                    for j in range(NT):
                        ins = nc.tensor.transpose(ps[:, 4 + n % 2, P * j:P * j + P],
                                                  Sx[:, n // 2 % SCRATCH, n % 2, P * j:P * j + P], c["ident"][:])
                    ins.then_inc(t_ready, 1)

                def values(n):
                    h, kt = n // NT, n % NT
                    if kt == 0:
                        pe.wait_ge(t_ev, NT * (h + 1))
                    if n == 0:
                        pe.wait_ge(vm_done, RG)
                    r = 32 * (h // RG)
                    nc.tensor.matmul(ps[r:r + 32, 6, :], Vm[:, kt, h // RG, 32 * (h % RG):32 * (h % RG) + 32],
                                     PT[:, h % 2, kt, :], start=(h % RG == 0 and kt == 0),
                                     stop=(h % RG == RG - 1 and kt == NT - 1)).then_inc(pv_done, 1)

                for k in range(STEPS + LAG + 6):
                    if k < STEPS:
                        relative(k)
                    for part, late in ((content, LAG), (turn, LAG + 2), (values, LAG + 6)):
                        if 0 <= k - late < STEPS:
                            part(k - late)
                pe.wait_ge(rs_done, 1)
                for t in range(NT):
                    ins = nc.tensor.transpose(ps[0:RH, 0, P * t:P * t + P], rs[:, t, :], c["ident"][:])
                ins.then_inc(rs_tr, 1)
                pe.wait_ge(rs_ev, 1)
                nc.tensor.matmul(ps[:, 1, :], sel[:], rsT[:], start=True, stop=True).then_inc(rs_ready, 1)
                pe.wait_ge(on_done, 1)
                for t in range(NT):
                    ins = nc.tensor.matmul(ps[:, 0, P * t:P * t + P], oT[:, P * t:P * t + P], wo[:], start=True, stop=True)
                ins.then_inc(y_ready, 1)

            @block.scalar
            def _(act):
                def relative(n):
                    if n % 2 == 0 and n // 2 >= BUFS:
                        act.wait_ge(wr[n // 2 % BUFS], 16 * (n // 2 // BUFS))
                    for j in range(2):
                        m = 2 * n + j
                        act.wait_ge(bd_ready, m + 1)
                        nc.scalar.copy(BD[:, n // 2 % BUFS, n % 2, HW * j:HW * j + HW], ps[:, BDB[m % 3], 0:HW])\
                            .then_inc(bd_ev, 1)

                def exps(n):
                    h, lt = n // NT, n % NT
                    act.wait_ge(sx_done, n + 1)
                    row = Sx[:, n // 2 % SCRATCH, n % 2, :]
                    nc.scalar.activation(row, row, ACT.Exp, scale=-1.0, bias=nb[:, h % 2, lt:lt + 1],
                                         accum_out=sums[:, lt, h:h + 1]).then_inc(exp_done, 1)

                act.wait_ge(zeroed, 1)
                for k in range(STEPS + LAG):
                    if k < STEPS:
                        relative(k)
                    if 1 <= k <= RG:
                        r = k - 1
                        nc.scalar.copy(Vm[:, :, :, 40 * r:40 * r + RD],
                                       V[:, bass.ds(b, 1)].rearrange("p b t (g e) -> p (b t) g e", g=RG)
                                       [:, :, :, RD * r:RD * r + RD]).then_inc(vm_done, 1)
                    if k >= LAG:
                        exps(k - LAG)
                act.wait_ge(rs_tr, 1)
                nc.scalar.copy(rsT[:], ps[0:RH, 0, :]).then_inc(rs_ev, 1)
                act.wait_ge(pv_done, STEPS)
                nc.scalar.copy(oT[:], ps[:, 6, :]).then_inc(o_ev, 1)

            @block.vector
            def _(v):
                def mask(dst, src, h, done, free, per):
                    if h >= 2:
                        v.wait_ge(free, per * (h - 1))
                    nc.vector.tensor_scalar(dst[:, h % 2, :], src[:, h // RG, bass.ds(b * N, N)].bitcast(F32),
                                            hm[:, h % RG:h % RG + 1], None, ALU.mult).then_inc(done, 1)

                def add(n):
                    h, lt, m = n // NT, n % NT, n // 2
                    v.wait_ge(ac_ready, n + 1)
                    v.wait_ge(rd[m % SCRATCH], 16 * (m // SCRATCH + 1))
                    if n >= 2 * NT:
                        v.wait_ge(exp_done, n - 2 * NT + 1)
                    row = Sx[:, m % SCRATCH, n % 2, :]
                    nc.vector.tensor_tensor_reduce(
                        out=row, in0=ps[:, 2 + n % 2, :], in1=row, scale=-SCALE,
                        scalar=-BIG, op0=ALU.add, op1=ALU.min, accum_out=nb[:, h % 2, lt:lt + 1]).then_inc(sx_done, 1)

                def evacuate(n):
                    v.wait_ge(t_ready, n + 1)
                    h, lt = n // NT, n % NT
                    if h >= 2:
                        v.wait_ge(pv_done, NT * (h - 1))
                    nc.vector.tensor_copy(PT[:, h % 2, :, P * lt:P * lt + P],
                                          ps[:, 4 + n % 2, :].rearrange("p (j n) -> p j n", j=NT)).then_inc(t_ev, 1)

                for k in range(STEPS + LAG + 2):
                    if k % NT == 0 and k // NT < RH:
                        mask(qv, Qv, k // NT, qv_done, bd_ready, 2 * NT)
                    if k >= LAG - 2 and (k - LAG + 2) % NT == 0 and (k - LAG + 2) // NT < RH:
                        mask(qu, Qu, (k - LAG + 2) // NT, qu_done, ac_ready, NT)
                    if 0 <= k - LAG < STEPS:
                        add(k - LAG)
                    if 0 <= k - LAG - 2 < STEPS:
                        evacuate(k - LAG - 2)
                link = Chain(v, link_)
                v.wait_ge(exp_done, NT * RH)
                nc.vector.reciprocal(rs[:], sums[:]).then_inc(rs_done, 1)
                v.wait_ge(rs_ready, 1)
                v.wait_ge(o_ev, 1)
                nc.vector.tensor_tensor(oT[:], oT[:], ps[:, 1, :], ALU.mult).then_inc(on_done, 1)
                v.wait_ge(y_ready, 1)
                for t in range(NT):
                    link.add(nc.vector.tensor_tensor(yb[:, t, :], ps[:, 0, P * t:P * t + P], bo[:], ALU.add))
                link.wait()
                nrm.variance(nc, link, yb, EPS).then_inc(var_, 1)
                v.wait_ge(pow_, 1)
                nrm.apply(nc, link, nrm.out, yb)
                xs = X[:, bass.ds(b * NT, NT), :]
                link.step(nc.vector.tensor_tensor(xs, xs, nrm.out[:], ALU.add))
        clear(nc, names)


GHID = 384
GC = GHID // P
QSCALE = 1.0 / 127.0


def gated_feed_forward(nc, X, ps, c, d):
    with ExitStack() as ctx:
        s = Store(nc, ctx, "g")
        wgu = s.sb("wgu", [P, 2, GHID])
        wd = s.sb("wd", [P, GC, D])
        with ExitStack() as ctx0:
            s0 = Store(nc, ctx0, "g0")
            gui = s0.sb("gui", [P, 2, GHID], I32)
            di = s0.sb("di", [P, GC, D], I32)
            names = w_in, done = s0.sems("w_in", "done")
            with nc.Block() as block:
                @block.sync
                def _(sp):
                    sp.dma_start(gui[:], d["g_wgu"]).then_inc(w_in, 16)
                    sp.dma_start(di[:], d["g_wd"]).then_inc(w_in, 16)

                @block.vector
                def _(v):
                    v.wait_ge(w_in, 32)
                    nc.vector.tensor_scalar(wgu[:], gui[:], QSCALE, None, ALU.mult).then_inc(done, 1)
                    nc.vector.tensor_scalar(wd[:], di[:], QSCALE, None, ALU.mult).then_inc(done, 1)
                    v.wait_ge(done, 2)
            clear(nc, names)
        xT = s.sb("xT", [P, N])
        G = s.sb("G", [P, 2, GHID])
        H = s.sb("H", [P, 2, GHID])
        HT = s.sb("HT", [P, 2, GC, P])
        nrm = Norm(s, "n")
        names = (norm_done, tr, xT_done, up_ready, g_done, h_done, hT_ready, hT_ev, y_ready, link_, var_, pow_) = s.sems(
            *"norm_done tr xT_done up_ready g_done h_done hT_ready hT_ev y_ready link var pow".split())
        with nc.Fori(0, B) as b:
            with nc.Block() as block:
                @block.gpsimd
                def _(pool):
                    for k in range(2):
                        pool.wait_ge(var_, k + 1)
                        nrm.power(nc, c).then_inc(pow_, 1)

                @block.tensor
                def _(pe):
                    pe.wait_ge(norm_done, 1)
                    for t in range(NT):
                        ins = nc.tensor.transpose(ps[:, 0, P * t:P * t + P], nrm.out[:, t, :], c["ident"][:])
                    ins.then_inc(tr, 1)
                    pe.wait_ge(xT_done, 1)
                    for t in range(NT + 1):
                        if t < NT:
                            if t >= 2:
                                pe.wait_ge(h_done, t - 1)
                            for j in range(2):
                                ins = nc.tensor.matmul(ps[:, 1 + 2 * (t % 2) + j, 0:GHID], xT[:, P * t:P * t + P], wgu[:, j, :],
                                                       start=True, stop=True)
                            ins.then_inc(up_ready, 1)
                        if t >= 1:
                            n = t - 1
                            pe.wait_ge(h_done, n + 1)
                            if n >= 2:
                                pe.wait_ge(hT_ev, n - 1)
                            for k in range(GC):
                                ins = nc.tensor.transpose(ps[:, 5 + n % 2, P * k:P * k + P], H[:, n % 2, P * k:P * k + P],
                                                          c["ident"][:])
                            ins.then_inc(hT_ready, 1)
                            pe.wait_ge(hT_ev, n + 1)
                            for k in range(GC):
                                ins = nc.tensor.matmul(ps[:, 7, P * n:P * n + P], HT[:, n % 2, k, :], wd[:, k, :],
                                                       start=(k == 0), stop=(k == GC - 1))
                            ins.then_inc(y_ready, 1)

                @block.scalar
                def _(act):
                    act.wait_ge(tr, 1)
                    nc.scalar.copy(xT[:], ps[:, 0, :]).then_inc(xT_done, 1)
                    for t in range(NT + 1):
                        if t < NT:
                            act.wait_ge(up_ready, t + 1)
                            if t >= 2:
                                act.wait_ge(h_done, t - 1)
                            nc.scalar.activation(G[:, t % 2, :], ps[:, 1 + 2 * (t % 2), 0:GHID], ACT.Silu).then_inc(g_done, 1)
                        if t >= 1:
                            n = t - 1
                            act.wait_ge(hT_ready, n + 1)
                            if n >= 2:
                                act.wait_ge(y_ready, n - 1)
                            nc.scalar.copy(HT[:, n % 2].rearrange("p k n -> p (k n)"), ps[:, 5 + n % 2, 0:GHID]).then_inc(hT_ev, 1)

                @block.vector
                def _(v):
                    link = Chain(v, link_)
                    xs = X[:, bass.ds(b * NT, NT), :]
                    nrm.variance(nc, link, xs, EPS).then_inc(var_, 1)
                    v.wait_ge(pow_, 1)
                    nrm.apply(nc, link, nrm.out, xs)
                    nc.vector.tensor_copy(nrm.st[:, 0, 0:1], nrm.out[:, 0, 0:1]).then_inc(norm_done, 1)
                    for t in range(NT):
                        v.wait_ge(g_done, t + 1)
                        if t >= 2:
                            v.wait_ge(hT_ready, t - 1)
                        nc.vector.tensor_tensor(H[:, t % 2, :], ps[:, 2 + 2 * (t % 2), 0:GHID], G[:, t % 2, :],
                                                ALU.mult).then_inc(h_done, 1)
                    v.wait_ge(y_ready, NT)
                    y = ps[:, 7, :].rearrange("p (t n) -> p t n", n=D)
                    v.wait_ge(norm_done, 1)
                    nrm.variance(nc, link, y, EPS).then_inc(var_, 1)
                    v.wait_ge(pow_, 2)
                    nrm.apply(nc, link, nrm.out, y)
                    link.step(nc.vector.tensor_tensor(xs, xs, nrm.out[:], ALU.add))
            clear(nc, names)


def arrays_of_rest(i):
    emb = i["L1_attn_rel_pos_emb"][MAX_LEN - (N - 1):MAX_LEN - (N - 1) + RW]
    p = np.arange(P)
    return {
        "r_w": np.stack([i["L1_attn_Wq"], i["L1_attn_Wk"], i["L1_attn_Wv"], i["L1_attn_Wr"]], axis=1),
        "r_gb": np.stack([i["L1_attn_gamma"], i["L1_attn_beta"]], axis=1),
        "r_uv": np.stack([i["L1_attn_u_bias"].reshape(P), i["L1_attn_v_bias"].reshape(P)], axis=1),
        "r_emb": emb.T,
        "r_wo": i["L1_attn_Wo"],
        "r_bo": rows(i["L1_attn_bo"]),
        "r_sel": (np.arange(P)[None, :] // RD == np.arange(RH)[:, None]).astype(np.float32),
        "r_hm": ((p[:, None] % 32) // RD == np.arange(RG)[None, :]).astype(np.float32),
        "g_wgu": np.stack([i["L1_ffn_w_gate"].T, i["L1_ffn_w_up"].T], axis=1),
        "g_wd": i["L1_ffn_w_down"].T.reshape(GC, P, D).transpose(1, 0, 2),
    }


def program(nc, d, out):
    with ExitStack() as ctx:
        s = Store(nc, ctx, "m")
        X = s.sb("X", [P, TT, D])
        c = {"ident": s.sb("ident", [P, P]), "identb": s.sb("identb", [P, P], BF16), "trib": s.sb("trib", [P, P], BF16),
             "mhalf": s.sb("mhalf", [P, 16])}
        ps = ctx.enter_context(nc.psum_tensor("ps", [P, 8, 512], F32))
        names = c_in, c_tri, c_done, done = s.sems("c_in", "c_tri", "c_done", "done")
        with ExitStack() as ctx0:
            tri = Store(nc, ctx0, "m0").sb("tri", [P, P])
            with nc.Block() as block:
                @block.sync
                def _(sp):
                    sp.dma_start(c["ident"][:], d["ident"]).then_inc(c_in, 16)
                    sp.dma_start(tri[:], d["tri"]).then_inc(c_tri, 16)

                @block.vector
                def _(v):
                    v.wait_ge(c_in, 16)
                    nc.vector.tensor_copy(c["identb"][:], c["ident"][:]).then_inc(c_done, 1)
                    v.wait_ge(c_tri, 16)
                    nc.vector.tensor_copy(c["trib"][:], tri[:]).then_inc(c_done, 1)
                    nc.vector.memset(c["mhalf"][:], -0.5).then_inc(c_done, 1)
                    v.wait_ge(c_done, 3)
        clear(nc, names)
        with ExitStack() as ctxz:
            RS = Store(nc, ctxz, "z").sb("RS", [P, TT, AH])
            zd = nc.dram_tensor("zd", (B, AH * AR, N), F32, kind="Internal").ap()
            causal_attention(nc, X, RS, zd, ps, c, d)
            output_and_residual(nc, X, RS, zd, ps, c, d)
        local_layers(nc, X, ps, c, d)
        relative_attention(nc, X, ps, c, d)
        gated_feed_forward(nc, X, ps, c, d)

        with nc.Block() as block:
            @block.sync
            def _(sp):
                sp.dma_start(out.rearrange("b (t p) d -> p (b t) d", p=P), X[:]).then_inc(done, 16)
                sp.wait_ge(done, 16)


def kernel(**inputs):
    import concourse.bacc as bacc
    from concourse.bass_utils import run_bass_kernel_spmd

    i = {k: np.asarray(v) for k, v in inputs.items()}
    arrays = {"in_" + k: np.ascontiguousarray(v) for k, v in (arrays_of(i) | arrays_of_layers(i) | arrays_of_rest(i)).items()}
    nc = bacc.Bacc("TRN2", target_bir_lowering=False, num_devices=1)
    d = {k[3:]: nc.dram_tensor(k, v.shape, mybir.dt.from_np(v.dtype), kind="ExternalInput").ap() for k, v in arrays.items()}
    out = nc.dram_tensor("out", (B, N, D), F32, kind="ExternalOutput").ap()
    program(nc, d, out)
    r = run_bass_kernel_spmd(nc, [arrays], core_ids=[0])
    return r.results[0]["out"]
```

```python
from contextlib import ExitStack

import numpy as np

import concourse.bass as bass
from concourse import mybir

ALU = mybir.AluOpType
ACT = mybir.ActivationFunctionType
AX = mybir.AxisListType
F32 = mybir.dt.float32
F32R = mybir.dt.float32r
BF16 = mybir.dt.bfloat16
I32 = mybir.dt.int32

P = 128
B, N, D = 4, 512, 128
NT = N // P
TT = B * NT
EPS = 1e-5
BIG = -1e30

AH, AD, AR, AV = 32, 32, 8, 16
GH = P // AD
AG = AH // GH
KN = N + AV
PITCH = N + AV
NB = 2


class Chain:

    def __init__(self, eng, sem):
        self.eng, self.sem, self.n = eng, sem, 0

    def add(self, ins):
        self.n += 1
        ins.then_inc(self.sem, 1)

    def wait(self):
        self.eng.wait_ge(self.sem, self.n)

    def step(self, ins):
        self.add(ins)
        self.wait()


class Store:

    def __init__(self, nc, ctx, tag):
        self.nc, self.ctx, self.tag = nc, ctx, tag

    def sb(self, name, shape, dt=F32):
        return self.ctx.enter_context(self.nc.sbuf_tensor(f"{self.tag}_{name}", shape, dt))

    def sem(self, name):
        return self.ctx.enter_context(self.nc.semaphore(f"{self.tag}_{name}"))

    def sems(self, *names):
        return [self.sem(n) for n in names]


def clear(nc, sems):
    nums = sorted(s.num for s in sems)
    starts = [n for n in nums if n - 1 not in nums]
    ends = [n + 1 for n in nums if n + 1 not in nums]
    for first, end in zip(starts, ends):
        nc.all_engine_barrier(sems_to_clear=range(first, end))


def causal_attention(nc, X, RS, zd, ps, c, d):
    with ExitStack() as ctx:
        s = Store(nc, ctx, "a")
        xnT = s.sb("xnT", [P, B * N])
        V = s.sb("V", [P, B, NT, AH * AR])
        V0 = s.sb("V0", [P, B, AG, GH * AR])
        W = s.sb("W", [P, 2, 4, P])
        bias = s.sb("bias", [P, 2, 4])
        vk = s.sb("vk", [P, 2, AV])
        x0 = s.sb("x0", [P, B, GH, 32])
        wv = s.sb("wv", [P, AH * AR])
        bv = s.sb("bv", [P, AH * AR])
        with ExitStack() as ctx0:
            s0 = Store(nc, ctx0, "a0")
            xn = s0.sb("xn", [P, 2, D])
            st = s0.sb("st", [P, TT, 6])
            mv = s0.sb("mv", [P, TT, 2])
            rstd = s0.sb("rstd", [P, TT])
            x_in, w_in, stats, stats_done, pow_done, xn_done, xt_done, xt_used, zeroed, vv_in, x0_done = s0.sems(
                "x_in", "w_in", "stats", "stats_done", "pow_done", "xn_done", "xt_done", "xt_used", "zeroed", "vv_in", "x0_done")
            with nc.Block() as block:
                @block.sync
                def _(sp):
                    sp.dma_start(X[:], d["x"].rearrange("b (t p) d -> p (b t) d", p=P)).then_inc(x_in, 16)
                    sp.dma_start(wv[:], d["a_wv"]).then_inc(w_in, 16)
                    sp.dma_start(bv[:], d["a_bv"]).then_inc(w_in, 16)
                    sp.dma_start(W[:, 0], d["a_w"][0]).then_inc(w_in, 16)
                    sp.dma_start(bias[:, 0], d["a_b"][0]).then_inc(w_in, 16)
                    sp.dma_start(vk[:, 0], d["a_vk"][0]).then_inc(w_in, 16)
                    for b in range(B):
                        sp.dma_start(V[P - AV:P, b, NT - 1, :], d["a_vv"]).then_inc(vv_in, 16)
                    sp.wait_ge(w_in, 80)
                    sp.wait_ge(vv_in, 16 * B)

                @block.gpsimd
                def _(pool):
                    nc.gpsimd.memset(V0[:], 0.0).then_inc(zeroed, 1)
                    nc.gpsimd.memset(x0[:], 0.0).then_inc(zeroed, 1)
                    pool.wait_ge(stats_done, 1)
                    nc.gpsimd.tensor_tensor(rstd[:], mv[:, :, 1], c["mhalf"][:, 0:TT], ALU.pow).then_inc(pow_done, 1)

                @block.vector
                def _(v):
                    link = Chain(v, stats)
                    v.wait_ge(x_in, 16)
                    for t in range(TT):
                        nc.vector.bn_stats(st[:, t, :], X[:, t, :]).then_inc(stats, 1)
                    link.n = TT
                    v.wait_ge(stats, TT)
                    for t in range(TT):
                        nc.vector.bn_aggr(mv[:, t, :], st[:, t, :]).then_inc(stats, 1)
                    link.n = 2 * TT
                    v.wait_ge(stats, 2 * TT)
                    nc.vector.tensor_scalar(mv[:, :, 1], mv[:, :, 1], EPS, None, ALU.add).then_inc(stats_done, 1)
                    v.wait_ge(pow_done, 1)
                    for t in range(TT):
                        if t >= 2:
                            v.wait_ge(xt_done, t - 1)
                        nc.vector.tensor_scalar(xn[:, t % 2, :], X[:, t, :], mv[:, t, 0:1], rstd[:, t:t + 1],
                                                ALU.subtract, ALU.mult).then_inc(xn_done, 1)
                    v.wait_ge(xn_done, TT)

                @block.tensor
                def _(pe):
                    for t in range(TT):
                        pe.wait_ge(xn_done, t + 1)
                        if t >= 4:
                            pe.wait_ge(xt_used, t - 3)
                        nc.tensor.transpose(ps[:, t % 4, 0:P], xn[:, t % 2, :], c["ident"][:]).then_inc(xt_done, 1)

                @block.scalar
                def _(act):
                    act.wait_ge(zeroed, 2)
                    for t in range(TT):
                        act.wait_ge(xt_done, t + 1)
                        if t % NT == 0:
                            first = ps[:, t % 4, 0:AV].rearrange("p (o k) -> p o k", o=1).to_broadcast([P, GH, AV])
                            nc.scalar.copy(x0[:, t // NT, :, 0:AV], first).then_inc(x0_done, 1)
                        nc.scalar.copy(xnT[:, P * t:P * t + P], ps[:, t % 4, 0:P]).then_inc(xt_used, 1)
        clear(nc, [x_in, w_in, stats, stats_done, pow_done, xn_done, xt_done, xt_used, zeroed, vv_in, x0_done])
        attention_groups(nc, s, RS, zd, ps, c, d, xnT, V, V0, x0, wv, bv, W, bias, vk)


def attention_groups(nc, s, RS, zd, ps, c, d, xnT, V, V0, x0, wv, bv, W, bias, vk):
    Qst = [s.sb(f"Qst{i}", [P, GH, NB, N], F32R) for i in range(2)]
    Kst = [s.sb(f"Kst{i}", [P, GH, NB, KN], F32R) for i in range(2)]
    qh = s.sb("qh", [P, NB, N], F32R)
    ql = s.sb("ql", [P, NB, N], F32R)
    kh = s.sb("kh", [P, NB, KN], F32R)
    kl = s.sb("kl", [P, NB, KN], F32R)
    rot = s.sb("rot", [P, 4, N])
    full = s.sb("full", [P, 2, N])
    Pm = s.sb("Pm", [P, 2, NT, PITCH])
    PT = s.sb("PT", [P, 2, 10, P])
    P0 = s.sb("P0", [P, 2, NT, GH * 32])
    P0T = s.sb("P0T", [P, N])
    Vm = s.sb("Vm", [P, 2, NT, GH * 40])
    V0m = s.sb("V0m", [P, 2, GH * AR])
    zs = s.sb("zs", [P, N])
    tab = s.sb("tab", [P, 4, N])
    nm = s.sb("nm", [P, 2, NT])
    sums = s.sb("sums", [P, NB, NT, GH])
    names = (w_in, pj_ready, stt_done, added, hi_done, lo_done, s_ready, nm_ready, exp_done, t_done, evd, eva, pv_done, o_rs,
             tab_in, pad_done, p0_done, p0_tr, p0_ev, vm_done, z_ready, z_ev, z_out, bounced, v_ready, v_done) = s.sems(
        *("w_in pj_ready stt_done added hi_done lo_done s_ready nm_ready exp_done t_done evd eva pv_done o_rs "
          "tab_in pad_done p0_done p0_tr p0_ev vm_done z_ready z_ev z_out bounced v_ready v_done").split())
    bounce = [[nc.dram_tensor(f"bounce{k}{m}", (2, P, KN), F32, kind="Internal").ap() for m in range(4)] for k in range(2)]
    stk = [s.sems(f"stk{k}0", f"stk{k}1") for k in range(2)]
    wb = lambda s_: (s_ + 1) // 2 % 2
    filled = lambda g2, s_: g2 * 2 * STK + STK * (s_ // 2 + 1)
    STK = 16 * 2 * 4
    PJ, O, SA, SC, TB = 0, 1, 2, 4, 5
    S_of = {3: 0, 2: 528, 1: 1024, 0: 1296}
    S = ps[:, SA:SC + 1, :].rearrange("p a n -> p (a n)")
    width = lambda qt: P * (qt + 1) + AV
    TBANK = [[(qt, 0) for qt in range(NT)], [(qt, 1) for qt in range(1, NT)], [(2, 2), (3, 2), (3, 3)]]
    AT = (0, 4, 7)
    KEYS = ((0, 4), (4, 7), (7, 9), (9, 10))

    def project(pe, s_, n, b):
        k = 8 * s_ + n
        if k >= 1:
            pe.wait_ge(stt_done, k)
        if s_ in (1, 3) and n == 0:
            pe.wait_ge(w_in, 24 * (s_ + 1))
        nc.tensor.matmul(ps[:, PJ, :], W[:, wb(s_), n % 4, :], xnT[:, b * N:(b + 1) * N], start=True, stop=True)\
            .then_inc(pj_ready, 1)

    def rotate_half(v, s_, n):
        k = 8 * s_ + n
        v.wait_ge(pj_ready, k + 1)
        if k >= 4:
            v.wait_ge(added, (k - 4) // 2 + 1)
        nc.vector.scalar_tensor_tensor(rot[:, n % 4, :], ps[:, PJ, :], bias[:, wb(s_), n % 4:n % 4 + 1], tab[:, n % 4, :],
                                       ALU.add, ALU.mult).then_inc(stt_done, 1)

    def add_pair(pool, s_, m):
        k = 4 * s_ + m
        pool.wait_ge(stt_done, 2 * k + 2)
        if k >= 2:
            pool.wait_ge(lo_done, k - 1)
        nc.gpsimd.tensor_tensor(full[:, m % 2, :], rot[:, 2 * (m % 2), :], rot[:, 2 * (m % 2) + 1, :],
                                ALU.add).then_inc(added, 1)

    def split_lo(pool, s_, m):
        k = 4 * s_ + m
        pool.wait_ge(hi_done, k + 1)
        hi, lo = ((qh, ql), (kh, kl))[m % 2]
        ins = nc.gpsimd.tensor_tensor(lo[:, m // 2, 0:N], full[:, m % 2, :], hi[:, m // 2, 0:N].bitcast(F32), ALU.subtract)
        if m % 2:
            ins = nc.gpsimd.tensor_tensor(kl[:, m // 2, N:KN], vk[:, wb(s_), :], kh[:, m // 2, N:KN].bitcast(F32), ALU.subtract)
        ins.then_inc(lo_done, 1)

    def split_hi(act, s_, m, n=None):
        k = 4 * s_ + m
        act.wait_ge(added, k + 1)
        if n is not None:
            act.wait_ge(stk[s_ % 2][m // 2], n)
        hi = (qh, kh)[m % 2]
        if m % 2:
            if s_ in (1, 3):
                act.wait_ge(w_in, 24 * (s_ + 1))
            nc.scalar.copy(kh[:, m // 2, N:KN], vk[:, wb(s_), :])
        nc.scalar.copy(hi[:, m // 2, 0:N], full[:, m % 2, :]).then_inc(hi_done, 1)

    def stack(sp, s_, m, buf):
        i, k = m // 2, 4 * s_ + m
        width_ = (N, KN)[m % 2]
        dst, halves = ((Qst, (qh, ql)), (Kst, (kh, kl)))[m % 2]
        for j, (src, made) in enumerate(zip(halves, (hi_done, lo_done))):
            sp.wait_ge(made, k + 1)
            sp.dma_start(bounce[s_ % 2][m][j, :, 0:width_], src[:, i].bitcast(F32)).then_inc(bounced, 16)
        sp.wait_ge(bounced, 32 * (k + 1))
        for block, j in enumerate(((0, 1, 0, 1), (0, 0, 1, 1))[m % 2]):
            sp.dma_start(dst[buf][32 * block:32 * block + 32, :, i].bitcast(F32),
                         bounce[s_ % 2][m][j, :, 0:width_].rearrange("(h c) n -> c h n", h=GH)).then_inc(stk[buf][i], 16)

    with nc.Block() as block:
        @block.sync
        def _(sp):
            sp.dma_start(tab[:], d["a_tab"]).then_inc(tab_in, 16)
            for m in range(4):
                stack(sp, 0, m, 0)

        @block.tensor
        def _(pe):
            for n in range(8):
                project(pe, 0, n, n // 4)
            for n in range(TT + B):
                if n >= 2:
                    pe.wait_ge(v_done, n - 1 if n - 2 < TT else TT + GH * (n - 1 - TT))
                if n < TT:
                    r = P - AV if n % NT == NT - 1 else P
                    nc.tensor.matmul(ps[0:r, 4 + n % 2, 0:AH * AR], xnT[:, P * n + AV:P * n + AV + r], wv[:],
                                     start=True, stop=True).then_inc(v_ready, 1)
                else:
                    lhs = x0[:, n - TT].rearrange("p h k -> p (h k)")
                    nc.tensor.matmul(ps[:, 4 + n % 2, 0:AH * AR], lhs, wv[:],
                                     start=True, stop=True).then_inc(v_ready, 1)

        @block.vector
        def _(v):
            v.wait_ge(tab_in, 16)
            for n in range(8):
                rotate_half(v, 0, n)
            for n in range(TT + B):
                v.wait_ge(v_ready, n + 1)
                if n < TT:
                    r = P - AV if n % NT == NT - 1 else P
                    nc.vector.tensor_tensor(V[0:r, n // NT, n % NT, :], ps[0:r, 4 + n % 2, 0:AH * AR], bv[0:r],
                                            ALU.add).then_inc(v_done, 1)
                else:
                    for h in range(GH):
                        r = slice(32 * h, 32 * h + 32)
                        own = slice(AR * h, AR * h + AR)
                        nc.vector.tensor_tensor(
                            V0[r, n - TT, :, own],
                            ps[r, 4 + n % 2, 0:AH * AR].rearrange("p (g c) -> p g c", g=AG)[:, :, own],
                            bv[r].rearrange("p (g c) -> p g c", g=AG)[:, :, own], ALU.add).then_inc(v_done, 1)

        @block.gpsimd
        def _(pool):
            for pad in (P0, Vm):
                nc.gpsimd.memset(pad[:], 0.0).then_inc(pad_done, 1)
            for m in range(4):
                add_pair(pool, 0, m)
                split_lo(pool, 0, m)
            pool.wait_ge(pad_done, 2)

        @block.scalar
        def _(act):
            for m in range(4):
                split_hi(act, 0, m)
    clear(nc, names)

    U = NB * GH
    GPI = 2
    STEPS = GPI * B // NB
    with nc.Fori(0, AG // GPI) as g2:
        group = lambda bb: g2 * GPI + bb // B
        with nc.Block() as block:
            @block.sync
            def _(sp):
                def store(bb):
                    b = bb % B
                    sp.wait_ge(z_ev, bb + 1)
                    if bb:
                        sp.wait_ge(z_out, 16 * bb)
                    sp.dma_start(zd[b, bass.ds(group(bb) * 32, 32), :], zs[32 * b:32 * b + 32, :]).then_inc(z_out, 16)

                def weights(k):
                    g = g2 * GPI + (0 if k else 1)
                    sp.dma_start(W[:, k], d["a_w"][bass.ds(g + 1, 1)].rearrange("g p c n -> p (g c) n")).then_inc(w_in, 16)
                    sp.dma_start(bias[:, k], d["a_b"][bass.ds(g + 1, 1)].rearrange("g p c -> p (g c)")).then_inc(w_in, 16)
                    sp.dma_start(vk[:, k], d["a_vk"][bass.ds(g + 1, 1)].rearrange("g p c -> p (g c)")).then_inc(w_in, 16)

                weights(1)
                sp.wait_ge(w_in, 48)
                for step in range(STEPS):
                    if step == 1:
                        weights(0)
                    for m in range(4):
                        if step:
                            sp.wait_ge(s_ready, 2 * GH * (NB * (step - 1) + m // 2 + 1))
                        stack(sp, step, m, (step + 1) % 2)
                        if m % 2 == 0 and 2 * step + m // 2 >= 1:
                            store(2 * step + m // 2 - 1)
                store(2 * STEPS - 1)
                sp.wait_ge(z_out, 16 * 2 * STEPS)
                sp.wait_ge(w_in, 96)

            @block.gpsimd
            def _(pool):
                def first_keys(u):
                    bb, h = u // GH, u % GH
                    pool.wait_ge(exp_done, 4 * u + 4)
                    if h == 0 and bb >= 2:
                        pool.wait_ge(p0_tr, bb - 1)
                    nc.gpsimd.tensor_copy(P0[:, bb % 2, :, 32 * h:32 * h + AV], Pm[:, u % 2, :, 0:AV]).then_inc(p0_done, 1)

                for k in range(STEPS * U):
                    if k % 2 == 1:
                        add_pair(pool, k // U, k % U // 2)
                    first_keys(k)
                    if k % 2 == 1:
                        split_lo(pool, k // U, k % U // 2)

            @block.tensor
            def _(pe):
                def scores(u, part):
                    q, k = Qst[u // U % 2], Kst[u // U % 2]
                    i, h = u % U // GH, u % GH
                    if h == 0 and part == 0:
                        pe.wait_ge(stk[u // U % 2][i], filled(g2, u // U))
                    if part == 0:
                        if u >= 1:
                            pe.wait_ge(exp_done, 4 * u - 2)
                        todo = [(1, [(0, 272)]), (0, [(0, 144)])]
                        last = 0
                    else:
                        if u >= 1:
                            pe.wait_ge(exp_done, 4 * u)
                        todo = [(3, [(0, 512), (512, 16)]), (2, [(0, 400)])]
                        last = 2
                    opened = set()
                    for qt, pieces in todo:
                        for at, w in pieces:
                            lo = S_of[qt] + at
                            nc.tensor.matmul(S[:, lo:lo + w], q[:, h, i, P * qt:P * qt + P], k[:, h, i, at:at + w],
                                             start=lo // 512 not in opened, stop=False)
                            opened.add(lo // 512)
                        edge = width(qt) - P
                        cuts = [(0, P)] if qt != 3 else [(0, 512 - edge), (512 - edge, P)]
                        for a, z in cuts:
                            lo = S_of[qt] + edge + a
                            end = (part == 0 and qt == 0) or (part == 1 and (qt == 2 or a == 0))
                            ins = nc.tensor.matmul(S[:, lo:lo + z - a], c["identb"][:], c["trib"][:, a:z],
                                                   start=False, stop=end)
                    ins.then_inc(s_ready, 1)

                def transposes(u):
                    pe.wait_ge(exp_done, 4 * u + 4)
                    for k in range(3):
                        if u >= 1:
                            if k != 1:
                                pe.wait_ge(eva, 2 * u - 1 + k // 2)
                            else:
                                pe.wait_ge(evd, u)
                        if k == 0 and u >= GH and u % GH == 0:
                            pe.wait_ge(p0_ev, u // GH)
                        for j, (qt, kt) in enumerate(TBANK[k]):
                            at = AV + P * kt
                            ins = nc.tensor.transpose(ps[:, TB + k, P * j:P * j + P], Pm[:, u % 2, qt, at:at + P],
                                                      c["ident"][:])
                        ins.then_inc(t_done, 1)

                def first_transposes(bb):
                    pe.wait_ge(p0_done, GH * (bb + 1))
                    pe.wait_ge(eva, 2 * GH * (bb + 1) - 1)
                    for qt in range(NT):
                        ins = nc.tensor.transpose(ps[:, TB, P * qt:P * qt + P], P0[:, bb % 2, qt, :], c["ident"][:])
                    ins.then_inc(p0_tr, 1)

                def values(u):
                    bb, h = u // GH, u % GH
                    out = ps[32 * (bb % B):32 * (bb % B) + 32, O, :]
                    pe.wait_ge(eva, 2 * u + 2)
                    pe.wait_ge(evd, u + 1)
                    if h == 0:
                        pe.wait_ge(vm_done, 2 * bb + 2)
                        if bb >= B:
                            pe.wait_ge(z_ev, bb - B + 1)
                    for kt in range(NT):
                        a, z = KEYS[kt]
                        ins = nc.tensor.matmul(out[:, P * kt:N], Vm[:, bb % 2, kt, 32 * h:32 * h + 32],
                                               PT[:, u % 2, a:z, :].rearrange("p j n -> p (j n)"),
                                               start=(h == 0 and kt == 0), stop=False)
                    ins.then_inc(pv_done, 1)
                    if h == GH - 1:
                        pe.wait_ge(p0_ev, bb + 1)
                        nc.tensor.matmul(out, V0m[:, bb % 2, :], P0T[:], start=False, stop=True).then_inc(z_ready, 1)

                for k in range(STEPS * U + 2):
                    if k < STEPS * U:
                        scores(k, 0)
                        step, n = k // U, k % U
                        project(pe, step, n, NB * ((step + 1) % 2) + n // 4)
                        scores(k, 1)
                    if 1 <= k <= STEPS * U:
                        transposes(k - 1)
                        if k % GH == 0:
                            first_transposes(k // GH - 1)
                    if k >= 2:
                        values(k - 2)

            @block.vector
            def _(v):
                def maxima(u):
                    for part, tiles in ((0, (1, 0)), (1, (3, 2))):
                        v.wait_ge(s_ready, 2 * u + part + 1)
                        for qt in tiles:
                            nc.vector.tensor_reduce(nm[:, u % 2, qt:qt + 1], S[:, S_of[qt]:S_of[qt] + width(qt)],
                                                    AX.X, ALU.max, negate=True).then_inc(nm_ready, 1)

                def evacuate(u):
                    v.wait_ge(t_done, 3 * u + 2)
                    if u >= 2:
                        v.wait_ge(pv_done, u - 1)
                    nc.vector.tensor_copy(PT[:, u % 2, 4:7, :].rearrange("p j n -> p (j n)"), ps[:, TB + 1, 0:3 * P])\
                        .then_inc(evd, 1)

                def first_evacuate(bb):
                    v.wait_ge(p0_tr, bb + 1)
                    if bb >= 1:
                        v.wait_ge(z_ready, bb)
                    nc.vector.tensor_copy(P0T[:], ps[:, TB, :]).then_inc(p0_ev, 1)

                def group_values(bb):
                    if bb >= 2:
                        v.wait_ge(z_ready, bb - 1)
                    nc.vector.tensor_copy(
                        Vm[:, bb % 2].rearrange("p t (h x) -> p t h x", h=GH)[:, :, :, 0:AR],
                        V[:, bb % B, :, bass.ds(group(bb) * (GH * AR), GH * AR)].rearrange("p t (h r) -> p t h r", h=GH)).then_inc(vm_done, 1)
                    nc.vector.tensor_copy(V0m[:, bb % 2, :], V0[:, bb % B, bass.ds(group(bb), 1), :].rearrange("p g c -> p (g c)"))\
                        .then_inc(vm_done, 1)

                def reciprocals(bb):
                    v.wait_ge(exp_done, 4 * GH * (bb + 1))
                    nc.vector.reciprocal(RS[:, NT * (bb % B):NT * (bb % B) + NT, bass.ds(group(bb) * GH, GH)], sums[:, bb % NB]).then_inc(o_rs, 1)

                def outputs(bb):
                    v.wait_ge(z_ready, bb + 1)
                    r = slice(32 * (bb % B), 32 * (bb % B) + 32)
                    if bb >= B:
                        v.wait_ge(z_out, 16 * (bb - B + 1))
                    nc.vector.tensor_copy(zs[r, :], ps[r, O, :]).then_inc(z_ev, 1)

                for k in range(STEPS * U + 3):
                    if k < STEPS * U:
                        maxima(k)
                        rotate_half(v, k // U, k % U)
                        if k % GH == 0:
                            group_values(k // GH)
                    if 1 <= k <= STEPS * U:
                        evacuate(k - 1)
                        if k % GH == 0:
                            reciprocals(k // GH - 1)
                            first_evacuate(k // GH - 1)
                    if k >= GH + 2 and (k - 2) % GH == 0:
                        outputs(k // GH - 1)

            @block.scalar
            def _(act):
                def exps(u):
                    i, h = u % U // GH, u % GH
                    if u >= 2:
                        act.wait_ge(t_done, 3 * (u - 1))
                        act.wait_ge(p0_done, u - 1)
                    if u >= U and h == 0:
                        act.wait_ge(o_rs, u // GH - NB + 1)
                    for part, tiles in ((0, (1, 0)), (1, (3, 2))):
                        act.wait_ge(nm_ready, 4 * u + 2 * part + 2)
                        for qt in tiles:
                            nc.scalar.activation(Pm[:, u % 2, qt, 0:width(qt)], S[:, S_of[qt]:S_of[qt] + width(qt)],
                                                 ACT.Exp, bias=nm[:, u % 2, qt:qt + 1],
                                                 accum_out=sums[:, i, qt, h:h + 1]).then_inc(exp_done, 1)

                def evacuate(u):
                    if u >= 2:
                        act.wait_ge(pv_done, u - 1)
                    for k, a, z in ((0, 0, 4), (2, 7, 10)):
                        act.wait_ge(t_done, 3 * u + k + 1)
                        nc.scalar.copy(PT[:, u % 2, a:z, :].rearrange("p j n -> p (j n)"), ps[:, TB + k, 0:P * (z - a)])\
                            .then_inc(eva, 1)

                for k in range(STEPS * U + 1):
                    if k < STEPS * U:
                        exps(k)
                    if k >= 1:
                        evacuate(k - 1)
                    if k % 2 == 1 and k < STEPS * U:
                        split_hi(act, k // U, k % U // 2, filled(g2, k // U))
        clear(nc, names)
    with nc.Block() as block:
        @block.sync
        def _(sp):
            for i in range(NB):
                sp.wait_ge(stk[0][i], STK * (AG + 1))
    clear(nc, [*names, *stk[0], *stk[1]])


def rope_tables():
    freq = (np.float32(10000.0) ** (np.arange(AD // 2, dtype=np.float32) / np.float32(AD / 2))).astype(np.float32)
    freq = np.concatenate([freq, freq])
    ang = (np.arange(N, dtype=np.float32)[:, None] / freq[None, :]).astype(np.float32)
    sign = np.where(np.arange(AD) < AD // 2, -1.0, 1.0)
    cos, sin = np.cos(ang).T, np.sin(ang).T * sign[:, None]
    q = AD ** -0.5
    t = np.stack([cos * q, sin * q, cos, sin], axis=1)
    return np.tile(t, (GH, 1, 1)).astype(np.float32)


def by_group(w):
    w = w.reshape(AG, GH, w.shape[1], w.shape[2]).transpose(0, 2, 1, 3)
    w = w.reshape(AG, w.shape[1], -1)
    return np.concatenate([w, w[:1]])


def swap(w):
    return np.roll(w, w.shape[-1] // 2, axis=-1)


def arrays_of(i):
    a = {"x": i["L0_attn_resid"]}
    wq, wk, bq, bk = i["L0_attn_W_Q"], i["L0_attn_W_K"], i["L0_attn_b_Q"], i["L0_attn_b_K"]
    a["a_w"] = np.stack([by_group(w) for w in (wq, swap(wq), wk, swap(wk))], axis=2)
    a["a_b"] = np.stack([by_group(b[:, None, :])[:, 0] for b in (bq, swap(bq), bk, swap(bk))], axis=2)
    a["a_vk"] = by_group(i["L0_attn_virtual_k"].transpose(1, 0, 2)).reshape(AG + 1, AV, P).transpose(0, 2, 1)
    a["a_vv"] = i["L0_attn_virtual_v"].reshape(AV, AH * AR)
    a["a_wv"] = i["L0_attn_W_V"].reshape(AH * AR, D).T
    a["a_bv"] = np.broadcast_to(i["L0_attn_b_V"].reshape(1, AH * AR), (P, AH * AR))
    a["a_wo"] = i["L0_attn_W_O"].reshape(2, P, D).transpose(1, 0, 2)
    a["a_sel"] = np.repeat(np.eye(AH, dtype=np.float32), AR, axis=1).reshape(AH, 2, P)
    a["a_tab"] = rope_tables()
    a["ident"] = np.eye(P, dtype=np.float32)
    kk = np.arange(P)
    a["tri"] = np.where(kk[None, :] > kk[:, None], BIG, 0.0).astype(np.float32)
    return a


def output_and_residual(nc, X, RS, zd, ps, c, d):
    with ExitStack() as ctx:
        s = Store(nc, ctx, "o")
        wo = s.sb("wo", [P, 2, D])
        sel = s.sb("sel", [AH, 2, P])
        z = s.sb("z", [P, B, 2, N])
        rsT = s.sb("rsT", [AH, 2, N])
        nrm = Norm(s, "on")
        names = w_in, z_in, r_tr, r_ev, r_ready, z_done, y_done, link_, pow_, var_ = s.sems(
            *"w_in z_in r_tr r_ev r_ready z_done y_done link pow var".split())
        with nc.Block() as block:
            @block.sync
            def _(sp):
                for b in range(B):
                    sp.dma_start(z[:, b], zd[b].rearrange("(j p) n -> p j n", p=P)).then_inc(z_in, 16)
                sp.dma_start(wo[:], d["a_wo"]).then_inc(w_in, 16)
                sp.dma_start(sel[:], d["a_sel"]).then_inc(w_in, 16)
                sp.wait_ge(w_in, 32)

            @block.tensor
            def _(pe):
                def spread(b):
                    if b >= 1:
                        pe.wait_ge(r_ev, b)
                    for t in range(NT):
                        ins = nc.tensor.transpose(ps[0:AH, 0, P * t:P * t + P], RS[:, NT * b + t, :], c["ident"][:])
                    ins.then_inc(r_tr, 1)
                    pe.wait_ge(r_ev, b + 1)
                    for j in range(2):
                        if b >= 1:
                            pe.wait_ge(z_done, 2 * b - 1 + j)
                        nc.tensor.matmul(ps[:, 1 + j, :], sel[:, j, :], rsT[:, b % 2, :], start=True, stop=True)\
                            .then_inc(r_ready, 1)

                pe.wait_ge(w_in, 32)
                spread(0)
                for b in range(B):
                    if b + 1 < B:
                        spread(b + 1)
                    pe.wait_ge(z_done, 2 * b + 2)
                    if b >= 2:
                        pe.wait_ge(var_, 2 * (b - 2) + 2)
                    for t in range(NT):
                        for j in range(2):
                            ins = nc.tensor.matmul(ps[:, 3 + b % 2, P * t:P * t + P], z[:, b, j, P * t:P * t + P], wo[:, j, :],
                                                   start=(j == 0), stop=(j == 1))
                    ins.then_inc(y_done, 1)

            @block.scalar
            def _(act):
                for b in range(B):
                    act.wait_ge(r_tr, b + 1)
                    if b >= 2:
                        act.wait_ge(r_ready, 2 * (b - 1))
                    nc.scalar.copy(rsT[:, b % 2, :], ps[0:AH, 0, :]).then_inc(r_ev, 1)

            @block.gpsimd
            def _(pool):
                for b in range(B):
                    pool.wait_ge(var_, 2 * b + 1)
                    nrm.power(nc, c).then_inc(pow_, 1)

            @block.vector
            def _(v):
                link = Chain(v, link_)
                v.wait_ge(z_in, 16 * B)

                def scale(b):
                    for j in range(2):
                        v.wait_ge(r_ready, 2 * b + j + 1)
                        nc.vector.tensor_tensor(z[:, b, j, :], z[:, b, j, :], ps[:, 1 + j, :], ALU.mult).then_inc(z_done, 1)

                scale(0)
                for b in range(B):
                    if b + 1 < B:
                        scale(b + 1)
                    v.wait_ge(y_done, b + 1)
                    y = ps[:, 3 + b % 2, :].rearrange("p (t n) -> p t n", n=D)
                    nrm.variance(nc, link, y, EPS).then_inc(var_, 1)
                    v.wait_ge(pow_, b + 1)
                    nrm.apply(nc, link, nrm.out, y)
                    nc.vector.tensor_tensor(X[:, NT * b:NT * b + NT, :], X[:, NT * b:NT * b + NT, :], nrm.out[:],
                                            ALU.add).then_inc(var_, 1)
                    v.wait_ge(var_, 2 * b + 2)
        clear(nc, names)


class Norm:

    def __init__(self, s, name):
        self.st = s.sb(name + "_st", [P, NT, 6])
        self.mv = s.sb(name + "_mv", [P, NT, 2])
        self.rstd = s.sb(name + "_rstd", [P, NT])
        self.out = s.sb(name + "_out", [P, NT, D])

    def variance(self, nc, link, x, eps):
        for t in range(NT):
            link.add(nc.vector.bn_stats(self.st[:, t, :], x[:, t, :]))
        link.wait()
        for t in range(NT):
            link.add(nc.vector.bn_aggr(self.mv[:, t, :], self.st[:, t, :]))
        link.wait()
        return nc.vector.tensor_scalar(self.mv[:, :, 1], self.mv[:, :, 1], eps, None, ALU.add)

    def power(self, nc, c):
        return nc.gpsimd.tensor_tensor(self.rstd[:], self.mv[:, :, 1], c["mhalf"][:, 0:NT], ALU.pow)

    def apply(self, nc, link, out, x):
        for t in range(NT):
            link.add(nc.vector.tensor_scalar(out[:, t, :], x[:, t, :], self.mv[:, t, 0:1], self.rstd[:, t:t + 1],
                                             ALU.subtract, ALU.mult))
        link.wait()


FL, FH, FD = 2, 8, 64
FI = FH * FD
FW = 64
HID = int(D * 4 * 2 / 3)
HC = [(0, P), (P, 2 * P), (2 * P, HID)]


def local_layers(nc, X, ps, c, d):
    with ExitStack() as ctx:
        s = Store(nc, ctx, "f")
        wqkv = s.sb("wqkv", [P, FL, 3 * FI])
        wo = s.sb("wo", [P, FL, 4, D])
        w1 = s.sb("w1", [P, FL, 2 * HID])
        w2 = s.sb("w2", [P, FL, 3, D])
        b1 = s.sb("b1", [P, FL, 2 * HID])
        b2 = s.sb("b2", [P, FL, D])
        lgb = s.sb("lgb", [P, FL, 2])
        tab = s.sb("tab", [P, FL, 2, 2, NT, FD])
        band = s.sb("band", [P, 2, 2 * P])
        hs = s.sb("hs", [P, NT, D])
        kz = s.sb("kz", [P, FH, N + P])
        with ExitStack() as ctx0:
            s0 = Store(nc, ctx0, "f0")
            base = s0.sb("base", [P, 2, 2, NT, FD])
            sc = s0.sb("sc", [P, FL, 2, 2, FD])
            names = w_in, sc_in, done = s0.sems("w_in", "sc_in", "done")
            with nc.Block() as block:
                @block.sync
                def _(sp):
                    for dst, src in ((base, "f_base"), (sc, "f_sc")):
                        sp.dma_start(dst[:], d[src]).then_inc(sc_in, 16)
                    for dst, src in ((wqkv, "f_wqkv"), (wo, "f_wo"), (w1, "f_w1"), (b1, "f_b1"), (b2, "f_b2"),
                                     (lgb, "f_lgb"), (band, "f_band")):
                        sp.dma_start(dst[:], d[src]).then_inc(w_in, 16)
                    for k, (a, z) in enumerate(HC):
                        sp.dma_start(w2[0:z - a, :, k, :], d["f_w2"][a:z]).then_inc(w_in, 16)
                    sp.wait_ge(w_in, 160)

                @block.gpsimd
                def _(pool):
                    nc.gpsimd.memset(kz[:], 0.0).then_inc(done, 1)
                    nc.gpsimd.memset(hs[:], 0.0).then_inc(done, 1)

                @block.vector
                def _(v):
                    v.wait_ge(sc_in, 32)
                    for l in range(FL):
                        for cs in range(2):
                            for t in range(NT):
                                nc.vector.tensor_tensor(tab[:, l, cs, :, t, :], base[:, cs, :, t, :], sc[:, l, cs, :, :],
                                                        ALU.mult).then_inc(done, 1)
                    v.wait_ge(done, 2 + FL * 2 * NT)
            clear(nc, names)
        xb = s.sb("xb", [P, NT, D])
        hT = s.sb("hT", [P, N])
        QK = s.sb("QK", [P, 2, 2 * FI])
        R1 = s.sb("R1", [P, 2, 2 * FI])
        R2 = s.sb("R2", [P, 2, 2 * FI])
        SQ = s.sb("SQ", [P, 2 * FI])
        ss = s.sb("ss", [P, 2, 2 * FH])
        rr = s.sb("rr", [P, 2, 2 * FH])
        Vb = s.sb("Vb", [P, NT, FI])
        qT = s.sb("qT", [P, 4, N])
        Sm = s.sb("Sm", [P, 2, 2, 2 * P])
        nb = s.sb("nb", [P, 2, 2])
        Pe = s.sb("Pe", [P, 2, 2, 2 * P])
        PT = s.sb("PT", [P, 2, 4, P])
        sums = s.sb("sums", [P, NT, FH])
        rs = s.sb("rs", [P, NT, FH])
        on = s.sb("on", [P, 2, FI])
        oT = s.sb("oT", [P, 2, 4, P])
        UG = s.sb("UG", [P, 2, HID])
        UA = s.sb("UA", [P, 2, HID])
        G = s.sb("G", [P, 2, HID])
        HT = s.sb("HT", [P, 2, 3, P])
        yb = s.sb("yb", [P, 2, D])
        nrm = Norm(s, "fn")
        names = (xb_ready, pe_zero, sh_copy, sh_dma, tr, hT_done, hn_done, qkv_ready, qk_ev, v_ev, sq_done, sq_used, cs_done, added, ss_done, rr_done,
                 rot_done, qkT_ready, qT_ev, kT_ev, s_ready, sm_done, exp_done, pt_ready, pt_ev, pv_done, on_done,
                 oT_ready, oT_ev, y_ready, y_used, up_ready, ug_done, gelu_done, ua_done, h_done, hT2_ready, hT2_ev,
                 y2_ready, y2_used, link_, var_, pow_) = s.sems(
            *("xb_ready pe_zero sh_copy sh_dma tr hT_done hn_done qkv_ready qk_ev v_ev sq_done sq_used cs_done added ss_done rr_done rot_done "
              "qkT_ready qT_ev kT_ev s_ready sm_done exp_done pt_ready pt_ev pv_done on_done oT_ready oT_ev y_ready "
              "y_used up_ready ug_done gelu_done ua_done h_done hT2_ready hT2_ev y2_ready y2_used link var pow").split())
        HP = FH // 2
        SEEN = slice(P - FW, 2 * P)
        UL = NT * HP
        qkv_bank = lambda T: 1 + 3 * (T % 2)
        shift_copies = lambda l, t=-1: (NT + 1) * l + 2 + t
        shift_transfers = lambda l, t=-1: 16 * ((2 * NT + 1) * l + 3 + 2 * t + (t < 0))
        with nc.Fori(0, B) as b:
            with nc.Block() as block:
                @block.sync
                def _(sp):
                    for l in range(FL):
                        sp.wait_ge(xb_ready, l + 1)
                        sp.dma_start(hs[1:P, :, FW:D], xb[0:P - 1, :, FW:D]).then_inc(sh_dma, 16)
                        sp.dma_start(hs[0:1, 1:NT, FW:D], xb[P - 1:P, 0:NT - 1, FW:D]).then_inc(sh_dma, 16)
                        sp.wait_ge(sh_dma, shift_transfers(l))
                        for t in range(NT):
                            sp.wait_ge(y_used, NT * l + t + 1)
                            sp.dma_start(hs[1:P, t, FW:D], xb[0:P - 1, t, FW:D]).then_inc(sh_dma, 16)
                            if t:
                                sp.dma_start(hs[0:1, t, FW:D], xb[P - 1:P, t - 1, FW:D]).then_inc(sh_dma, 16)
                            sp.wait_ge(sh_dma, shift_transfers(l, t))

                @block.gpsimd
                def _(pool):
                    pool.wait_ge(var_, 1)
                    nrm.power(nc, c).then_inc(pow_, 1)
                    nc.gpsimd.memset(Pe[:, :, :, 0:P - FW], 0.0).then_inc(pe_zero, 1)
                    for l in range(FL):
                        pool.wait_ge(xb_ready, l + 1)
                        nc.gpsimd.tensor_copy(hs[:, :, 0:FW], xb[:, :, 0:FW]).then_inc(sh_copy, 1)
                        for t in range(NT):
                            T = NT * l + t
                            pool.wait_ge(ss_done, T + 1)
                            if T >= 2:
                                pool.wait_ge(rot_done, T - 1)
                            nc.gpsimd.tensor_tensor(rr[:, T % 2, :], ss[:, T % 2, :], c["mhalf"][:, 0:2 * FH],
                                                    ALU.pow).then_inc(rr_done, 1)
                            if T % 2 == 0:
                                pool.wait_ge(cs_done, 6 * (T + 1))
                                nc.gpsimd.tensor_tensor(R1[:, T % 2], R1[:, T % 2], R2[:, T % 2], ALU.add).then_inc(added, 1)
                        for t in range(NT):
                            pool.wait_ge(y_used, NT * l + t + 1)
                            nc.gpsimd.tensor_copy(hs[:, t, 0:FW], xb[:, t, 0:FW]).then_inc(sh_copy, 1)
                            pool.wait_ge(var_, 2 + NT * l + t)
                            nc.gpsimd.tensor_tensor(nrm.rstd[:, t:t + 1], nrm.mv[:, t, 1:2], c["mhalf"][:, 0:1],
                                                    ALU.pow).then_inc(pow_, 1)
                    pool.wait_ge(var_, 2 + NT * FL)
                    nrm.power(nc, c).then_inc(pow_, 1)

                @block.scalar
                def _(act):
                    for l in range(FL):
                        act.wait_ge(tr, 2 * l + 1)
                        nc.scalar.copy(hT[:], ps[:, 0, :]).then_inc(hT_done, 1)
                        for t in range(NT + 2):
                            if t < NT:
                                T = NT * l + t
                                act.wait_ge(qkv_ready, T + 1)
                                if T >= 2:
                                    act.wait_ge(rot_done, T - 1)
                                k = qkv_bank(T)
                                nc.scalar.copy(QK[:, T % 2, :], ps[:, k:k + 2, :].rearrange("p a n -> p (a n)")).then_inc(qk_ev, 1)
                                if T >= 1:
                                    act.wait_ge(sq_used, T)
                                nc.scalar.activation(SQ[:], ps[:, k:k + 2, :].rearrange("p a n -> p (a n)"), ACT.Square)\
                                    .then_inc(sq_done, 1)
                                if l and t == 0:
                                    act.wait_ge(pv_done, UL * l)
                                nc.scalar.copy(Vb[:, t, :], ps[:, k + 2, :]).then_inc(v_ev, 1)
                            if t >= 2:
                                T = NT * l + t - 2
                                act.wait_ge(qkT_ready, T + 1)
                                nc.scalar.copy(qT[:, :, P * (t - 2):P * (t - 1)], ps[:, 7, :].rearrange("p (h n) -> p h n", n=P))\
                                    .then_inc(qT_ev, 1)
                                for z in range(2):
                                    r = slice(64 * z, 64 * z + 64)
                                    nc.scalar.copy(kz[r, z:FH:2, P * (t - 1):P * t],
                                                   ps[r, 0, :].rearrange("p (h n) -> p h n", n=P)).then_inc(kT_ev, 1)

                        def out_turn(t):
                            T = NT * l + t
                            act.wait_ge(oT_ready, T + 1)
                            if T >= 2:
                                act.wait_ge(y_ready, T - 1)
                            nc.scalar.copy(oT[:, T % 2].rearrange("p h n -> p (h n)"), ps[:, 0, :]).then_inc(oT_ev, 1)

                        for k in range(UL):
                            u = UL * l + k
                            t, hp = k // HP, k % HP
                            if u >= 2:
                                act.wait_ge(pt_ready, u - 1)
                            if l and k == 0:
                                act.wait_ge(on_done, NT * l)
                            for j in range(2):
                                act.wait_ge(sm_done, 2 * u + j + 1)
                                nc.scalar.activation(Pe[:, u % 2, j, SEEN], Sm[:, u % 2, j, SEEN], ACT.Exp, scale=-1.0,
                                                     bias=nb[:, u % 2, j:j + 1],
                                                     accum_out=sums[:, t, 2 * hp + j:2 * hp + j + 1]).then_inc(exp_done, 1)
                            if hp == 3 and t >= 1:
                                out_turn(t - 1)
                        out_turn(NT - 1)
                        act.wait_ge(tr, 2 * l + 2)
                        nc.scalar.activation(hT[:], ps[:, 0, :], ACT.Identity, scale=lgb[:, l, 0:1],
                                             bias=lgb[:, l, 1:2]).then_inc(hT_done, 1)
                        for t in range(NT + 1):
                            if t < NT:
                                T = NT * l + t
                                act.wait_ge(ug_done, T + 1)
                                if T >= 2:
                                    act.wait_ge(h_done, T - 1)
                                nc.scalar.activation(G[:, T % 2, :], UG[:, T % 2, :], ACT.Gelu).then_inc(gelu_done, 1)
                            if t >= 1:
                                T = NT * l + t - 1
                                act.wait_ge(hT2_ready, T + 1)
                                if T >= 2:
                                    act.wait_ge(y2_ready, T - 1)
                                for k, (a, z) in enumerate(HC):
                                    ins = nc.scalar.copy(HT[0:z - a, T % 2, k, :], ps[0:z - a, 5 + T % 2, P * k:P * k + P])
                                    ins.then_inc(hT2_ev, 1)

                @block.tensor
                def _(pe):
                    def turn(src, bank, n):
                        for j in range(n):
                            ins = nc.tensor.transpose(ps[:, bank, P * j:P * j + P], src(j), c["ident"][:])
                        return ins

                    for l in range(FL):
                        pe.wait_ge(sh_copy, shift_copies(l))
                        pe.wait_ge(sh_dma, shift_transfers(l))
                        turn(lambda j: hs[:, j, :], 0, NT).then_inc(tr, 1)
                        pe.wait_ge(hT_done, 2 * l + 1)
                        for t in range(NT + 2):
                            if t < NT:
                                T = NT * l + t
                                if T >= 2:
                                    pe.wait_ge(sq_done, T - 1)
                                    pe.wait_ge(v_ev, T - 1)
                                if l and t == 0:
                                    pe.wait_ge(y2_used, 2 * NT * l)
                                for j in range(3):
                                    ins = nc.tensor.matmul(ps[:, qkv_bank(T) + j, :], hT[:, P * t:P * t + P],
                                                           wqkv[:, l, FI * j:FI * j + FI], start=True, stop=True)
                                ins.then_inc(qkv_ready, 1)
                            if t >= 2:
                                T = NT * l + t - 2
                                pe.wait_ge(rot_done, T + 1)
                                if t >= 3:
                                    pe.wait_ge(qT_ev, T)
                                    pe.wait_ge(kT_ev, 2 * T)
                                turn(lambda j: R1[:, T % 2, P * j:P * j + P], 7, 4)
                                turn(lambda j: R1[:, T % 2, FI + P * j:FI + P * j + P], 0, 4).then_inc(qkT_ready, 1)

                        def scores(k):
                            u = UL * l + k
                            t, hp = k // HP, k % HP
                            if k == 0:
                                pe.wait_ge(qT_ev, NT * (l + 1))
                                pe.wait_ge(kT_ev, 2 * NT * (l + 1))
                                pe.wait_ge(v_ev, NT * (l + 1))
                            if u >= 2:
                                pe.wait_ge(sm_done, 2 * (u - 1))
                            for j in range(2):
                                ins = nc.tensor.matmul(ps[:, 1 + u % 2, 2 * P * j + P - FW:2 * P * j + 2 * P],
                                                       qT[:, hp, P * t:P * t + P], kz[:, 2 * hp + j, P * t + P - FW:P * t + 2 * P],
                                                       start=True, stop=True)
                            ins.then_inc(s_ready, 1)

                        def p_turn(k):
                            u = UL * l + k
                            pe.wait_ge(exp_done, 2 * u + 2)
                            if u == 0:
                                pe.wait_ge(pe_zero, 1)
                            if u >= 2:
                                pe.wait_ge(pt_ev, u - 1)
                            turn(lambda j: Pe[:, u % 2, j // 2, P * (j % 2):P * (j % 2) + P], 3 + u % 2, 4).then_inc(pt_ready, 1)

                        def values(k):
                            u = UL * l + k
                            t, hp = k // HP, k % HP
                            T = NT * l + t
                            pe.wait_ge(pt_ev, u + 1)
                            if hp == 0 and T >= 2:
                                pe.wait_ge(on_done, T - 1)
                            for j in range(2):
                                h = 2 * hp + j
                                kts = [0, 1] if t else [1]
                                for i in kts:
                                    ins = nc.tensor.matmul(ps[:, 5 + T % 2, FD * h:FD * h + FD], PT[:, u % 2, 2 * j + i, :],
                                                           Vb[:, t - 1 + i, FD * h:FD * h + FD], start=(i == kts[0]), stop=(i == 1))
                            ins.then_inc(pv_done, 1)

                        def out_turn(t):
                            T = NT * l + t
                            pe.wait_ge(on_done, T + 1)
                            if T >= 1:
                                pe.wait_ge(oT_ev, T)
                            turn(lambda j: on[:, T % 2, P * j:P * j + P], 0, 4).then_inc(oT_ready, 1)

                        def out_product(t):
                            T = NT * l + t
                            pe.wait_ge(oT_ev, T + 1)
                            if T >= 1 and t >= 1:
                                pe.wait_ge(y_used, T)
                            for j in range(4):
                                ins = nc.tensor.matmul(ps[:, 7, 0:D], oT[:, T % 2, j, :], wo[:, l, j, :],
                                                       start=(j == 0), stop=(j == 3))
                            ins.then_inc(y_ready, 1)

                        for k in range(UL + 2):
                            if k < UL:
                                scores(k)
                            if 1 <= k <= UL:
                                p_turn(k - 1)
                            if k >= 2:
                                values(k - 2)
                                if (k - 2) % HP == 1 and k - 2 > HP:
                                    out_turn((k - 2) // HP - 1)
                                if (k - 2) % HP == 2 and k - 2 > HP:
                                    out_product((k - 2) // HP - 1)
                        out_turn(NT - 1)
                        out_product(NT - 1)
                        pe.wait_ge(hn_done, NT * (l + 1))
                        turn(lambda j: nrm.out[:, j, :], 0, NT).then_inc(tr, 1)
                        pe.wait_ge(hT_done, 2 * l + 2)
                        for t in range(NT + 1):
                            if t < NT:
                                T = NT * l + t
                                if t >= 2:
                                    pe.wait_ge(ua_done, T - 1)
                                for j in range(2):
                                    ins = nc.tensor.matmul(ps[:, 1 + 2 * (T % 2) + j, 0:HID], hT[:, P * t:P * t + P],
                                                           w1[:, l, HID * j:HID * j + HID], start=True, stop=True)
                                ins.then_inc(up_ready, 1)
                            if t >= 1:
                                T = NT * l + t - 1
                                pe.wait_ge(h_done, T + 1)
                                if T >= 2:
                                    pe.wait_ge(hT2_ev, 3 * (T - 1))
                                for k, (a, z) in enumerate(HC):
                                    ins = nc.tensor.transpose(ps[0:z - a, 5 + T % 2, P * k:P * k + P], UA[:, T % 2, a:z],
                                                              c["ident"][:])
                                ins.then_inc(hT2_ready, 1)
                                pe.wait_ge(hT2_ev, 3 * (T + 1))
                                if T >= 1:
                                    pe.wait_ge(y2_used, 2 * T)
                                for k, (a, z) in enumerate(HC):
                                    ins = nc.tensor.matmul(ps[:, 7, 0:D], HT[0:z - a, T % 2, k, :], w2[0:z - a, l, k, :],
                                                           start=(k == 0), stop=(k == 2))
                                ins.then_inc(y2_ready, 1)

                @block.vector
                def _(v):
                    link = Chain(v, link_)
                    xs = X[:, bass.ds(b * NT, NT), :]

                    def norm(out, x, eps, n):
                        nrm.variance(nc, link, x, eps).then_inc(var_, 1)
                        v.wait_ge(pow_, n)
                        nrm.apply(nc, link, out, x)

                    norm(xb, xs, EPS, 1)
                    nc.vector.tensor_copy(yb[:, 0, 0:1], xb[:, 0, 0:1]).then_inc(xb_ready, 1)
                    for l in range(FL):
                        def square_sums(t):
                            T = NT * l + t
                            v.wait_ge(sq_done, T + 1)
                            nc.vector.tensor_reduce(ss[:, T % 2, :], SQ[:].rearrange("p (h e) -> p h e", e=FD),
                                                    AX.X, ALU.add).then_inc(sq_used, 1)
                            v.wait_ge(sq_used, T + 1)
                            nc.vector.tensor_scalar(ss[:, T % 2, :], ss[:, T % 2, :], 1e-24, None, ALU.max).then_inc(ss_done, 1)

                        def rotate(t):
                            T = NT * l + t
                            v.wait_ge(qk_ev, T + 1)
                            q4 = QK[:, T % 2].rearrange("p (k h e) -> p k h e", k=2, e=FD)
                            r4 = R1[:, T % 2].rearrange("p (k h e) -> p k h e", k=2, e=FD)
                            s4 = R2[:, T % 2].rearrange("p (k h e) -> p k h e", k=2, e=FD)
                            if T >= 2:
                                v.wait_ge(qkT_ready, T - 1)
                            for k in range(2):
                                cos = tab[:, l, 0, k, t, :].rearrange("p (h e) -> p h e", h=1).to_broadcast([P, FH, FD])
                                nc.vector.tensor_tensor(r4[:, k], q4[:, k], cos, ALU.mult).then_inc(cs_done, 1)
                                for z in range(2):
                                    e, f = slice(32 * z, 32 * z + 32), slice(32 - 32 * z, 64 - 32 * z)
                                    sin = tab[:, l, 1, k, t, e].rearrange("p (h e) -> p h e", h=1).to_broadcast([P, FH, FD // 2])
                                    nc.vector.tensor_tensor(s4[:, k, :, e], q4[:, k, :, f], sin, ALU.mult).then_inc(cs_done, 1)

                        def unit_length(t):
                            T = NT * l + t
                            if T % 2:
                                v.wait_ge(cs_done, 6 * (T + 1))
                                link.step(nc.vector.tensor_tensor(R1[:, T % 2], R1[:, T % 2], R2[:, T % 2], ALU.add))
                            else:
                                v.wait_ge(added, T // 2 + 1)
                            v.wait_ge(rr_done, T + 1)
                            r3 = R1[:, T % 2].rearrange("p (h e) -> p h e", e=FD)
                            nc.vector.tensor_tensor(
                                r3, r3, rr[:, T % 2, :].rearrange("p (h o) -> p h o", o=1).to_broadcast([P, 2 * FH, FD]),
                                ALU.mult).then_inc(rot_done, 1)

                        def mask(k):
                            u = UL * l + k
                            t = k // HP
                            v.wait_ge(s_ready, u + 1)
                            if u >= 2:
                                v.wait_ge(exp_done, 2 * (u - 1))
                            for j in range(2):
                                nc.vector.tensor_tensor_reduce(
                                    out=Sm[:, u % 2, j, SEEN], in0=ps[:, 1 + u % 2, 2 * P * j + P - FW:2 * P * j + 2 * P],
                                    in1=band[:, min(t, 1), SEEN], scale=-8.0, scalar=-8 * BIG, op0=ALU.add, op1=ALU.min,
                                    accum_out=nb[:, u % 2, j:j + 1]).then_inc(sm_done, 1)

                        def p_evac(k):
                            u = UL * l + k
                            v.wait_ge(pt_ready, u + 1)
                            if u >= 2:
                                v.wait_ge(pv_done, u - 1)
                            nc.vector.tensor_copy(PT[:, u % 2].rearrange("p j n -> p (j n)"), ps[:, 3 + u % 2, :]).then_inc(pt_ev, 1)

                        def divide(t):
                            T = NT * l + t
                            v.wait_ge(exp_done, 2 * (UL * l + HP * (t + 1)))
                            link.step(nc.vector.reciprocal(rs[:, t, :], sums[:, t, :]))
                            v.wait_ge(pv_done, UL * l + HP * (t + 1))
                            if T >= 2:
                                v.wait_ge(oT_ready, T - 1)
                            nc.vector.tensor_tensor(
                                on[:, T % 2].rearrange("p (h e) -> p h e", e=FD), ps[:, 5 + T % 2, :].rearrange("p (h e) -> p h e", e=FD),
                                rs[:, t, :].rearrange("p (h o) -> p h o", o=1).to_broadcast([P, FH, FD]), ALU.mult).then_inc(on_done, 1)

                        def attention_residual(t):
                            T = NT * l + t
                            v.wait_ge(y_ready, T + 1)
                            ins = nc.vector.tensor_tensor(xb[:, t, :], xb[:, t, :], ps[:, 7, 0:D], ALU.add)
                            ins.then_inc(y_used, 1)

                        def statistics(t):
                            v.wait_ge(sh_copy, shift_copies(l, t))
                            v.wait_ge(sh_dma, shift_transfers(l, t))
                            link.step(nc.vector.bn_stats(nrm.st[:, t, :], hs[:, t, :]))
                            link.step(nc.vector.bn_aggr(nrm.mv[:, t, :], nrm.st[:, t, :]))
                            nc.vector.tensor_scalar(nrm.mv[:, t, 1:2], nrm.mv[:, t, 1:2], EPS, None, ALU.add).then_inc(var_, 1)

                        def normalise(t):
                            v.wait_ge(pow_, 2 + NT * l + t)
                            nc.vector.tensor_scalar(nrm.out[:, t, :], hs[:, t, :], nrm.mv[:, t, 0:1], nrm.rstd[:, t:t + 1],
                                                    ALU.subtract, ALU.mult).then_inc(hn_done, 1)

                        for t in range(NT + 1):
                            if t < NT:
                                square_sums(t)
                                rotate(t)
                            if t >= 1:
                                unit_length(t - 1)
                        for k in range(UL + 5):
                            if k < UL:
                                mask(k)
                            if 1 <= k <= UL:
                                p_evac(k - 1)
                            if 3 <= k < UL + 3 and (k - 3) % HP == HP - 1:
                                divide((k - 3) // HP)
                            if k >= 5 + HP and (k - 5) % HP == 0:
                                attention_residual((k - 5) // HP - 1)
                            if k >= 7 + HP and (k - 7) % HP == 0:
                                statistics((k - 7) // HP - 1)
                            if k >= 8 + HP and (k - 8) % HP == 0:
                                normalise((k - 8) // HP - 1)
                        attention_residual(NT - 1)
                        statistics(NT - 1)
                        normalise(NT - 1)
                        for t in range(NT + 1):
                            if t < NT:
                                T = NT * l + t
                                k = 1 + 2 * (T % 2)
                                v.wait_ge(up_ready, T + 1)
                                if T >= 2:
                                    v.wait_ge(gelu_done, T - 1)
                                nc.vector.tensor_tensor(UG[:, T % 2, :], ps[:, k + 1, 0:HID], b1[:, l, HID:2 * HID],
                                                        ALU.add).then_inc(ug_done, 1)
                                if T >= 2:
                                    v.wait_ge(hT2_ready, T - 1)
                                nc.vector.tensor_tensor(UA[:, T % 2, :], ps[:, k, 0:HID], b1[:, l, 0:HID],
                                                        ALU.add).then_inc(ua_done, 1)
                                v.wait_ge(ua_done, T + 1)
                                v.wait_ge(gelu_done, T + 1)
                                nc.vector.tensor_tensor(UA[:, T % 2, :], UA[:, T % 2, :], G[:, T % 2, :], ALU.mult).then_inc(h_done, 1)
                            if t >= 1:
                                T = NT * l + t - 1
                                v.wait_ge(y2_ready, T + 1)
                                if T >= 2:
                                    v.wait_ge(y2_used, 2 * (T - 1))
                                nc.vector.tensor_tensor(yb[:, T % 2, :], ps[:, 7, 0:D], b2[:, l, :], ALU.add).then_inc(y2_used, 1)
                                v.wait_ge(y2_used, 2 * T + 1)
                                nc.vector.tensor_tensor(xb[:, t - 1, :], xb[:, t - 1, :], yb[:, T % 2, :], ALU.add).then_inc(y2_used, 1)
                        v.wait_ge(y2_used, 2 * NT * (l + 1))
                        if l + 1 < FL:
                            nc.vector.tensor_copy(yb[:, 0, 0:1], xb[:, 0, 0:1]).then_inc(xb_ready, 1)
                            v.wait_ge(xb_ready, l + 2)
                    norm(nrm.out, xb, EPS, 2 + NT * FL)
                    link.step(nc.vector.tensor_tensor(xs, xs, nrm.out[:], ALU.add))
            clear(nc, names)


def xpos_tables():
    half = np.arange(0, FD, 2, dtype=np.float32)
    inv = (1.0 / 10000.0 ** (half / FD)).astype(np.float32)
    t = np.arange(N, dtype=np.float32)
    fr = (t[:, None] * inv[None, :]).astype(np.float32)
    fr = np.concatenate([fr, fr], axis=-1)
    base = ((half + 0.4 * FD) / (1.4 * FD)).astype(np.float32)
    power = ((t - N // 2) / float(FW // 2)).astype(np.float32)
    scale = (base[None, :] ** power[:, None]).astype(np.float32)
    scale = np.concatenate([scale, scale], axis=-1)
    sign = np.where(np.arange(FD) < FD // 2, -1.0, 1.0)
    cos, sin = np.cos(fr), np.sin(fr) * sign
    a = np.stack([np.stack([cos * scale, cos / scale]), np.stack([sin * scale, sin / scale])])
    return a.reshape(2, 2, NT, P, FD).transpose(3, 0, 1, 2, 4).astype(np.float32)


def band_masks():
    q, k = np.arange(P)[:, None], np.arange(2 * P)[None, :]
    ok = (k <= q + P) & (k >= q + P - FW)
    return np.stack([np.where(ok & (k >= P), 0.0, BIG), np.where(ok, 0.0, BIG)], axis=1).astype(np.float32)


def rows(v):
    return np.broadcast_to(v[None], (P,) + v.shape)


def arrays_of_layers(i):
    qs, ks = i["L0_ffn_q_scale"], i["L0_ffn_k_scale"]
    return {
        "f_wqkv": i["L0_ffn_wqkv"].transpose(1, 0, 2),
        "f_wo": i["L0_ffn_wo"].reshape(FL, 4, P, D).transpose(2, 0, 1, 3),
        "f_w1": i["L0_ffn_w1"].transpose(1, 0, 2),
        "f_w2": i["L0_ffn_w2"].transpose(1, 0, 2),
        "f_b1": rows(i["L0_ffn_b1"]),
        "f_b2": rows(i["L0_ffn_b2"]),
        "f_lgb": np.stack([i["L0_ffn_ln_g"], i["L0_ffn_ln_b"]], axis=-1).transpose(1, 0, 2),
        "f_sc": rows(np.stack([np.stack([qs, ks], 1), np.stack([swap(qs), swap(ks)], 1)], 1)),
        "f_base": xpos_tables(),
        "f_band": band_masks(),
    }


RH, RD = 16, 8
RG = 4
RW = 2 * N
BW = N + P
MAX_LEN = 625


def relative_attention(nc, X, ps, c, d):
    with ExitStack() as ctx:
        s = Store(nc, ctx, "r")
        Qu = s.sb("Qu", [P, RG, B * N], F32R)
        Qv = s.sb("Qv", [P, RG, B * N], F32R)
        Kst = s.sb("Kst", [P, RG, B * N], F32R)
        Rst = s.sb("Rst", [P, RG, RW], F32R)
        V = s.sb("V", [P, B, NT, P])
        wo = s.sb("wo", [P, D])
        bo = s.sb("bo", [P, D])
        hm = s.sb("hm", [P, RG])
        sel = s.sb("sel", [RH, P])
        with ExitStack() as ctx0:
            make_stacks(nc, Store(nc, ctx0, "r0"), X, ps, c, d, Qu, Qv, Kst, Rst, V, wo, bo, hm, sel)
        relative_heads(nc, s, X, ps, c, d, Qu, Qv, Kst, Rst, V, wo, bo, hm, sel)


def make_stacks(nc, s, X, ps, c, d, Qu, Qv, Kst, Rst, V, wo, bo, hm, sel):
    w = s.sb("w", [P, 4, P])
    gb = s.sb("gb", [P, 2])
    uv = s.sb("uv", [P, 2])
    emb = s.sb("emb", [P, RW])
    xT = s.sb("xT", [P, N])
    full = s.sb("full", [P, 3, N])
    hi = s.sb("hi", [P, 3, B * N], F32R)
    lo = s.sb("lo", [P, 3, B * N], F32R)
    rhi = s.sb("rhi", [P, RW], F32R)
    rlo = s.sb("rlo", [P, RW], F32R)
    n1, n2 = Norm(s, "n1"), Norm(s, "n2")
    names = (w_in, r_ready, rhi_done, rlo_done, norm_done, tr, xT_done, p_ready, full_done, v_ev, hi_done, lo_done,
             bounced, stacked, link_, var_, pow_) = s.sems(
        *"w_in r_ready rhi_done rlo_done norm_done tr xT_done p_ready full_done v_ev hi_done lo_done bounced stacked link var pow".split())
    QKR = 3
    r_bounce = nc.dram_tensor("r_bounce", (2, P, RW), F32, kind="Internal").ap()
    bounce = nc.dram_tensor("qk_bounce", (QKR, 2, P, B * N), F32, kind="Internal").ap()
    bank = lambda b: 4 * (b % 2)

    with nc.Block() as block:
        @block.sync
        def _(sp):
            sent = 0

            def stack(dst, there, halves, made, blocks, at):
                nonlocal sent
                for k, (src, (sem, n)) in enumerate(zip(halves, made)):
                    sp.wait_ge(sem, n)
                    sp.dma_start(there[k, :, at], src.bitcast(F32)).then_inc(bounced, 16)
                sent += 32
                sp.wait_ge(bounced, sent)
                for k, half in enumerate(blocks):
                    sp.dma_start(dst[32 * k:32 * k + 32, :, at].bitcast(F32),
                                 there[half, :, at].rearrange("(g c) n -> c g n", g=RG)).then_inc(stacked, 16)

            for dst, src in ((w, "r_w"), (gb, "r_gb"), (uv, "r_uv"), (emb, "r_emb"), (wo, "r_wo"), (bo, "r_bo"), (hm, "r_hm"),
                             (sel, "r_sel")):
                sp.dma_start(dst[:], d[src]).then_inc(w_in, 16)
            stack(Rst, r_bounce, (rhi[:], rlo[:]), ((rhi_done, 1), (rlo_done, 2)), (0, 0, 1, 1), slice(0, RW))
            for b in range(B):
                at = slice(b * N, b * N + N)
                for j, (dst, blocks) in enumerate(((Qu, (0, 1, 0, 1)), (Qv, (0, 1, 0, 1)), (Kst, (0, 0, 1, 1)))):
                    n = QKR * b + j + 1
                    stack(dst, bounce[j], (hi[:, j, at], lo[:, j, at]), ((hi_done, n), (lo_done, n)), blocks, at)
            sp.wait_ge(stacked, 16 * 4 * (1 + QKR * B))

        @block.gpsimd
        def _(pool):
            for k in range(2 * B):
                pool.wait_ge(var_, k + 1)
                (n1, n2)[k % 2].power(nc, c).then_inc(pow_, 1)

        @block.tensor
        def _(pe):
            pe.wait_ge(w_in, 128)
            for k in range(2):
                ins = nc.tensor.matmul(ps[:, 6 + k, :], w[:, 3, :], emb[:, N * k:N * k + N], start=True, stop=True)
            ins.then_inc(r_ready, 1)
            for b in range(B):
                pe.wait_ge(norm_done, NT * (b + 1))
                if b == 1:
                    pe.wait_ge(rlo_done, 2)
                if b >= 2:
                    pe.wait_ge(full_done, QKR * (b - 1))
                    pe.wait_ge(v_ev, b - 1)
                for t in range(NT):
                    ins = nc.tensor.transpose(ps[:, bank(b), P * t:P * t + P], n2.out[:, t, :], c["ident"][:])
                ins.then_inc(tr, 1)
                pe.wait_ge(xT_done, b + 1)
                for j in range(2):
                    nc.tensor.matmul(ps[:, bank(b) + 1 + j, :], w[:, j, :], xT[:], start=True, stop=True).then_inc(p_ready, 1)
                for t in range(NT):
                    ins = nc.tensor.matmul(ps[:, bank(b) + 3, P * t:P * t + P], xT[:, P * t:P * t + P], w[:, 2, :],
                                           start=True, stop=True)
                ins.then_inc(p_ready, 1)

        @block.scalar
        def _(act):
            act.wait_ge(r_ready, 1)
            nc.scalar.copy(rhi[:], ps[:, 6:8, :].rearrange("p a n -> p (a n)")).then_inc(rhi_done, 1)
            for b in range(B):
                act.wait_ge(tr, b + 1)
                if b >= 1:
                    act.wait_ge(p_ready, 3 * b)
                nc.scalar.activation(xT[:], ps[:, bank(b), :], ACT.Identity, scale=gb[:, 0:1], bias=gb[:, 1:2])\
                    .then_inc(xT_done, 1)
                act.wait_ge(p_ready, 3 * b + 3)
                nc.scalar.copy(V[:, b].rearrange("p t n -> p (t n)"), ps[:, bank(b) + 3, :]).then_inc(v_ev, 1)
                for j in range(QKR):
                    act.wait_ge(full_done, QKR * b + j + 1)
                    nc.scalar.copy(hi[:, j, b * N:b * N + N], full[:, j, :]).then_inc(hi_done, 1)

        @block.vector
        def _(v):
            link = Chain(v, link_)

            def norms(b):
                xs = X[:, b * NT:b * NT + NT, :]
                n1.variance(nc, link, xs, EPS).then_inc(var_, 1)
                v.wait_ge(pow_, 2 * b + 1)
                n1.apply(nc, link, n1.out, xs)
                n2.variance(nc, link, n1.out, 1e-6).then_inc(var_, 1)
                v.wait_ge(pow_, 2 * b + 2)
                if b >= 1:
                    v.wait_ge(tr, b)
                for t in range(NT):
                    nc.vector.tensor_scalar(n2.out[:, t, :], n1.out[:, t, :], n2.mv[:, t, 0:1], n2.rstd[:, t:t + 1],
                                            ALU.subtract, ALU.mult).then_inc(norm_done, 1)

            norms(0)
            v.wait_ge(rhi_done, 1)
            for k in range(2):
                nc.vector.tensor_tensor(rlo[:, N * k:N * k + N], ps[:, 6 + k, :], rhi[:, N * k:N * k + N].bitcast(F32),
                                        ALU.subtract).then_inc(rlo_done, 1)
            for b in range(B):
                if b + 1 < B:
                    norms(b + 1)
                if b >= 1:
                    v.wait_ge(lo_done, QKR * b)
                v.wait_ge(p_ready, 3 * b + 1)
                for j in range(2):
                    nc.vector.tensor_scalar(full[:, j, :], ps[:, bank(b) + 1, :], uv[:, j:j + 1], None, ALU.add)\
                        .then_inc(full_done, 1)
                v.wait_ge(p_ready, 3 * b + 2)
                nc.vector.tensor_copy(full[:, 2, :], ps[:, bank(b) + 2, :]).then_inc(full_done, 1)
                for j in range(QKR):
                    v.wait_ge(full_done, QKR * b + j + 1)
                    v.wait_ge(hi_done, QKR * b + j + 1)
                    nc.vector.tensor_tensor(lo[:, j, b * N:b * N + N], full[:, j, :], hi[:, j, b * N:b * N + N].bitcast(F32),
                                            ALU.subtract).then_inc(lo_done, 1)
    clear(nc, names)


def relative_heads(nc, s, X, ps, c, d, Qu, Qv, Kst, Rst, V, wo, bo, hm, sel):
    STEPS = RH * NT
    PAIRS = STEPS // 2
    BUFS, SCRATCH = 3, 5
    LAG = 8
    spill = [nc.dram_tensor(f"spill{k}", (2, P, BW), F32, kind="Internal").ap() for k in range(SCRATCH)]
    qu = s.sb("qu", [P, 2, N], F32R)
    qv = s.sb("qv", [P, 2, N], F32R)
    BD = s.sb("BD", [P, BUFS, 2, BW])
    Sx = s.sb("Sx", [P, SCRATCH, 2, N])
    PT = s.sb("PT", [P, 2, NT, N])
    Vm = s.sb("Vm", [P, NT, RG, P])
    nb = s.sb("nb", [P, 2, NT])
    sums = s.sb("sums", [P, NT, RH])
    rs = s.sb("rs", [P, NT, RH])
    rsT = s.sb("rsT", [RH, N])
    oT = s.sb("oT", [P, N])
    yb = s.sb("yb", [P, NT, D])
    nrm = Norm(s, "n")
    names = (qv_done, qu_done, bd_ready, bd_ev, wr0, wr1, wr2, rd0, rd1, rd2, rd3, rd4, ac_ready, sx_done, exp_done, t_ready,
             t_ev, pv_done, rs_done, on_done, zeroed, vm_done, rs_tr, rs_ev, rs_ready, o_ev, y_ready, y_done, link_, var_, pow_) = s.sems(
        *("qv_done qu_done bd_ready bd_ev wr0 wr1 wr2 rd0 rd1 rd2 rd3 rd4 ac_ready sx_done exp_done t_ready t_ev pv_done rs_done "
          "on_done zeroed vm_done rs_tr rs_ev rs_ready o_ev y_ready y_done link var pow").split())
    wr, rd = (wr0, wr1, wr2), (rd0, rd1, rd2, rd3, rd4)
    assert len(rd) == SCRATCH and len(wr) == BUFS
    BDB = (0, 1, 7)
    HW = BW // 2
    SCALE = RD ** -0.5
    with nc.Fori(0, B) as b:
        with nc.Block() as block:
            @block.sync
            def _(sp):
                for k in range(PAIRS + 1):
                    if k < PAIRS:
                        sp.wait_ge(bd_ev, 4 * (k + 1))
                        if k >= SCRATCH:
                            sp.wait_ge(rd[k % SCRATCH], 16 * (k // SCRATCH))
                        sp.dma_start(spill[k % SCRATCH].rearrange("t p n -> p t n"), BD[:, k % BUFS])\
                            .then_inc(wr[k % BUFS], 16)
                    if k >= 1:
                        m = k - 1
                        sp.wait_ge(wr[m % BUFS], 16 * (m // BUFS + 1))
                        if m >= SCRATCH:
                            sp.wait_ge(t_ready, 2 * (m - SCRATCH + 1))
                        a = spill[m % SCRATCH]
                        skew = bass.AP(tensor=a.tensor, offset=P - 1, ap=[[BW - 1, P], [P * BW, 2], [1, N]])
                        sp.dma_start(Sx[:, m % SCRATCH], skew).then_inc(rd[m % SCRATCH], 16)
                for k in range(SCRATCH):
                    sp.wait_ge(rd[k], 16 * len(range(k, PAIRS, SCRATCH)))

            @block.gpsimd
            def _(pool):
                nc.gpsimd.memset(Vm[:], 0.0).then_inc(zeroed, 1)
                pool.wait_ge(var_, 1)
                nrm.power(nc, c).then_inc(pow_, 1)

            @block.tensor
            def _(pe):
                def relative(n):
                    h, lt = n // NT, n % NT
                    pe.wait_ge(qv_done, h + 1)
                    for j in range(2):
                        m = 2 * n + j
                        if m >= 3:
                            pe.wait_ge(bd_ev, m - 2)
                        r0 = N - P - P * lt + HW * j
                        nc.tensor.matmul(ps[:, BDB[m % 3], 0:HW], qv[:, h % 2, P * lt:P * lt + P],
                                         Rst[:, h // RG, r0:r0 + HW], start=True, stop=True).then_inc(bd_ready, 1)

                def content(n):
                    h, lt = n // NT, n % NT
                    pe.wait_ge(qu_done, h + 1)
                    if n >= 2:
                        pe.wait_ge(sx_done, n - 1)
                    nc.tensor.matmul(ps[:, 2 + n % 2, :], qu[:, h % 2, P * lt:P * lt + P], Kst[:, h // RG, bass.ds(b * N, N)],
                                     start=True, stop=True).then_inc(ac_ready, 1)

                def turn(n):
                    pe.wait_ge(exp_done, n + 1)
                    if n >= 2:
                        pe.wait_ge(t_ev, n - 1)
                    for j in range(NT):
                        ins = nc.tensor.transpose(ps[:, 4 + n % 2, P * j:P * j + P],
                                                  Sx[:, n // 2 % SCRATCH, n % 2, P * j:P * j + P], c["ident"][:])
                    ins.then_inc(t_ready, 1)

                def values(n):
                    h, kt = n // NT, n % NT
                    if kt == 0:
                        pe.wait_ge(t_ev, NT * (h + 1))
                    if n == 0:
                        pe.wait_ge(vm_done, RG)
                    r = 32 * (h // RG)
                    nc.tensor.matmul(ps[r:r + 32, 6, :], Vm[:, kt, h // RG, 32 * (h % RG):32 * (h % RG) + 32],
                                     PT[:, h % 2, kt, :], start=(h % RG == 0 and kt == 0),
                                     stop=(h % RG == RG - 1 and kt == NT - 1)).then_inc(pv_done, 1)

                for k in range(STEPS + LAG + 6):
                    if k < STEPS:
                        relative(k)
                    for part, late in ((content, LAG), (turn, LAG + 2), (values, LAG + 6)):
                        if 0 <= k - late < STEPS:
                            part(k - late)
                pe.wait_ge(rs_done, 1)
                for t in range(NT):
                    ins = nc.tensor.transpose(ps[0:RH, 0, P * t:P * t + P], rs[:, t, :], c["ident"][:])
                ins.then_inc(rs_tr, 1)
                pe.wait_ge(rs_ev, 1)
                nc.tensor.matmul(ps[:, 1, :], sel[:], rsT[:], start=True, stop=True).then_inc(rs_ready, 1)
                pe.wait_ge(on_done, 1)
                for t in range(NT):
                    ins = nc.tensor.matmul(ps[:, 0, P * t:P * t + P], oT[:, P * t:P * t + P], wo[:], start=True, stop=True)
                ins.then_inc(y_ready, 1)

            @block.scalar
            def _(act):
                def relative(n):
                    if n % 2 == 0 and n // 2 >= BUFS:
                        act.wait_ge(wr[n // 2 % BUFS], 16 * (n // 2 // BUFS))
                    for j in range(2):
                        m = 2 * n + j
                        act.wait_ge(bd_ready, m + 1)
                        nc.scalar.copy(BD[:, n // 2 % BUFS, n % 2, HW * j:HW * j + HW], ps[:, BDB[m % 3], 0:HW])\
                            .then_inc(bd_ev, 1)

                def exps(n):
                    h, lt = n // NT, n % NT
                    act.wait_ge(sx_done, n + 1)
                    row = Sx[:, n // 2 % SCRATCH, n % 2, :]
                    nc.scalar.activation(row, row, ACT.Exp, scale=-1.0, bias=nb[:, h % 2, lt:lt + 1],
                                         accum_out=sums[:, lt, h:h + 1]).then_inc(exp_done, 1)

                act.wait_ge(zeroed, 1)
                for k in range(STEPS + LAG):
                    if k < STEPS:
                        relative(k)
                    if 1 <= k <= RG:
                        r = k - 1
                        nc.scalar.copy(Vm[:, :, :, 40 * r:40 * r + RD],
                                       V[:, bass.ds(b, 1)].rearrange("p b t (g e) -> p (b t) g e", g=RG)
                                       [:, :, :, RD * r:RD * r + RD]).then_inc(vm_done, 1)
                    if k >= LAG:
                        exps(k - LAG)
                act.wait_ge(rs_tr, 1)
                nc.scalar.copy(rsT[:], ps[0:RH, 0, :]).then_inc(rs_ev, 1)
                act.wait_ge(pv_done, STEPS)
                nc.scalar.copy(oT[:], ps[:, 6, :]).then_inc(o_ev, 1)

            @block.vector
            def _(v):
                def mask(dst, src, h, done, free, per):
                    if h >= 2:
                        v.wait_ge(free, per * (h - 1))
                    nc.vector.tensor_scalar(dst[:, h % 2, :], src[:, h // RG, bass.ds(b * N, N)].bitcast(F32),
                                            hm[:, h % RG:h % RG + 1], None, ALU.mult).then_inc(done, 1)

                def add(n):
                    h, lt, m = n // NT, n % NT, n // 2
                    v.wait_ge(ac_ready, n + 1)
                    v.wait_ge(rd[m % SCRATCH], 16 * (m // SCRATCH + 1))
                    if n >= 2 * NT:
                        v.wait_ge(exp_done, n - 2 * NT + 1)
                    row = Sx[:, m % SCRATCH, n % 2, :]
                    nc.vector.tensor_tensor_reduce(
                        out=row, in0=ps[:, 2 + n % 2, :], in1=row, scale=-SCALE,
                        scalar=-BIG, op0=ALU.add, op1=ALU.min, accum_out=nb[:, h % 2, lt:lt + 1]).then_inc(sx_done, 1)

                def evacuate(n):
                    v.wait_ge(t_ready, n + 1)
                    h, lt = n // NT, n % NT
                    if h >= 2:
                        v.wait_ge(pv_done, NT * (h - 1))
                    nc.vector.tensor_copy(PT[:, h % 2, :, P * lt:P * lt + P],
                                          ps[:, 4 + n % 2, :].rearrange("p (j n) -> p j n", j=NT)).then_inc(t_ev, 1)

                for k in range(STEPS + LAG + 2):
                    if k % NT == 0 and k // NT < RH:
                        mask(qv, Qv, k // NT, qv_done, bd_ready, 2 * NT)
                    if k >= LAG - 2 and (k - LAG + 2) % NT == 0 and (k - LAG + 2) // NT < RH:
                        mask(qu, Qu, (k - LAG + 2) // NT, qu_done, ac_ready, NT)
                    if 0 <= k - LAG < STEPS:
                        add(k - LAG)
                    if 0 <= k - LAG - 2 < STEPS:
                        evacuate(k - LAG - 2)
                link = Chain(v, link_)
                v.wait_ge(exp_done, NT * RH)
                nc.vector.reciprocal(rs[:], sums[:]).then_inc(rs_done, 1)
                v.wait_ge(rs_ready, 1)
                v.wait_ge(o_ev, 1)
                nc.vector.tensor_tensor(oT[:], oT[:], ps[:, 1, :], ALU.mult).then_inc(on_done, 1)
                v.wait_ge(y_ready, 1)
                for t in range(NT):
                    link.add(nc.vector.tensor_tensor(yb[:, t, :], ps[:, 0, P * t:P * t + P], bo[:], ALU.add))
                link.wait()
                nrm.variance(nc, link, yb, EPS).then_inc(var_, 1)
                v.wait_ge(pow_, 1)
                nrm.apply(nc, link, nrm.out, yb)
                xs = X[:, bass.ds(b * NT, NT), :]
                link.step(nc.vector.tensor_tensor(xs, xs, nrm.out[:], ALU.add))
        clear(nc, names)


GHID = 384
GC = GHID // P
QSCALE = 1.0 / 127.0


def gated_feed_forward(nc, X, ps, c, d):
    with ExitStack() as ctx:
        s = Store(nc, ctx, "g")
        wgu = s.sb("wgu", [P, 2, GHID])
        wd = s.sb("wd", [P, GC, D])
        with ExitStack() as ctx0:
            s0 = Store(nc, ctx0, "g0")
            gui = s0.sb("gui", [P, 2, GHID], I32)
            di = s0.sb("di", [P, GC, D], I32)
            names = w_in, done = s0.sems("w_in", "done")
            with nc.Block() as block:
                @block.sync
                def _(sp):
                    sp.dma_start(gui[:], d["g_wgu"]).then_inc(w_in, 16)
                    sp.dma_start(di[:], d["g_wd"]).then_inc(w_in, 16)

                @block.vector
                def _(v):
                    v.wait_ge(w_in, 32)
                    nc.vector.tensor_scalar(wgu[:], gui[:], QSCALE, None, ALU.mult).then_inc(done, 1)
                    nc.vector.tensor_scalar(wd[:], di[:], QSCALE, None, ALU.mult).then_inc(done, 1)
                    v.wait_ge(done, 2)
            clear(nc, names)
        xT = s.sb("xT", [P, 2, N])
        G = s.sb("G", [P, 2, GHID])
        H = s.sb("H", [P, 2, GHID])
        HT = s.sb("HT", [P, 2, GC, P])
        n_in, n_out = Norm(s, "ni"), Norm(s, "no")
        names = (norm_done, tr, xT_done, up_ready, g_done, h_done, hT_ready, hT_ev, y_ready, x_done, link_, var_, pow_) = s.sems(
            *"norm_done tr xT_done up_ready g_done h_done hT_ready hT_ev y_ready x_done link var pow".split())
        XT, UP, HTB, Y = 0, 1, 5, 6
        NORMS = [n_in]
        for n in range(1, TT):
            if n % NT == 1 and n > NT:
                NORMS.append(n_out)
            if n % NT == 2 and n // NT + 1 < B:
                NORMS.append(n_in)
        NORMS.append(n_out)
        with nc.Block() as block:
            @block.gpsimd
            def _(pool):
                for k, norm in enumerate(NORMS):
                    pool.wait_ge(var_, k + 1)
                    norm.power(nc, c).then_inc(pow_, 1)

            @block.tensor
            def _(pe):
                def turn_x(b):
                    pe.wait_ge(norm_done, NT * (b + 1))
                    for t in range(NT):
                        ins = nc.tensor.transpose(ps[:, XT, P * t:P * t + P], n_in.out[:, t, :], c["ident"][:])
                    ins.then_inc(tr, 1)

                def up(n):
                    b, t = n // NT, n % NT
                    if t == 0:
                        pe.wait_ge(xT_done, b + 1)
                    if n >= 2:
                        pe.wait_ge(h_done, n - 1)
                    for j in range(2):
                        ins = nc.tensor.matmul(ps[:, UP + 2 * (n % 2) + j, 0:GHID], xT[:, b % 2, P * t:P * t + P], wgu[:, j, :],
                                               start=True, stop=True)
                    ins.then_inc(up_ready, 1)

                def turn_h(n):
                    pe.wait_ge(h_done, n + 1)
                    if n >= 1:
                        pe.wait_ge(hT_ev, n)
                    for k in range(GC):
                        ins = nc.tensor.transpose(ps[:, HTB, P * k:P * k + P], H[:, n % 2, P * k:P * k + P], c["ident"][:])
                    ins.then_inc(hT_ready, 1)

                def down(n):
                    b, t = n // NT, n % NT
                    pe.wait_ge(hT_ev, n + 1)
                    if t == 0 and b >= 2:
                        pe.wait_ge(x_done, b - 1)
                    for k in range(GC):
                        ins = nc.tensor.matmul(ps[:, Y + b % 2, P * t:P * t + P], HT[:, n % 2, k, :], wd[:, k, :],
                                               start=(k == 0), stop=(k == GC - 1))
                    ins.then_inc(y_ready, 1)

                turn_x(0)
                for n in range(TT + 2):
                    if n < TT:
                        up(n)
                    if 1 <= n <= TT:
                        turn_h(n - 1)
                    if n >= 2:
                        down(n - 2)
                    if n % NT == NT - 1 and n // NT + 1 < B:
                        turn_x(n // NT + 1)

            @block.scalar
            def _(act):
                def take_x(b):
                    act.wait_ge(tr, b + 1)
                    nc.scalar.copy(xT[:, b % 2, :], ps[:, XT, :]).then_inc(xT_done, 1)

                take_x(0)
                for n in range(TT + 1):
                    if n < TT:
                        act.wait_ge(up_ready, n + 1)
                        if n >= 2:
                            act.wait_ge(h_done, n - 1)
                        nc.scalar.activation(G[:, n % 2, :], ps[:, UP + 2 * (n % 2), 0:GHID], ACT.Silu).then_inc(g_done, 1)
                    if n >= 1:
                        m = n - 1
                        act.wait_ge(hT_ready, m + 1)
                        if m >= 2:
                            act.wait_ge(y_ready, m - 1)
                        nc.scalar.copy(HT[:, m % 2].rearrange("p k n -> p (k n)"), ps[:, HTB, 0:GHID]).then_inc(hT_ev, 1)
                    if n % NT == NT - 1 and n // NT + 1 < B:
                        take_x(n // NT + 1)

            @block.vector
            def _(v):
                link = Chain(v, link_)
                norms = 0

                def enter(b):
                    nonlocal norms
                    norms += 1
                    xs = X[:, b * NT:b * NT + NT, :]
                    n_in.variance(nc, link, xs, EPS).then_inc(var_, 1)
                    v.wait_ge(pow_, norms)
                    if b >= 1:
                        v.wait_ge(tr, b)
                    for t in range(NT):
                        nc.vector.tensor_scalar(n_in.out[:, t, :], xs[:, t, :], n_in.mv[:, t, 0:1], n_in.rstd[:, t:t + 1],
                                                ALU.subtract, ALU.mult).then_inc(norm_done, 1)

                def leave(b):
                    nonlocal norms
                    norms += 1
                    xs = X[:, b * NT:b * NT + NT, :]
                    y = ps[:, Y + b % 2, :].rearrange("p (t n) -> p t n", n=D)
                    v.wait_ge(y_ready, NT * (b + 1))
                    n_out.variance(nc, link, y, EPS).then_inc(var_, 1)
                    v.wait_ge(pow_, norms)
                    n_out.apply(nc, link, n_out.out, y)
                    nc.vector.tensor_tensor(xs, xs, n_out.out[:], ALU.add).then_inc(x_done, 1)
                    v.wait_ge(x_done, b + 1)

                enter(0)
                for n in range(TT):
                    v.wait_ge(g_done, n + 1)
                    if n >= 2:
                        v.wait_ge(hT_ready, n - 1)
                    nc.vector.tensor_tensor(H[:, n % 2, :], ps[:, UP + 1 + 2 * (n % 2), 0:GHID], G[:, n % 2, :],
                                            ALU.mult).then_inc(h_done, 1)
                    if n % NT == 1 and n > NT:
                        leave(n // NT - 1)
                    if n % NT == 2 and n // NT + 1 < B:
                        enter(n // NT + 1)
                leave(B - 1)
        clear(nc, names)


def arrays_of_rest(i):
    emb = i["L1_attn_rel_pos_emb"][MAX_LEN - (N - 1):MAX_LEN - (N - 1) + RW]
    p = np.arange(P)
    return {
        "r_w": np.stack([i["L1_attn_Wq"], i["L1_attn_Wk"], i["L1_attn_Wv"], i["L1_attn_Wr"]], axis=1),
        "r_gb": np.stack([i["L1_attn_gamma"], i["L1_attn_beta"]], axis=1),
        "r_uv": np.stack([i["L1_attn_u_bias"].reshape(P), i["L1_attn_v_bias"].reshape(P)], axis=1),
        "r_emb": emb.T,
        "r_wo": i["L1_attn_Wo"],
        "r_bo": rows(i["L1_attn_bo"]),
        "r_sel": (np.arange(P)[None, :] // RD == np.arange(RH)[:, None]).astype(np.float32),
        "r_hm": ((p[:, None] % 32) // RD == np.arange(RG)[None, :]).astype(np.float32),
        "g_wgu": np.stack([i["L1_ffn_w_gate"].T, i["L1_ffn_w_up"].T], axis=1),
        "g_wd": i["L1_ffn_w_down"].T.reshape(GC, P, D).transpose(1, 0, 2),
    }


def program(nc, d, out):
    with ExitStack() as ctx:
        s = Store(nc, ctx, "m")
        X = s.sb("X", [P, TT, D])
        c = {"ident": s.sb("ident", [P, P]), "identb": s.sb("identb", [P, P], BF16), "trib": s.sb("trib", [P, P], BF16),
             "mhalf": s.sb("mhalf", [P, 16])}
        ps = ctx.enter_context(nc.psum_tensor("ps", [P, 8, 512], F32))
        names = c_in, c_tri, c_done, done = s.sems("c_in", "c_tri", "c_done", "done")
        with ExitStack() as ctx0:
            tri = Store(nc, ctx0, "m0").sb("tri", [P, P])
            with nc.Block() as block:
                @block.sync
                def _(sp):
                    sp.dma_start(c["ident"][:], d["ident"]).then_inc(c_in, 16)
                    sp.dma_start(tri[:], d["tri"]).then_inc(c_tri, 16)

                @block.vector
                def _(v):
                    v.wait_ge(c_in, 16)
                    nc.vector.tensor_copy(c["identb"][:], c["ident"][:]).then_inc(c_done, 1)
                    v.wait_ge(c_tri, 16)
                    nc.vector.tensor_copy(c["trib"][:], tri[:]).then_inc(c_done, 1)
                    nc.vector.memset(c["mhalf"][:], -0.5).then_inc(c_done, 1)
                    v.wait_ge(c_done, 3)
        clear(nc, names)
        with ExitStack() as ctxz:
            RS = Store(nc, ctxz, "z").sb("RS", [P, TT, AH])
            zd = nc.dram_tensor("zd", (B, AH * AR, N), F32, kind="Internal").ap()
            causal_attention(nc, X, RS, zd, ps, c, d)
            output_and_residual(nc, X, RS, zd, ps, c, d)
        local_layers(nc, X, ps, c, d)
        relative_attention(nc, X, ps, c, d)
        gated_feed_forward(nc, X, ps, c, d)

        with nc.Block() as block:
            @block.sync
            def _(sp):
                sp.dma_start(out.rearrange("b (t p) d -> p (b t) d", p=P), X[:]).then_inc(done, 16)
                sp.wait_ge(done, 16)


def kernel(**inputs):
    import concourse.bacc as bacc
    from concourse.bass_utils import run_bass_kernel_spmd

    i = {k: np.asarray(v) for k, v in inputs.items()}
    arrays = {"in_" + k: np.ascontiguousarray(v) for k, v in (arrays_of(i) | arrays_of_layers(i) | arrays_of_rest(i)).items()}
    nc = bacc.Bacc("TRN2", target_bir_lowering=False, num_devices=1)
    d = {k[3:]: nc.dram_tensor(k, v.shape, mybir.dt.from_np(v.dtype), kind="ExternalInput").ap() for k, v in arrays.items()}
    out = nc.dram_tensor("out", (B, N, D), F32, kind="ExternalOutput").ap()
    program(nc, d, out)
    r = run_bass_kernel_spmd(nc, [arrays], core_ids=[0])
    return r.results[0]["out"]
```
